# Optimizing a Trainium2 kernel written in Bass

```python
import numpy as np
import jax
import jax.numpy as jnp

def _softmax(x, axis=-1):
    return jax.nn.softmax(x, axis=axis)

def _gelu(x):
    return jax.nn.gelu(x, approximate=True)

def _silu(x):
    return jax.nn.silu(x)

def _sigmoid(x):
    return jax.nn.sigmoid(x)

def _layernorm(x, axis=-1, eps=1e-05):
    m = jnp.mean(x, axis=axis, keepdims=True)
    v = jnp.var(x, axis=axis, keepdims=True)
    return (x - m) / jnp.sqrt(v + eps)

def _scatter_add(tgt, idx, src, axis=0):
    return tgt.at[idx].add(src)

def _segment_sum(src, seg, n):
    return jax.ops.segment_sum(src, seg, n)
kernel_name = 'mk_macaron_d1_jaxref_r8_8a7b65'

def setup_inputs(seed: int=0):
    np.random.seed(seed)
    _w = jnp.asarray

    def _L0_attn_setup():
        import jax, jax.numpy as jnp
        import numpy as np
        B, T, C = (8, 256, 128)
        HS = 64
        H = C // HS
        LORA_R = 32
        TD_R = 64

        def _wkv6(r, k, v, w, u):
            n = r.shape[-1]
            decay = jnp.exp(-jnp.exp(w))

            def per_head(rt, kt, vt, dt, uh):

                def step(S, inp):
                    ri, ki, vi, di = inp
                    kv = ki[:, None] * vi[None, :]
                    y = ri @ (S + uh[:, None] * kv)
                    S = di[:, None] * S + kv
                    return (S, y)
                S0 = jnp.zeros((n, n), rt.dtype)
                _, ys = jax.lax.scan(step, S0, (rt, kt, vt, dt))
                return ys
            f = jax.vmap(per_head, in_axes=(0, 0, 0, 0, 0))
            f = jax.vmap(f, in_axes=(0, 0, 0, 0, None))
            return f(r, k, v, decay, u)
        key = jax.random.key(seed)
        ks = jax.random.split(key, 20)
        inp = {'x': jax.random.normal(ks[0], (B, T, C), jnp.float32), 'miu_x': jax.random.uniform(ks[1], (1, 1, C), jnp.float32), 'lambda_': jax.random.uniform(ks[2], (5, 1, 1, C), jnp.float32), 'A_lora': jax.random.normal(ks[3], (C, LORA_R * 5), jnp.float32) * 0.01, 'B_lora': jax.random.normal(ks[4], (5, LORA_R, C), jnp.float32) * 0.01, 'td_miu': -6.0 + 5.0 * jax.random.uniform(ks[5], (1, 1, C), jnp.float32), 'td_A': jax.random.normal(ks[6], (C, TD_R), jnp.float32) * 0.01, 'td_B': jax.random.normal(ks[7], (TD_R, C), jnp.float32) * 0.01, 'u': jax.random.normal(ks[8], (H, HS), jnp.float32) * 0.1, 'Wr': jax.random.normal(ks[9], (C, C), jnp.float32) * 0.02, 'Wk': jax.random.normal(ks[10], (C, C), jnp.float32) * 0.02, 'Wv': jax.random.normal(ks[11], (C, C), jnp.float32) * 0.02, 'Wg': jax.random.normal(ks[12], (C, C), jnp.float32) * 0.02, 'Wo': jax.random.normal(ks[13], (C, C), jnp.float32) * 0.02, 'gn_gamma': jnp.ones((C,), jnp.float32), 'gn_beta': jnp.zeros((C,), jnp.float32)}
        return inp
    _L0_attn_in = _L0_attn_setup()

    def _L0_ffn_setup():
        import jax, jax.numpy as jnp
        import numpy as np
        B, N, D, H, E = (4, 128, 128, 16, 8)
        DK = D // H
        HID = 4 * D
        EPS = 1e-05

        def _layernorm(x, w, b):
            m = jnp.mean(x, axis=-1, keepdims=True)
            v = jnp.mean(jnp.square(x - m), axis=-1, keepdims=True)
            return (x - m) * jax.lax.rsqrt(v + EPS) * w + b

        def _msa(x, w_qkv, w_proj):
            b, n, d = x.shape
            qkv = (x @ w_qkv).reshape(b, n, 3, H, DK)
            q = qkv[:, :, 0].transpose(0, 2, 1, 3)
            k = qkv[:, :, 1].transpose(0, 2, 1, 3)
            v = qkv[:, :, 2].transpose(0, 2, 1, 3)
            attn = jnp.einsum('bhnd,bhmd->bhnm', q, k) * (1.0 / np.sqrt(DK))
            attn = jax.nn.softmax(attn, axis=-1)
            y = jnp.einsum('bhnm,bhmd->bhnd', attn, v)
            y = y.transpose(0, 2, 1, 3).reshape(b, n, d)
            return y @ w_proj

        def _moe_mlp(x, gate_w, gate_b, w1, w2):
            b, n, d = x.shape
            xf = x.reshape(b * n, d)
            logits = xf @ gate_w + gate_b
            one_hot = jax.nn.one_hot(jnp.argmax(logits, axis=-1), E, dtype=xf.dtype)
            h = jax.nn.gelu(jnp.einsum('td,edh->teh', xf, w1), approximate=True)
            y = jnp.einsum('teh,ehd->ted', h, w2)
            out = jnp.einsum('te,ted->td', one_hot, y)
            return out.reshape(b, n, d)
        key = jax.random.key(seed)
        ks = jax.random.split(key, 8)
        s = 0.02
        return {'x': jax.random.normal(ks[0], (B, N, D), jnp.float32), 'ln1_w': jnp.ones((D,), jnp.float32), 'ln1_b': jnp.zeros((D,), jnp.float32), 'w_qkv': jax.random.normal(ks[1], (D, 3 * D), jnp.float32) * s, 'w_proj': jax.random.normal(ks[2], (D, D), jnp.float32) * s, 'ln2_w': jnp.ones((D,), jnp.float32), 'ln2_b': jnp.zeros((D,), jnp.float32), 'gate_w': jax.random.normal(ks[3], (D, E), jnp.float32) * s, 'gate_b': jnp.zeros((E,), jnp.float32), 'w1': jax.random.normal(ks[4], (E, D, HID), jnp.float32) * s, 'w2': jax.random.normal(ks[5], (E, HID, D), jnp.float32) * s}
    _L0_ffn_in = _L0_ffn_setup()
    _d = {'L0_attn_x': _L0_attn_in['x'], 'L0_attn_miu_x': _L0_attn_in['miu_x'], 'L0_attn_lambda_': _L0_attn_in['lambda_'], 'L0_attn_A_lora': _L0_attn_in['A_lora'], 'L0_attn_B_lora': _L0_attn_in['B_lora'], 'L0_attn_td_miu': _L0_attn_in['td_miu'], 'L0_attn_td_A': _L0_attn_in['td_A'], 'L0_attn_td_B': _L0_attn_in['td_B'], 'L0_attn_u': _L0_attn_in['u'], 'L0_attn_Wr': _L0_attn_in['Wr'], 'L0_attn_Wk': _L0_attn_in['Wk'], 'L0_attn_Wv': _L0_attn_in['Wv'], 'L0_attn_Wg': _L0_attn_in['Wg'], 'L0_attn_Wo': _L0_attn_in['Wo'], 'L0_attn_gn_gamma': _L0_attn_in['gn_gamma'], 'L0_attn_gn_beta': _L0_attn_in['gn_beta'], 'L0_ffn_ln1_w': _L0_ffn_in['ln1_w'], 'L0_ffn_ln1_b': _L0_ffn_in['ln1_b'], 'L0_ffn_w_qkv': _L0_ffn_in['w_qkv'], 'L0_ffn_w_proj': _L0_ffn_in['w_proj'], 'L0_ffn_ln2_w': _L0_ffn_in['ln2_w'], 'L0_ffn_ln2_b': _L0_ffn_in['ln2_b'], 'L0_ffn_gate_w': _L0_ffn_in['gate_w'], 'L0_ffn_gate_b': _L0_ffn_in['gate_b'], 'L0_ffn_w1': _L0_ffn_in['w1'], 'L0_ffn_w2': _L0_ffn_in['w2']}
    _x0 = _d['L0_attn_x']
    _d['L0_attn_x'] = jax.random.normal(jax.random.fold_in(jax.random.key(seed), 1), (8, 512, 128), dtype=_x0.dtype)
    del _x0
    return _d

def reference(L0_attn_x, L0_attn_miu_x, L0_attn_lambda_, L0_attn_A_lora, L0_attn_B_lora, L0_attn_td_miu, L0_attn_td_A, L0_attn_td_B, L0_attn_u, L0_attn_Wr, L0_attn_Wk, L0_attn_Wv, L0_attn_Wg, L0_attn_Wo, L0_attn_gn_gamma, L0_attn_gn_beta, L0_ffn_ln1_w, L0_ffn_ln1_b, L0_ffn_w_qkv, L0_ffn_w_proj, L0_ffn_ln2_w, L0_ffn_ln2_b, L0_ffn_gate_w, L0_ffn_gate_b, L0_ffn_w1, L0_ffn_w2):

    def _L0_attn_ref(x, miu_x, lambda_, A_lora, B_lora, td_miu, td_A, td_B, u, Wr, Wk, Wv, Wg, Wo, gn_gamma, gn_beta):
        import jax, jax.numpy as jnp
        import numpy as np
        B, T, C = (8, 256, 128)
        HS = 64
        H = C // HS
        LORA_R = 32
        TD_R = 64

        def _wkv6(r, k, v, w, u):
            n = r.shape[-1]
            decay = jnp.exp(-jnp.exp(w))

            def per_head(rt, kt, vt, dt, uh):

                def step(S, inp):
                    ri, ki, vi, di = inp
                    kv = ki[:, None] * vi[None, :]
                    y = ri @ (S + uh[:, None] * kv)
                    S = di[:, None] * S + kv
                    return (S, y)
                S0 = jnp.zeros((n, n), rt.dtype)
                _, ys = jax.lax.scan(step, S0, (rt, kt, vt, dt))
                return ys
            f = jax.vmap(per_head, in_axes=(0, 0, 0, 0, 0))
            f = jax.vmap(f, in_axes=(0, 0, 0, 0, None))
            return f(r, k, v, decay, u)
        b, t, c = x.shape
        h, n = u.shape
        x_last = jnp.pad(x, ((0, 0), (1, 0), (0, 0)))[:, :t]
        dxa = x_last - x
        xm = x + dxa * miu_x
        lora_h = jnp.tanh(xm @ A_lora).reshape(b, t, 5, -1)
        miu = lambda_ + jnp.einsum('btfi,fic->fbtc', lora_h, B_lora)
        xx = x[None] + dxa[None] * miu
        w_in, k_in, v_in, r_in, g_in = xx
        k = k_in @ Wk.T
        v = v_in @ Wv.T
        r = r_in @ Wr.T
        g = jax.nn.silu(g_in @ Wg.T)
        w = td_miu + jnp.tanh(w_in @ td_A) @ td_B

        def to_heads(z):
            return z.reshape(b, t, h, n).transpose(0, 2, 1, 3)
        y = _wkv6(to_heads(r), to_heads(k), to_heads(v), to_heads(w), u)
        y = y.transpose(0, 2, 1, 3)
        eps = 1e-05 * h
        mean = y.mean(-1, keepdims=True)
        var = y.var(-1, keepdims=True)
        yn = (y - mean) * jax.lax.rsqrt(var + eps)
        yn = yn * gn_gamma.reshape(h, n) + gn_beta.reshape(h, n)
        yn = yn.reshape(b, t, c)
        return yn * g @ Wo.T

    def _L0_ffn_ref(x, ln1_w, ln1_b, w_qkv, w_proj, ln2_w, ln2_b, gate_w, gate_b, w1, w2):
        import jax, jax.numpy as jnp
        import numpy as np
        B, N, D, H, E = (4, 128, 128, 16, 8)
        DK = D // H
        HID = 4 * D
        EPS = 1e-05

        def _layernorm(x, w, b):
            m = jnp.mean(x, axis=-1, keepdims=True)
            v = jnp.mean(jnp.square(x - m), axis=-1, keepdims=True)
            return (x - m) * jax.lax.rsqrt(v + EPS) * w + b

        def _msa(x, w_qkv, w_proj):
            b, n, d = x.shape
            qkv = (x @ w_qkv).reshape(b, n, 3, H, DK)
            q = qkv[:, :, 0].transpose(0, 2, 1, 3)
            k = qkv[:, :, 1].transpose(0, 2, 1, 3)
            v = qkv[:, :, 2].transpose(0, 2, 1, 3)
            attn = jnp.einsum('bhnd,bhmd->bhnm', q, k) * (1.0 / np.sqrt(DK))
            attn = jax.nn.softmax(attn, axis=-1)
            y = jnp.einsum('bhnm,bhmd->bhnd', attn, v)
            y = y.transpose(0, 2, 1, 3).reshape(b, n, d)
            return y @ w_proj

        def _moe_mlp(x, gate_w, gate_b, w1, w2):
            b, n, d = x.shape
            xf = x.reshape(b * n, d)
            logits = xf @ gate_w + gate_b
            one_hot = jax.nn.one_hot(jnp.argmax(logits, axis=-1), E, dtype=xf.dtype)
            h = jax.nn.gelu(jnp.einsum('td,edh->teh', xf, w1), approximate=True)
            y = jnp.einsum('teh,ehd->ted', h, w2)
            out = jnp.einsum('te,ted->td', one_hot, y)
            return out.reshape(b, n, d)
        x = x + _msa(_layernorm(x, ln1_w, ln1_b), w_qkv, w_proj)
        x = x + _moe_mlp(_layernorm(x, ln2_w, ln2_b), gate_w, gate_b, w1, w2)
        return x
    x = L0_attn_x
    x = x + 0.5 * _L0_ffn_ref(_layernorm(x, axis=-1), L0_ffn_ln1_w, L0_ffn_ln1_b, L0_ffn_w_qkv, L0_ffn_w_proj, L0_ffn_ln2_w, L0_ffn_ln2_b, L0_ffn_gate_w, L0_ffn_gate_b, L0_ffn_w1, L0_ffn_w2)
    x = x + _L0_attn_ref(_layernorm(x, axis=-1), L0_attn_miu_x, L0_attn_lambda_, L0_attn_A_lora, L0_attn_B_lora, L0_attn_td_miu, L0_attn_td_A, L0_attn_td_B, L0_attn_u, L0_attn_Wr, L0_attn_Wk, L0_attn_Wv, L0_attn_Wg, L0_attn_Wo, L0_attn_gn_gamma, L0_attn_gn_beta)
    x = x + 0.5 * _L0_ffn_ref(_layernorm(x, axis=-1), L0_ffn_ln1_w, L0_ffn_ln1_b, L0_ffn_w_qkv, L0_ffn_w_proj, L0_ffn_ln2_w, L0_ffn_ln2_b, L0_ffn_gate_w, L0_ffn_gate_b, L0_ffn_w1, L0_ffn_w2)
    return x

_drawn_inputs = setup_inputs


def setup_inputs(seed=0):
    import zlib

    import numpy as np

    out = dict(_drawn_inputs(seed))
    spreads = {'L0_attn_gn_gamma': (1.0, 0.6),
     'L0_attn_gn_beta': (0.0, 0.8),
     'L0_ffn_ln1_w': (1.0, 0.6),
     'L0_ffn_ln1_b': (0.0, 0.8),
     'L0_ffn_ln2_w': (1.0, 0.6),
     'L0_ffn_ln2_b': (0.0, 2.0),
     'L0_ffn_gate_b': (0.0, 0.289)}
    factors = {'L0_attn_miu_x': 8.0,
     'L0_attn_lambda_': 4.852,
     'L0_attn_A_lora': 8.0,
     'L0_attn_B_lora': 8.0,
     'L0_attn_td_miu': 5.08,
     'L0_attn_td_A': 64.0,
     'L0_attn_td_B': 64.0,
     'L0_attn_u': 8.0,
     'L0_attn_Wr': 3.679,
     'L0_attn_Wk': 3.702,
     'L0_attn_Wv': 3.674,
     'L0_attn_Wg': 3.674,
     'L0_attn_Wo': 3.692,
     'L0_ffn_w_qkv': 8.0,
     'L0_ffn_w_proj': 8.0}
    for name, (base, spread) in spreads.items():
        noise = np.random.default_rng([zlib.crc32(name.encode()), seed]).standard_normal(out[name].shape)
        drawn = base * np.exp(spread * noise) if base else spread * noise
        out[name] = jnp.asarray(drawn.astype(out[name].dtype))
    for name, factor in factors.items():
        out[name] = (out[name] * factor).astype(out[name].dtype)
    return out
```

```python
from contextlib import ExitStack

import concourse.bass as bass
from concourse import mybir

F32 = mybir.dt.float32
BF16 = mybir.dt.bfloat16
I32 = mybir.dt.int32
ALU = mybir.AluOpType
ACT = mybir.ActivationFunctionType
AX_X = mybir.AxisListType.X
ds = bass.ds

P = 128
B, T = 8, 512
TOK = B * T
NT = TOK // P
TPB = T // P
H, DK = 16, 8
GROUP = 4
NG = H // GROUP
SPLITS = 3
ROWS = SPLITS * SPLITS * DK
MAXROW = 96
STACK = MAXROW + SPLITS
VW = 32
E, HID = 8, 512
HC = HID // P
SLOTS = TOK // P + E
EPS = 1e-5
SL = 4
ST = NT // SL
SW = ST * P


def own(nc, name):
    return f"{name}_{nc.next_id()}"


class Phase(ExitStack):

    def __init__(self, nc):
        super().__init__()
        self.nc, self.semaphores = nc, []

    def semaphore(self, name):
        self.semaphores.append(self.nc.alloc_semaphore(own(self.nc, name)))
        return self.semaphores[-1]

    def __exit__(self, *failure):
        if failure[0] is None:
            self.nc.clear_and_free_semaphores(self.semaphores)
            self.nc.all_engine_barrier()
        return super().__exit__(*failure)


def wait_apart(eng, passed, *waits):
    for sem, value in waits:
        eng.wait_ge(sem, value)
    eng.sem_inc(passed, 1)


class LayerNorm:

    def __init__(self, nc, ctx, name, tiles, eps, width=P):
        self.nc, self.tiles, self.eps, self.width = nc, tiles, eps, width

        def sb(what, shape):
            return ctx.enter_context(nc.sbuf_tensor(own(nc, f"{name}_{what}"), shape, F32))

        self.total, self.mean = sb("total", [P, tiles]), sb("mean", [P, tiles])
        self.square_sum, self.var = sb("square_sum", [P, tiles]), sb("var", [P, tiles])
        self.rstd, self.power = sb("rstd", [P, tiles]), sb("power", [P, tiles])
        self.centered, self.square = sb("centered", [P, tiles, width]), sb("square", [P, tiles, width])

        def sem(what):
            return ctx.semaphore(f"{name}_{what}")

        self.passed = sem("passed")
        self.vec_step, self.pool_step = sem("vec_step"), sem("pool_step")
        self.is_centered, self.is_squared = sem("is_centered"), sem("is_squared")
        self.var_ready, self.done = sem("var_ready"), sem("done")

    def wide(self, a):
        return a[:].unsqueeze(2).broadcast_to([P, self.tiles, self.width])

    def start(self, pool):
        self.nc.gpsimd.memset(self.power[:], -0.5).then_inc(self.done, 1)

    def center(self, vec, n, src):
        v = self.nc.vector
        v.tensor_reduce(self.total[:], src, AX_X, ALU.add).then_inc(self.vec_step, 1)
        vec.wait_ge(self.vec_step, 3 * n + 1)
        v.tensor_scalar(self.mean[:], self.total[:], 1.0 / self.width, None, ALU.mult).then_inc(self.vec_step, 1)
        vec.wait_ge(self.vec_step, 3 * n + 2)
        vec.wait_ge(self.done, n + 1)
        v.tensor_tensor(self.centered[:], src, self.wide(self.mean), ALU.subtract).then_inc(self.is_centered, 1)

    def squares(self, act, n):
        act.wait_ge(self.is_centered, n + 1)
        self.nc.scalar.activation(self.square[:], self.centered[:], ACT.Square).then_inc(self.is_squared, 1)

    def variance(self, vec, n):
        v = self.nc.vector
        vec.wait_ge(self.is_squared, n + 1)
        v.tensor_reduce(self.square_sum[:], self.square[:], AX_X, ALU.add).then_inc(self.vec_step, 1)
        vec.wait_ge(self.vec_step, 3 * n + 3)
        v.tensor_scalar(self.var[:], self.square_sum[:], 1.0 / self.width, self.eps, ALU.mult,
                        ALU.add).then_inc(self.var_ready, 1)

    def scale(self, pool, n, dst):
        g = self.nc.gpsimd
        pool.wait_ge(self.var_ready, n + 1)
        g.tensor_tensor(self.rstd[:], self.var[:], self.power[:], ALU.pow).then_inc(self.pool_step, 1)
        wait_apart(pool, self.passed, (self.pool_step, n + 1))
        g.tensor_tensor(dst, self.centered[:], self.wide(self.rstd), ALU.mult).then_inc(self.done, 1)

    def wait_done(self, eng, n):
        eng.wait_ge(self.done, n + 2)

    def done_free(self, eng, n):
        eng.wait_ge(self.done, n + 1)


def load_constants(nc, ctx, d, zeros, xs):
    s = {}

    def sb(name, shape, dt=F32):
        s[name] = ctx.enter_context(nc.sbuf_tensor(own(nc, name), shape, dt))
        return s[name]

    loads = [(sb("ident", [P, P]), d["ident"]), (sb("w_qkv", [P, 3 * P]), d["L0_ffn_w_qkv"]),
             (sb("w_proj", [P, P]), d["L0_ffn_w_proj"])]
    for name in ("ln1_w", "ln1_b", "ln2_w", "ln2_b"):
        loads.append((sb(name, [P, 1]), d["L0_ffn_" + name].rearrange("(c a) -> c a", a=1)))
    loads += [(sb("gate_w", [P, E]), d["L0_ffn_gate_w"]),
              (sb("gate_b", [P, E]), d["L0_ffn_gate_b"].rearrange("(a e) -> a e", a=1).broadcast_to([P, E])),
              (sb("below", [P, P]), d["below"]),
              (sb("counts", [P, SLOTS]), d["counts"]), (sb("restart", [P, E * NT]), d["restart"]),
              (sb("w1", [P, E, HID]), d["L0_ffn_w1"].rearrange("e c h -> c e h")),
              (sb("w2", [P, E, HC, P]), d["L0_ffn_w2"].rearrange("e (k c) d -> c e k d", c=P))]
    a = "L0_attn_"
    for name in ("WkT", "WvT", "WrT", "WgT", "WoT"):
        loads.append((sb(name, [P, P]), d[name]))
    loads += [(sb("A_lora", [P, 5 * LORA]), d[a + "A_lora"]), (sb("td_A", [P, HS]), d[a + "td_A"]),
              (sb("td_B", [HS, P]), d[a + "td_B"]), (sb("B_lora4", [LORA, P]), d[a + "B_lora"][4]),
              (sb("lambda", [P, 5]), d["lambda_columns"]), (sb("miu_x", [P, 1]), d[a + "miu_x"].rearrange("a b c -> c (a b)")),
              (sb("td_miu", [P, 1]), d[a + "td_miu"].rearrange("a b c -> c (a b)")),
              (sb("u", [P, 1]), d[a + "u"].rearrange("h (n a) -> (h n) a", a=1)),
              (sb("gn_w", [P, 1]), d[a + "gn_gamma"].rearrange("(c a) -> c a", a=1)),
              (sb("gn_b", [P, 1]), d[a + "gn_beta"].rearrange("(c a) -> c a", a=1)),
              (sb("level_masks", [P, DIAG_LEVELS + 1, BLOCK], I32), d["level_masks"])]
    sb("B_lora", [P, 4, P])
    sb("gn_w_half", [P, 1])
    sb("gn_b_half", [P, 1])
    sb("ident16", [P, P], BF16)
    sb("ones", [P, P])
    loaded = ctx.semaphore("constants_loaded")
    cast = ctx.semaphore("ident_cast")
    zeros_set, zeroed = ctx.semaphore("zeros_set"), ctx.semaphore("zeroed")
    with nc.Block() as block:
        @block.sync
        def _(sp):
            for dst, src in loads:
                sp.dma_start(dst[:], src).then_inc(loaded, 16)
            sp.wait_ge(zeros_set, 2)
            for f in range(4):
                at = slice(f * LORA, (f + 1) * LORA)
                sp.dma_start(s["B_lora"][at, f, :], d[a + "B_lora"][f]).then_inc(loaded, 16)
            sp.wait_ge(loaded, 16 * (len(loads) + 4))

        @block.vector
        def _(vec):
            vec.wait_ge(loaded, 16 * (len(loads) + 4))
            nc.vector.tensor_copy(s["ident16"][:], s["ident"][:]).then_inc(cast, 1)
            nc.vector.memset(s["ones"][:], 1.0).then_inc(cast, 1)
            vec.wait_ge(cast, 2)

        @block.gpsimd
        def _(pool):
            nc.gpsimd.memset(s["B_lora"][:], 0.0).then_inc(zeros_set, 1)
            nc.gpsimd.memset(zeros[:], 0.0).then_inc(zeros_set, 1)
            pool.wait_ge(zeros_set, 2)
            rows = xs.rearrange("(n p) c -> p n c", p=P)
            for i in range(0, SLOTS, NT // 4):
                pool.dma_start(rows[:, i:i + NT // 4, :], zeros[:, 0:NT // 4, :]).then_inc(zeroed, 16)
            pool.wait_ge(zeroed, 16 * (SLOTS // (NT // 4)))
    return s


def qkv_phase(nc, ps, s, x_all, z_all, v_all, x_dram, qd, kd):
    with Phase(nc) as ctx:
        def sb(name, shape, dt=F32):
            return ctx.enter_context(nc.sbuf_tensor(own(nc, name), shape, dt))

        sems = []

        def sem(name):
            x = ctx.semaphore(name)
            sems.append(x)
            return x

        lna = LayerNorm(nc, ctx, "lna", ST, EPS)
        lnb = LayerNorm(nc, ctx, "lnb", ST, EPS)
        zn = sb("zn", [P, ST, P])
        hT = sb("hT", [P, SW])
        parts = {k: sb(k + "_parts", [P, SPLITS, SW], BF16) for k in "qk"}
        rest = {k: sb(k + "_rest", [P, SW]) for k in "qk"}
        x_loaded, ones_set, turned, h_ready = sem("x_loaded"), sem("ones_set"), sem("turned"), sem("h_ready")
        made = {k: sem(k + "_made") for k in "qkv"}
        high, mid, low, diff = ({k: sem(k + w) for k in "qk"} for w in ("_high", "_mid", "_low", "_diff"))
        v_kept, stored = sem("v_kept"), {k: sem(k + "_stored") for k in "qk"}
        psT = ps[:, 0:2, :]
        psX = {"q": ps[:, 2:4, :], "k": ps[:, 4:6, :]}
        psV = ps[:, 6:8, :]
        flat = "p a b -> p (a b)"

        with nc.Block() as block:
            @block.sync
            def _(sp):
                if x_dram is not None:
                    src = x_dram.rearrange("b t c -> (b t) c").rearrange("(n p) c -> p n c", p=P)
                    for i in range(SL):
                        if i:
                            sp.wait_ge(x_loaded, 16 * i)
                        sp.dma_start(x_all[:, i * ST:(i + 1) * ST, :], src[:, i * ST:(i + 1) * ST, :]).then_inc(x_loaded, 16)
                with sp.Fori(0, SL) as n:
                    for k, dram in (("q", qd), ("k", kd)):
                        sp.wait_ge(low[k], n + 1)
                        sp.wait_ge(mid[k], n + 1)
                        sp.wait_ge(high[k], n + 1)
                        sp.dma_start(dram[:, :, ds(n * SW, SW)], parts[k][:]).then_inc(stored[k], 16)
                for k in "qk":
                    sp.wait_ge(stored[k], 16 * SL)

            @block.vector
            def _(vec):
                v = nc.vector
                vec.wait_ge(ones_set, 1)
                with vec.Fori(0, SL) as n:
                    if x_dram is not None:
                        vec.wait_ge(x_loaded, 16 * n + 16)
                    x = x_all[:, ds(n * ST, ST), :]
                    lna.center(vec, n, x)
                    lna.variance(vec, n)
                    lna.wait_done(vec, n)
                    lnb.center(vec, n, z_all[:, ds(n * ST, ST), :])
                    lnb.variance(vec, n)
                    vec.wait_ge(made["v"], n + 1)
                    v.tensor_copy(v_all[:, ds(n * ST, ST), :, 0:DK],
                                  psV.rearrange("p a (t h d) -> p (a t) h d", h=H, d=DK)).then_inc(v_kept, 1)
                    for k in "qk":
                        vec.wait_ge(high[k], n + 1)
                        v.tensor_tensor(rest[k][:], psX[k].rearrange(flat), parts[k][:, 0, :],
                                        ALU.subtract).then_inc(diff[k], 1)

            @block.scalar
            def _(act):
                a = nc.scalar
                with act.Fori(0, SL) as n:
                    lna.squares(act, n)
                    lnb.squares(act, n)
                    act.wait_ge(turned, n + 1)
                    a.activation(hT[:], psT.rearrange(flat), ACT.Identity, bias=s["ln1_b"][:, 0:1],
                                 scale=s["ln1_w"][:, 0:1]).then_inc(h_ready, 1)
                    for k in "qk":
                        act.wait_ge(made[k], n + 1)
                        a.activation(parts[k][:, 0, :], psX[k].rearrange(flat), ACT.Copy).then_inc(high[k], 1)
                    for k in "qk":
                        act.wait_ge(diff[k], n + 1)
                        a.activation(parts[k][:, 1, :], rest[k][:], ACT.Copy).then_inc(mid[k], 1)
                    for k in "qk":
                        act.wait_ge(stored[k], 16 * n + 16)

            @block.gpsimd
            def _(pool):
                g = nc.gpsimd
                lna.start(pool)
                lnb.start(pool)
                g.memset(v_all[:], 1.0).then_inc(ones_set, 1)
                with pool.Fori(0, SL) as n:
                    lna.scale(pool, n, z_all[:, ds(n * ST, ST), :])
                    lnb.scale(pool, n, zn[:])
                    for k in "qk":
                        pool.wait_ge(mid[k], n + 1)
                        g.tensor_tensor(parts[k][:, 2, :], rest[k][:], parts[k][:, 1, :],
                                        ALU.subtract).then_inc(low[k], 1)

            @block.tensor
            def _(pe):
                t = nc.tensor
                with pe.Fori(0, SL) as n:
                    lnb.wait_done(pe, n)
                    for i in range(ST):
                        last = t.transpose(psT[:, i // TPB, (i % TPB) * P:(i % TPB + 1) * P], zn[:, i, :], s["ident"][:])
                    last.then_inc(turned, 1)
                    pe.wait_ge(h_ready, n + 1)
                    for j, k in enumerate("qk"):
                        for i in range(2):
                            last = t.matmul(psX[k][:, i, :], s["w_qkv"][:, j * P:(j + 1) * P], hT[:, i * T:(i + 1) * T],
                                            start=True, stop=True)
                        last.then_inc(made[k], 1)
                    for i in range(ST):
                        last = t.matmul(psV[:, i // TPB, (i % TPB) * P:(i % TPB + 1) * P], hT[:, i * P:(i + 1) * P],
                                        s["w_qkv"][:, 2 * P:], start=True, stop=True)
                    last.then_inc(made["v"], 1)


def attention_phase(nc, ps, s, v_all, y_all, qd, kd):
    with Phase(nc) as ctx:
        def sb(name, shape, dt=F32):
            return ctx.enter_context(nc.sbuf_tensor(own(nc, name), shape, dt))

        def sem(name):
            return ctx.semaphore(name)

        qs = [sb(f"q_stack{i}", [P, GROUP, T], BF16) for i in range(NG)]
        ks = [sb(f"k_stack{i}", [P, GROUP, T], BF16) for i in range(NG)]
        vs = [sb(f"v_stack{i}", [P, TPB, GROUP, VW]) for i in range(NG)]
        probs = [sb(f"probs{i}", [P, GROUP, T]) for i in range(2)]
        maxima = sb("maxima", [P, GROUP, TPB])
        neg_rest = sb("neg_rest", [P, GROUP * TPB])
        neg_parts = sb("neg_parts", [P, SPLITS, GROUP * TPB], BF16)
        max_rows = [sb(f"max_rows{i}", [SPLITS * GROUP * TPB, P], BF16) for i in range(2)]
        oT = sb("oT", [P, T])
        inv = sb("inv", [P, TPB, GROUP])

        stacks_set = sem("stacks_set")
        loaded = [sem(f"stack_loaded{i}") for i in range(NG)]
        pool_passed, pe_passed = sem("pool_passed"), sem("pe_passed")
        v_staged = sem("v_staged")
        s_ready, s_read = sem("s_ready"), sem("s_read")
        e_ready, e_read = sem("e_ready"), sem("e_read")
        pv_unit = sem("pv_unit")
        split_step, split_done, rows_turned, rows_kept, rows_placed = (
            sem("split_step"), sem("split_done"), sem("rows_turned"), sem("rows_kept"), sem("rows_placed"))
        o_kept, o_turned, inv_ready, o_done = sem("o_kept"), sem("o_turned"), sem("inv_ready"), sem("o_done")

        psS = ps[:, 0:4, :]
        psE = ps[:, 4:6, :]
        psO = [ps[:, 6, :], ps[:, 7, :]]
        NMAX = GROUP * TPB
        PER_LOAD = 16 * 2 * SPLITS * SPLITS
        PLACED = 16 * SPLITS

        def bodies(eng, step):
            for g in range(NG):
                step(0, g, True, False)
            with eng.Fori(1, B - 1) as b:
                for g in range(NG):
                    step(b, g, False, False)
            for g in range(NG):
                step(B - 1, g, False, True)

        with nc.Block() as block:
            @block.sync
            def _(sp):
                def load_group(b, g):
                    heads = slice(g * GROUP * DK, (g + 1) * GROUP * DK)
                    for a in range(SPLITS):
                        for c in range(SPLITS):
                            r = (SPLITS * a + c) * DK
                            for st, dram, part in ((qs, qd, a), (ks, kd, c)):
                                sp.dma_start(st[g][r:r + DK, :, :],
                                             dram[heads, part, ds(b * T, T)].rearrange("(h i) t -> i h t", i=DK)
                                             ).then_inc(loaded[g], 16)

                sp.wait_ge(stacks_set, 3)
                for g in range(NG):
                    load_group(0, g)
                with sp.Fori(1, B) as b:
                    for g in range(NG):
                        sp.wait_ge(e_ready, GROUP * TPB * (NG * b + g - NG + 1))
                        load_group(b, g)

            @block.gpsimd
            def _(pool):
                g_ = nc.gpsimd
                for i in range(NG):
                    last = g_.memset(qs[i][:], 0.0)
                last.then_inc(stacks_set, 1)

                def stage(b, g):
                    g_.tensor_copy(vs[g][:, :, :, 0:DK + 1],
                                   v_all[:, ds(b * TPB, TPB), g * GROUP:(g + 1) * GROUP, :]).then_inc(v_staged, 1)

                def place(g, i, count):
                    wait_apart(pool, pool_passed, (rows_kept, count))
                    for c in range(SPLITS):
                        pool.dma_start(qs[g][MAXROW + c:MAXROW + c + 1, :, :].rearrange("c h (q t) -> c (h q) t", q=TPB),
                                       max_rows[i][c * NMAX:(c + 1) * NMAX, :]).then_inc(rows_placed, 16)

                pool.wait_ge(stacks_set, 3)
                for g in range(NG):
                    stage(0, g)
                place(0, 0, 1)

                def step(b, g, first, last):
                    if not (last and g == NG - 1):
                        place((g + 1) % NG, (g + 1) % 2, NG * b + g + 2)
                    if not first or g > 0:
                        bb, gg = (b, g - 1) if g else (b - 1, NG - 1)
                        if not last or g == 0:
                            pool.wait_ge(pv_unit, TPB * (NG * b + g))
                            stage(bb + 1, gg)

                bodies(pool, step)

            @block.tensor
            def _(pe):
                t = nc.tensor

                def s_pair(g, u, pair, count):
                    if not (isinstance(count, int) and count < 2):
                        pe.wait_ge(s_read, count - 1)
                    for h in (2 * pair, 2 * pair + 1):
                        last = t.matmul(psS[:, h, :], qs[g][0:MAXROW, h, u * P:(u + 1) * P], ks[g][0:MAXROW, h, :],
                                        start=True, stop=True)
                    last.then_inc(s_ready, 1)

                def e_head(g, u, h, count):
                    if not (isinstance(count, int) and count < 2):
                        pe.wait_ge(e_read, count - 1)
                    last = t.matmul(psE[:, h % 2, :], ks[g][0:STACK, h, u * P:(u + 1) * P], qs[g][0:STACK, h, :],
                                    start=True, stop=True)
                    last.then_inc(e_ready, 1)
                    return last

                def pv(g, u, unit):
                    pe.wait_ge(e_read, 4 * unit + 4)
                    for h in range(GROUP):
                        last = t.matmul(psO[g % 2][VW * h:VW * (h + 1), :], vs[g][:, u, h, :], probs[u % 2][:, h, :],
                                        start=(u == 0), stop=(u == TPB - 1))
                    last.then_inc(pv_unit, 1)

                def turn_max(g, count, *bank_free):
                    wait_apart(pe, pe_passed, (split_done, count), *bank_free)
                    t.transpose(psO[g % 2][0:SPLITS * NMAX, 0:P // 2].bitcast(BF16),
                                neg_parts[:].rearrange("p c m -> p (c m)"), s["ident16"][:]).then_inc(rows_turned, 1)

                pe.wait_ge(stacks_set, 3)
                for i in range(2):
                    pe.wait_ge(loaded[i], PER_LOAD)
                    for u in range(TPB):
                        for pair in range(2):
                            s_pair(i, u, pair, 8 * i + 2 * u + pair)
                    if i == 0:
                        turn_max(0, 1)

                def step(b, g, first, last):
                    G = NG * b + g
                    ahead = not (last and g >= NG - 2)
                    g2, b2 = (g + 2) % NG, (b if g < 2 else b + 1)
                    for u in range(TPB):
                        if u == 0:
                            pe.wait_ge(rows_placed, PLACED * (G + 1))
                            if ahead:
                                pe.wait_ge(loaded[g2], PER_LOAD * (b2 + 1))
                        unit = TPB * G + u
                        e_head(g, u, 0, 4 * unit)
                        e_head(g, u, 1, 4 * unit + 1)
                        if ahead:
                            s_pair(g2, u, 0, 8 * (G + 2) + 2 * u)
                        e_head(g, u, 2, 4 * unit + 2)
                        if u > 0:
                            if u == 1:
                                pe.wait_ge(v_staged, G + 1)
                                if not (first and g < 2):
                                    pe.wait_ge(rows_kept, G + 1)
                                    pe.wait_ge(o_done, G - 1)
                                else:
                                    pe.wait_ge(rows_kept, G + 1)
                            pv(g, u - 1, unit - 1)
                        elif not (first and g == 0):
                            pv((g - 1) % NG, TPB - 1, unit - 1)
                        e3 = e_head(g, u, 3, 4 * unit + 3)
                        if u == 1 and not (first and g == 0):
                            turn_o((g - 1) % NG, G)
                        if ahead:
                            s_pair(g2, u, 1, 8 * (G + 2) + 2 * u + 1)
                        if u == 2 and not (last and g == NG - 1):
                            turn_max((g + 1) % NG, G + 2, *([] if first and g == 0 else [(o_done, G)]))
                    return e3

                def turn_o(g, count):
                    pe.wait_ge(o_kept, count)
                    for q in range(TPB):
                        last = t.transpose(psO[g % 2][:, q * P:(q + 1) * P], oT[:, q * P:(q + 1) * P], s["ident"][:])
                    last.then_inc(o_turned, 1)

                bodies(pe, step)
                pv(NG - 1, TPB - 1, TPB * NG * B - 1)
                turn_o(NG - 1, NG * B)

            @block.scalar
            def _(act):
                a = nc.scalar

                def keep_rows(g, i, count):
                    act.wait_ge(rows_turned, count)
                    if not (isinstance(count, int) and count < 3):
                        act.wait_ge(rows_placed, PLACED * (count - 2))
                    a.activation(max_rows[i][:], psO[g % 2][0:SPLITS * NMAX, 0:P // 2].bitcast(BF16),
                                 ACT.Copy).then_inc(rows_kept, 1)

                def keep_o(g, count):
                    act.wait_ge(pv_unit, TPB * count)
                    if not (isinstance(count, int) and count < 2):
                        act.wait_ge(o_turned, count - 1)
                    a.activation(oT[:], psO[g % 2], ACT.Copy).then_inc(o_kept, 1)

                keep_rows(0, 0, 1)

                def step(b, g, first, last):
                    G = NG * b + g
                    for u in range(TPB):
                        unit = TPB * G + u
                        for h in range(GROUP):
                            act.wait_ge(e_ready, 4 * unit + h + 1)
                            if h == 0 and not (first and g == 0 and u < 2):
                                act.wait_ge(pv_unit, unit - 1)
                            a.activation(probs[u % 2][:, h, :], psE[:, h % 2, :], ACT.Exp,
                                         scale=float(DK) ** -0.5).then_inc(e_read, 1)
                            if u == 0 and h == 3 and not (first and g == 0):
                                keep_o((g - 1) % NG, G)
                        if u == 2 and not (last and g == NG - 1):
                            keep_rows((g + 1) % NG, (g + 1) % 2, G + 2)

                bodies(act, step)
                keep_o(NG - 1, NG * B)

            @block.vector
            def _(vec):
                v = nc.vector
                for i in range(NG):
                    v.memset(ks[i][:], 0.0).then_inc(split_step, 1)
                vec.wait_ge(split_step, NG)
                for i in range(NG):
                    last = v.memset(ks[i][MAXROW:STACK, :, :], 1.0)
                last.then_inc(stacks_set, 1)
                for i in range(NG):
                    last = v.memset(vs[i][:], 0.0)
                last.then_inc(stacks_set, 1)
                base = NG

                def reduce_pair(u, pair, count):
                    vec.wait_ge(s_ready, count + 1)
                    v.tensor_reduce(maxima[:, 2 * pair:2 * pair + 2, u:u + 1], psS[:, 2 * pair:2 * pair + 2, :], AX_X,
                                    ALU.max).then_inc(s_read, 1)

                def split_max(group):
                    vec.wait_ge(s_read, 8 * group + 8)
                    if not (isinstance(group, int) and group == 0):
                        vec.wait_ge(rows_turned, group)
                    m = maxima[:].rearrange("p h q -> p (h q)")
                    n = base + 3 * group
                    v.tensor_scalar(neg_parts[:, 0, :], m, -1.0, None, ALU.mult).then_inc(split_step, 1)
                    vec.wait_ge(split_step, n + 1)
                    v.scalar_tensor_tensor(neg_rest[:], m, -1.0, neg_parts[:, 0, :], ALU.mult,
                                           ALU.subtract).then_inc(split_step, 1)
                    vec.wait_ge(split_step, n + 2)
                    v.tensor_copy(neg_parts[:, 1, :], neg_rest[:]).then_inc(split_step, 1)
                    vec.wait_ge(split_step, n + 3)
                    v.tensor_tensor(neg_parts[:, 2, :], neg_rest[:], neg_parts[:, 1, :],
                                    ALU.subtract).then_inc(split_done, 1)

                def normalize(b, g, count):
                    vec.wait_ge(o_turned, count)
                    if not (isinstance(count, int) and count == 1):
                        vec.wait_ge(o_done, count - 1)
                    o = psO[g % 2].rearrange("p (q h w) -> p q h w", q=TPB, h=GROUP)
                    v.reciprocal(inv[:], o[:, :, :, DK]).then_inc(inv_ready, 1)
                    vec.wait_ge(inv_ready, count)
                    v.tensor_tensor(y_all[:, ds(b * TPB, TPB), g * GROUP * DK:(g + 1) * GROUP * DK].rearrange(
                        "p q (h d) -> p q h d", h=GROUP), o[:, :, :, 0:DK],
                        inv[:].unsqueeze(3).broadcast_to([P, TPB, GROUP, DK]), ALU.mult).then_inc(o_done, 1)

                for i in range(2):
                    for u in range(TPB):
                        for pair in range(2):
                            reduce_pair(u, pair, 8 * i + 2 * u + pair)
                    split_max(i)

                def step(b, g, first, last):
                    G = NG * b + g
                    for u in range(TPB):
                        if not (last and g >= NG - 2):
                            for pair in range(2):
                                reduce_pair(u, pair, 8 * (G + 2) + 2 * u + pair)
                        if u == 1 and not (first and g == 0):
                            bb, gg = (b, g - 1) if g else (b - 1, NG - 1)
                            normalize(bb, gg, G)
                    if not (last and g >= NG - 2):
                        split_max(G + 2)

                bodies(vec, step)
                normalize(B - 1, NG - 1, NG * B)


def project_phase(nc, ps, s, x_all, z_all, y_all, logits):
    with Phase(nc) as ctx:
        def sb(name, shape, dt=F32):
            return ctx.enter_context(nc.sbuf_tensor(own(nc, name), shape, dt))

        def sem(name):
            return ctx.semaphore(name)

        ln = LayerNorm(nc, ctx, "ln2", ST, EPS)
        y_in, normed = sb("y_in", [P, ST, P]), sb("normed", [P, ST, P])
        yT, h2T, x1 = sb("yT", [P, SW]), sb("h2T", [P, SW]), sb("x1", [P, ST, P])
        y_loaded, y_turned, y_kept, projected, x1_ready, halved = (
            sem("y_loaded"), sem("y_turned"), sem("y_kept"), sem("projected"), sem("x1_ready"), sem("halved"))
        norm_stored, h_turned, h_kept, gated, logits_kept = (
            sem("norm_stored"), sem("h_turned"), sem("h_kept"), sem("gated"), sem("logits_kept"))
        psY, psP, psH, psL = ps[:, 0:2, :], ps[:, 2:4, :], ps[:, 4:6, :], ps[:, 6, 0:ST * E]
        flat = "p a b -> p (a b)"

        def tile(bank_pair, i):
            return bank_pair[:, i // TPB, (i % TPB) * P:(i % TPB + 1) * P]

        with nc.Block() as block:
            @block.sync
            def _(sp):
                sp.dma_start(y_in[:], y_all[:, 0:ST, :]).then_inc(y_loaded, 16)
                with sp.Fori(0, SL - 1) as n:
                    sp.wait_ge(y_turned, n + 1)
                    sp.wait_ge(y_loaded, 16 * n + 16)
                    sp.dma_start(y_in[:], y_all[:, ds((n + 1) * ST, ST), :]).then_inc(y_loaded, 16)
                    ln.wait_done(sp, n)
                    sp.dma_start(y_all[:, ds(n * ST, ST), :], normed[:]).then_inc(norm_stored, 16)
                ln.wait_done(sp, SL - 1)
                sp.dma_start(y_all[:, (SL - 1) * ST:, :], normed[:]).then_inc(norm_stored, 16)
                sp.wait_ge(norm_stored, 16 * SL)

            @block.tensor
            def _(pe):
                t = nc.tensor
                with pe.Fori(0, SL) as n:
                    pe.wait_ge(y_loaded, 16 * n + 16)
                    for i in range(ST):
                        last = t.transpose(tile(psY, i), y_in[:, i, :], s["ident"][:])
                    last.then_inc(y_turned, 1)
                    pe.wait_ge(y_kept, n + 1)
                    for i in range(ST):
                        last = t.matmul(tile(psP, i), yT[:, i * P:(i + 1) * P], s["w_proj"][:], start=True, stop=True)
                    last.then_inc(projected, 1)
                    ln.wait_done(pe, n)
                    for i in range(ST):
                        last = t.transpose(tile(psH, i), normed[:, i, :], s["ident"][:])
                    last.then_inc(h_turned, 1)
                    pe.wait_ge(h_kept, n + 1)
                    for i in range(ST):
                        last = t.matmul(psL[:, i * E:(i + 1) * E], h2T[:, i * P:(i + 1) * P], s["gate_w"][:],
                                        start=True, stop=True)
                    last.then_inc(gated, 1)

            @block.scalar
            def _(act):
                a = nc.scalar
                with act.Fori(0, SL) as n:
                    act.wait_ge(y_turned, n + 1)
                    a.activation(yT[:], psY.rearrange(flat), ACT.Copy).then_inc(y_kept, 1)
                    ln.squares(act, n)
                    act.wait_ge(h_turned, n + 1)
                    a.activation(h2T[:], psH.rearrange(flat), ACT.Identity, bias=s["ln2_b"][:, 0:1],
                                 scale=s["ln2_w"][:, 0:1]).then_inc(h_kept, 1)

            @block.vector
            def _(vec):
                v = nc.vector
                with vec.Fori(0, SL) as n:
                    here = ds(n * ST, ST)
                    vec.wait_ge(projected, n + 1)
                    v.tensor_tensor(x1[:], z_all[:, here, :], psP.rearrange("p a (t c) -> p (a t) c", c=P),
                                    ALU.add).then_inc(x1_ready, 1)
                    vec.wait_ge(x1_ready, n + 1)
                    ln.center(vec, n, x1[:])
                    v.scalar_tensor_tensor(x_all[:, here, :], x1[:], 0.5, x_all[:, here, :], ALU.mult,
                                           ALU.add).then_inc(halved, 1)
                    ln.variance(vec, n)
                    vec.wait_ge(gated, n + 1)
                    v.tensor_tensor(logits[:, here, :], psL.rearrange("p (t e) -> p t e", e=E),
                                    s["gate_b"][:].unsqueeze(1).broadcast_to([P, ST, E]), ALU.add).then_inc(logits_kept, 1)
                vec.wait_ge(logits_kept, SL)
                vec.wait_ge(halved, SL)

            @block.gpsimd
            def _(pool):
                ln.start(pool)
                ln.scale(pool, 0, normed[:])
                with pool.Fori(1, SL) as n:
                    pool.wait_ge(norm_stored, 16 * n)
                    pool.wait_ge(h_turned, n)
                    ln.scale(pool, n, normed[:])


def route_phase(nc, ps, s, y_all, logits, slot, expert, xs):
    with Phase(nc) as ctx:
        def sb(name, shape, dt=F32):
            return ctx.enter_context(nc.sbuf_tensor(own(nc, name), shape, dt))

        def sem(name):
            return ctx.semaphore(name)

        best, first = sb("best", [P, NT]), sb("first", [P, NT])
        equal, one_hot = sb("equal", [P, NT, E]), sb("one_hot", [P, NT, E])
        tile_count, running = sb("tile_count", [P, E, NT]), sb("running", [P, E, NT])
        tiles, tiles_end, base = sb("tiles", [P, E]), sb("tiles_end", [P, E]), sb("base", [P, E])
        place, slot_f, over = sb("place", [P, NT, E]), sb("slot_f", [P, NT]), sb("over", [P, SLOTS, E])
        expert_f = sb("expert_f", [P, SLOTS])
        step, one_hot_ready, ranked, slots_ready, scattered = (
            sem("step"), sem("one_hot_ready"), sem("ranked"), sem("slots_ready"), sem("scattered"))
        rank = ps[:, 0, 0:NT * E]
        count = ps[:, 0, NT * E:2 * NT * E]
        c = s["counts"]

        with nc.Block() as block:
            @block.vector
            def _(vec):
                v = nc.vector
                done = [0]

                def link(ins):
                    done[0] += 1
                    ins.then_inc(step, 1)
                    vec.wait_ge(step, done[0])

                experts = c[:, 0:E].unsqueeze(1)
                link(v.tensor_reduce(best[:], logits[:], AX_X, ALU.max))
                link(v.tensor_tensor(equal[:], logits[:], best[:].unsqueeze(2).broadcast_to([P, NT, E]), ALU.is_equal))
                link(v.tensor_scalar(over[:, 0, :], c[:, 0:E], float(E), None, ALU.subtract))
                link(v.tensor_tensor(equal[:], equal[:], over[:, 0:1, :].broadcast_to([P, NT, E]), ALU.mult))
                link(v.tensor_reduce(first[:], equal[:], AX_X, ALU.min))
                link(v.tensor_tensor(one_hot[:], over[:, 0:1, :].broadcast_to([P, NT, E]),
                                     first[:].unsqueeze(2).broadcast_to([P, NT, E]), ALU.is_equal))
                link(v.tensor_copy(base[:], c[:, 0:E]))
                v.tensor_copy(slot_f[:], first[:]).then_inc(one_hot_ready, 1)
                vec.wait_ge(ranked, 1)
                link(v.tensor_copy(tile_count[:], count.rearrange("p (t e) -> p e t", e=E)))
                link(v.tensor_tensor_scan(running[:].rearrange("p e t -> p (e t)"), s["restart"][:],
                                          tile_count[:].rearrange("p e t -> p (e t)"), 0.0, ALU.mult, ALU.add))
                link(v.tensor_scalar(place[:, :, 0], c[:, 0:NT], float(P), None, ALU.mult))
                total = running[:, :, NT - 1]
                above = equal[:].rearrange("p t e -> p (t e)").rearrange("p (e t) -> p e t", e=E)
                link(v.tensor_tensor(above, total.unsqueeze(2).broadcast_to([P, E, NT]),
                                     place[:, :, 0].unsqueeze(1).broadcast_to([P, E, NT]), ALU.is_gt))
                link(v.tensor_reduce(tiles[:], above, AX_X, ALU.add))
                link(v.tensor_tensor_scan(tiles_end[:], s["ones"][:, 0:E], tiles[:], 0.0, ALU.mult, ALU.add))
                link(v.tensor_tensor(base[:], tiles_end[:], tiles[:], ALU.subtract))
                link(v.tensor_tensor(running[:], running[:], tile_count[:], ALU.subtract))
                link(v.tensor_tensor(place[:], running[:].rearrange("p e t -> p t e"),
                                     rank.rearrange("p (t e) -> p t e", e=E), ALU.add))
                link(v.tensor_scalar(base[:], base[:], float(P), None, ALU.mult))
                link(v.tensor_tensor(place[:], place[:], base[:].unsqueeze(1).broadcast_to([P, NT, E]), ALU.add))
                link(v.tensor_tensor(place[:], place[:], one_hot[:], ALU.mult))
                link(v.tensor_reduce(slot_f[:], place[:], AX_X, ALU.add))
                link(v.tensor_copy(slot[:], slot_f[:]))
                link(v.tensor_tensor(over[:], c[:, 0:SLOTS].unsqueeze(2).broadcast_to([P, SLOTS, E]),
                                     tiles_end[:].unsqueeze(1).broadcast_to([P, SLOTS, E]), ALU.is_ge))
                link(v.tensor_reduce(expert_f[:], over[:], AX_X, ALU.add))
                link(v.tensor_scalar(expert_f[:], expert_f[:], float(E - 1), None, ALU.min))
                v.tensor_copy(expert[:], expert_f[:]).then_inc(slots_ready, 1)

            @block.tensor
            def _(pe):
                t = nc.tensor
                hot = one_hot[:].rearrange("p t e -> p (t e)")
                pe.wait_ge(one_hot_ready, 1)
                t.matmul(rank, s["below"][:], hot, start=True, stop=True)
                t.matmul(count, s["ones"][:], hot, start=True, stop=True).then_inc(ranked, 1)

            @block.gpsimd
            def _(pool):
                pool.wait_ge(slots_ready, 1)
                for i in range(NT):
                    pool.indirect_dma_start(xs, bass.IndirectOffsetOnAxis(ap=slot[:, i:i + 1], axis=0),
                                            y_all[:, i, :], None).then_inc(scattered, 16)
                pool.wait_ge(scattered, 16 * NT)


def expert_phase(nc, ps, s, expert, xs, ys):
    with Phase(nc) as ctx:
        def sb(name, shape, dt=F32):
            return [ctx.enter_context(nc.sbuf_tensor(own(nc, f"{name}{i}"), shape, dt)) for i in range(2)]

        def sem(name):
            return ctx.semaphore(name)

        xt, xT, hid, hidT, yt = sb("xt", [P, P]), sb("xT", [P, P]), sb("hid", [P, HID]), sb("hidT", [P, HID]), sb("yt", [P, P])
        x_loaded, x_turned, xT_kept = [sem("x_loaded0"), sem("x_loaded1")], sem("x_turned"), sem("xT_kept")
        first_done, hid_kept, hid_turned, hidT_kept = (
            sem("first_done"), sem("hid_kept"), sem("hid_turned"), sem("hidT_kept"))
        passed = sem("passed")
        second_done, y_kept, y_stored = sem("second_done"), sem("y_kept"), [sem("y_stored0"), sem("y_stored1")]
        psX, psH, psT, psY = ([ps[:, 2 * k + i, :] for i in range(2)] for k in range(4))

        def pipeline(eng, step, stages):
            for j in range(6):
                step(j, j % 2, lambda k, j=j: j >= k)
            with eng.Fori(3, SLOTS // 2) as pair:
                for i in range(2):
                    step(2 * pair + i, i, lambda k: True)
            for j in range(SLOTS, SLOTS + stages):
                step(j, j % 2, lambda k, j=j: j - k < SLOTS)

        def after(eng, sem_, j, back, per=1):
            if not isinstance(j, int) or j - back >= 0:
                eng.wait_ge(sem_, (j - back + 1) * per)

        with nc.Block() as block:
            @block.sync
            def _(sp):
                def load(j, i):
                    sp.dma_start(xt[i][:], xs[ds(j * P, P), :]).then_inc(x_loaded[i], 16)

                load(0, 0)
                load(1, 1)
                with sp.Fori(1, SLOTS // 2) as pair:
                    for i in range(2):
                        sp.wait_ge(x_turned, 2 * pair + i - 1)
                        load(2 * pair + i, i)

            @block.tensor
            def _(pe):
                t = nc.tensor

                def weights_of(j):
                    return pe.value_load(expert[0:1, ds(j, 1)], min_val=0, max_val=E - 1)

                def step(j, i, present):
                    o = 1 - i
                    if present(0):
                        pe.wait_ge(x_loaded[i], 16 * ((j - i) // 2 + 1) if isinstance(j, int) else 8 * (j - i) + 16)
                        after(pe, xT_kept, j, 2)
                        t.transpose(psX[i][:, 0:P], xt[i][:], s["ident"][:]).then_inc(x_turned, 1)
                    if present(1):
                        after(pe, xT_kept, j, 1)
                        after(pe, hid_kept, j, 3)
                        e = weights_of(j - 1)
                        t.matmul(psH[o], xT[o][:], s["w1"][:, ds(e, 1), :], start=True, stop=True).then_inc(first_done, 1)
                    if present(2):
                        after(pe, hid_kept, j, 2)
                        after(pe, hidT_kept, j, 4)
                        for c in range(HC):
                            last = t.transpose(psT[i][:, c * P:(c + 1) * P], hid[i][:, c * P:(c + 1) * P], s["ident"][:])
                        last.then_inc(hid_turned, 1)
                    if present(3):
                        after(pe, hidT_kept, j, 3)
                        after(pe, y_kept, j, 5)
                        e = weights_of(j - 3)
                        for c in range(HC):
                            last = t.matmul(psY[o][:, 0:P], hidT[o][:, c * P:(c + 1) * P], s["w2"][:, ds(e, 1), c, :],
                                            start=(c == 0), stop=(c == HC - 1))
                        last.then_inc(second_done, 1)

                pipeline(pe, step, 3)

            @block.scalar
            def _(act):
                a = nc.scalar

                def step(j, i, present):
                    o = 1 - i
                    if present(0):
                        after(act, x_turned, j, 0)
                        after(act, first_done, j, 2)
                        a.activation(xT[i][:], psX[i][:, 0:P], ACT.Identity, bias=s["ln2_b"][:, 0:1],
                                     scale=s["ln2_w"][:, 0:1]).then_inc(xT_kept, 1)
                    if present(1):
                        after(act, first_done, j, 1)
                        after(act, hid_turned, j, 3)
                        a.activation(hid[o][:], psH[o], ACT.Gelu_apprx_tanh).then_inc(hid_kept, 1)

                pipeline(act, step, 3)

            @block.vector
            def _(vec):
                v = nc.vector

                def step(j, i, present):
                    o = 1 - i
                    if present(2):
                        after(vec, hid_turned, j, 2)
                        after(vec, second_done, j, 4)
                        v.tensor_copy(hidT[i][:], psT[i]).then_inc(hidT_kept, 1)
                    if present(3):
                        after(vec, second_done, j, 3)
                        if not isinstance(j, int) or j >= 5:
                            vec.wait_ge(y_stored[o], 16 * ((j - 3 - o) // 2) if isinstance(j, int) else 8 * (j - 3 - o))
                        v.tensor_copy(yt[o][:], psY[o][:, 0:P]).then_inc(y_kept, 1)

                pipeline(vec, step, 3)

            @block.gpsimd
            def _(pool):
                with pool.Fori(0, SLOTS // 2) as pair:
                    for i in range(2):
                        wait_apart(pool, passed, (y_kept, 2 * pair + i + 1))
                        pool.dma_start(ys[ds((2 * pair + i) * P, P), :], yt[i][:]).then_inc(y_stored[i], 16)
                for i in range(2):
                    pool.wait_ge(y_stored[i], 16 * (SLOTS // 2))


def combine_phase(nc, x_all, y_all, slot, ys):
    with Phase(nc) as ctx:
        gathered = [ctx.semaphore(f"gathered{i}") for i in range(SL)]
        added = ctx.semaphore("added")
        with nc.Block() as block:
            @block.gpsimd
            def _(pool):
                for i in range(NT):
                    pool.indirect_dma_start(y_all[:, i, :], None, ys,
                                            bass.IndirectOffsetOnAxis(ap=slot[:, i:i + 1], axis=0)
                                            ).then_inc(gathered[i // ST], 16)

            @block.vector
            def _(vec):
                for n in range(SL):
                    vec.wait_ge(gathered[n], 16 * ST)
                    here = slice(n * ST, (n + 1) * ST)
                    nc.vector.scalar_tensor_tensor(x_all[:, here, :], y_all[:, here, :], 0.5, x_all[:, here, :],
                                                   ALU.mult, ALU.add).then_inc(added, 1)
                vec.wait_ge(added, SL)


class Signal:

    def __init__(self, nc, ctx, name, per=1):
        self.sem, self.per = ctx.semaphore(name), per

    def wait(self, eng, b, k=None):
        eng.wait_ge(self.sem, self.per * b + (self.per if k is None else k) + 1)

    def at(self, b, k=None):
        return self.sem, self.per * b + (self.per if k is None else k) + 1

    def free(self, eng, b):
        if not isinstance(b, int) or b > 0:
            self.wait(eng, b, 0)


F_W, F_K, F_V, F_R, F_G = range(5)
LORA = 32
NH, HS = 2, 64
BLOCK = 32
DIAG_LEVELS = 5
LEVELS = 7
GN_EPS = 1e-5 * NH


def turn_phase(nc, ps, s, x_all, zT):
    with Phase(nc) as ctx:
        ln = LayerNorm(nc, ctx, "lnr", ST, EPS)
        normed = ctx.enter_context(nc.sbuf_tensor(own(nc, "r_normed"), [P, ST, P], F32))
        turned, kept, zero = (ctx.semaphore(n) for n in ("r_turned", "r_kept", "r_zero"))
        with nc.Block() as block:
            @block.vector
            def _(vec):
                with vec.Fori(0, SL) as n:
                    ln.center(vec, n, x_all[:, ds(n * ST, ST), :])
                    ln.variance(vec, n)

            @block.scalar
            def _(act):
                with act.Fori(0, SL) as n:
                    ln.squares(act, n)
                    act.wait_ge(turned, n + 1)
                    nc.scalar.activation(zT[:, ds(n * (ST // TPB), ST // TPB), 1:], ps[:, 0:ST // TPB, :],
                                         ACT.Copy).then_inc(kept, 1)

            @block.gpsimd
            def _(pool):
                ln.start(pool)
                nc.gpsimd.memset(zT[:, :, 0:1], 0.0).then_inc(zero, 1)
                ln.scale(pool, 0, normed[:])
                with pool.Fori(1, SL) as n:
                    pool.wait_ge(turned, n)
                    ln.scale(pool, n, normed[:])

            @block.tensor
            def _(pe):
                with pe.Fori(0, SL) as n:
                    ln.wait_done(pe, n)
                    for i in range(ST):
                        last = nc.tensor.transpose(ps[:, i // TPB, (i % TPB) * P:(i % TPB + 1) * P], normed[:, i, :],
                                                   s["ident"][:])
                    last.then_inc(turned, 1)


def recurrence_phase(nc, ps, s, x_all, zT):
    with Phase(nc) as ctx:
        def sb(name, shape, dt=F32):
            return ctx.enter_context(nc.sbuf_tensor(own(nc, "r_" + name), shape, dt))

        def two(name, shape, dt=F32):
            return [sb(f"{name}{i}", shape, dt) for i in range(2)]

        def signal(name, per=1):
            x = Signal(nc, ctx, "r_" + name, per)
            signals.append(x)
            return x

        signals = []
        passed = {e: ctx.semaphore("r_passed_" + e) for e in ("vec", "pool", "pe")}
        dxa, xm, lora, lora4 = sb("dxa", [P, T]), sb("xm", [P, T]), sb("lora", [P, T]), sb("lora4", [LORA, T])
        shift, mixed = two("shift", [P, T]), [sb(f"mixed{f}", [P, T]) for f in range(5)]
        td_hidden, rate, gate_tanh = sb("td_hidden", [HS, T]), sb("rate", [P, T]), sb("gate_tanh", [P, T])
        q0, k0, ru, v_rows, decay, gate = (two("q0", [P, T]), two("k0", [P, T]), two("ru", [P, T]),
                                           two("v_rows", [P, TPB, P]), two("decay", [P, T]), two("gate", [P, T]))
        qx, kx = two("qx", [P, T]), two("kx", [P, T])
        block_decay = [sb(f"block_decay{l}", [P, T >> l]) for l in range(1, LEVELS + 1)]
        q_factor = [sb(f"q_factor{l}", [P, T >> (l + 1), 2]) for l in range(LEVELS)]
        k_factor = [sb(f"k_factor{l}", [P, T >> (l + 1), 2]) for l in range(LEVELS)]
        diag = sb("diag", [P, NH, TPB, BLOCK])
        aT = sb("aT", [P, NH, TPB, P])
        kT = sb("kT", [P, TPB, P])
        state = [sb(f"state{c}", [P, P]) for c in range(1, TPB)]
        gn = LayerNorm(nc, ctx, "gn", TPB * NH, GN_EPS, HS)
        yn, yg, ygT = sb("yn", [P, TPB, P]), sb("yg", [P, T]), sb("ygT", [P, T])

        dxa_ready, xm_ready, shift_ready = signal("dxa_ready"), signal("xm_ready"), signal("shift_ready", 5)
        lora_made, lora_kept, miu_made, mixed_ready = (
            signal("lora_made"), signal("lora_kept", 2), signal("miu_made", 5), signal("mixed_ready", 5))
        td_made, td_kept, w_made, rate_ready, decay_ready = (
            signal("td_made"), signal("td_kept"), signal("w_made"), signal("rate_ready"), signal("decay_ready"))
        k_made, r_made, v_made, g_made = signal("k_made"), signal("r_made"), signal("v_made"), signal("g_made")
        k_kept, r_kept, ru_kept, v_kept, gt_kept, g_kept = (
            signal("k_kept"), signal("r_kept"), signal("ru_kept"), signal("v_kept"), signal("gt_kept"), signal("g_kept"))
        factors, chain = signal("factors", LEVELS), signal("chain", LEVELS)
        q_next, k_next = signal("q_next", LEVELS), signal("k_next", LEVELS)
        level_made, level_kept = signal("level_made", DIAG_LEVELS + 1), signal("level_kept", DIAG_LEVELS + 1)
        far_made, far_kept, near_kept = signal("far_made", 2), signal("far_kept", 3), signal("near_kept", BLOCK // 8)
        kT_made, kT_kept, kv_made, state_step = (
            signal("kT_made"), signal("kT_kept"), signal("kv_made"), signal("state_step", 2 * (TPB - 1)))
        y_made, yn_turned, yg_ready, ygT_ready, out_made, x_added = (
            signal("y_made"), signal("yn_turned"), signal("yg_ready"), signal("ygT_ready"), signal("out_made"),
            signal("x_added"))

        def batches(eng, mix, scan):
            mix(0, 0)
            with eng.Fori(0, B // 2 - 1) as pair:
                mix(2 * pair + 1, 1)
                scan(2 * pair, 0)
                mix(2 * pair + 2, 0)
                scan(2 * pair + 1, 1)
            mix(B - 1, 1)
            scan(B - 2, 0)
            scan(B - 1, 1)

        started, halved = ctx.semaphore("r_started"), ctx.semaphore("r_halved")
        with nc.Block() as block:
            @block.gpsimd
            def _(pool):
                g = nc.gpsimd
                gn.start(pool)
                for x in signals:
                    pool.sem_inc(x.sem, 1)
                n = 0
                for x, value in ([(diag, 0.0), (aT, 0.0)] + [(x, 0.0) for x in state]
                                 + [(x, 1.0) for x in q_factor + k_factor]):
                    g.memset(x[:], value).then_inc(started, 1)
                    n += 1
                pool.wait_ge(started, n)

            @block.vector
            def _(vec):
                nc.vector.tensor_scalar(s["gn_w_half"][:], s["gn_w"][:], 0.5, None, ALU.mult).then_inc(halved, 1)
                nc.vector.tensor_scalar(s["gn_b_half"][:], s["gn_b"][:], 0.5, None, ALU.mult).then_inc(halved, 1)
                vec.wait_ge(halved, 2)

        with nc.Block() as block:
            @block.vector
            def _(vec):
                v = nc.vector

                def mix(b, i):
                    x = zT[:, ds(b, 1), 1:].rearrange("p a t -> p (a t)")
                    before = zT[:, ds(b, 1), 0:T].rearrange("p a t -> p (a t)")
                    shift_ready.free(vec, b)
                    v.tensor_tensor(dxa[:], before, x, ALU.subtract).then_inc(dxa_ready.sem, 1)
                    dxa_ready.wait(vec, b)
                    lora_made.free(vec, b)
                    v.scalar_tensor_tensor(xm[:], dxa[:], s["miu_x"][:, 0:1], x, ALU.mult, ALU.add).then_inc(xm_ready.sem, 1)
                    for f in range(5):
                        miu_made.wait(vec, b, f + 1)
                        if f >= 2:
                            mixed_ready.wait(vec, b, f - 1)
                        else:
                            mixed_ready.free(vec, b)
                        v.scalar_tensor_tensor(shift[f % 2][:], ps[:, MIU_BANK[f], :], s["lambda"][:, f:f + 1], dxa[:],
                                               ALU.add, ALU.mult).then_inc(shift_ready.sem, 1)
                    r_kept.wait(vec, b)
                    if not isinstance(b, int) or b >= 2:
                        level_made.free(vec, b - 1)
                    v.tensor_scalar(ru[i][:], q0[i][:], s["u"][:, 0:1], None, ALU.mult).then_inc(ru_kept.sem, 1)
                    gt_kept.wait(vec, b)
                    if not isinstance(b, int) or b >= 2:
                        ygT_ready.free(vec, b - 1)
                    v.scalar_tensor_tensor(gate[i][:], gate_tanh[:], 1.0, ps[:, G_BANK, :], ALU.add,
                                           ALU.mult).then_inc(g_kept.sem, 1)

                def scan(b, i):
                    decay_ready.wait(vec, b)
                    for l in range(LEVELS):
                        src = decay[i] if l == 0 else block_decay[l - 1]
                        pairs = src[:].rearrange("p (n two) -> p n two", two=2)
                        if l:
                            chain.wait(vec, b, l)
                        else:
                            factors.free(vec, b)
                            state_step.free(vec, b)
                        v.tensor_tensor(block_decay[l][:], pairs[:, :, 0], pairs[:, :, 1], ALU.mult).then_inc(chain.sem, 1)
                    for l in range(LEVELS):
                        src = q0[i] if l == 0 else qx[l % 2]
                        dst = qx[(l + 1) % 2]
                        factors.wait(vec, b, l + 1)
                        if l == 0:
                            r_kept.wait(vec, b)
                            y_made.free(vec, b)
                            q_next.free(vec, b)
                        else:
                            q_next.wait(vec, b, l)
                            if l <= DIAG_LEVELS:
                                level_made.wait(vec, b, l + 1)
                            else:
                                far_made.wait(vec, b, 1)
                        m = 1 << l
                        v.tensor_tensor(dst[:].rearrange("p (n two m) -> p n two m", two=2, m=m).rearrange("p n two m -> p (n two) m"),
                                        src[:].rearrange("p (k m) -> p k m", m=m),
                                        q_factor[l][:].rearrange("p n two -> p (n two)").unsqueeze(2).broadcast_to([P, T // m, m]),
                                        ALU.mult).then_inc(q_next.sem, 1)
                        if l < DIAG_LEVELS + 1:
                            keep_level(b, l)
                    kv_made.wait(vec, b)
                    for c in range(1, TPB):
                        for h in range(NH):
                            at = slice(h * HS, (h + 1) * HS)
                            kv = ps[at, KV_BANK, (c - 1) * P + h * HS:(c - 1) * P + (h + 1) * HS]
                            n = 2 * (c - 1) + h
                            if c == 1:
                                v.tensor_copy(state[0][at, at], kv).then_inc(state_step.sem, 1)
                            else:
                                state_step.wait(vec, b, n - 1)
                                v.scalar_tensor_tensor(state[c - 1][at, at], state[c - 2][at, at],
                                                       block_decay[LEVELS - 1][at, c - 1:c], kv, ALU.mult,
                                                       ALU.add).then_inc(state_step.sem, 1)
                    y_made.wait(vec, b)
                    gn.center(vec, b, ps[:, Y_BANK, :].rearrange("p (n w) -> p n w", w=HS))
                    gn.variance(vec, b)
                    yn_turned.wait(vec, b)
                    ygT_ready.free(vec, b)
                    v.tensor_scalar(yg[:], ps[:, YT_BANK, :], s["gn_w_half"][:, 0:1], s["gn_b_half"][:, 0:1], ALU.mult,
                                    ALU.add).then_inc(yg_ready.sem, 1)
                    yg_ready.wait(vec, b)
                    out_made.free(vec, b)
                    v.tensor_tensor(ygT[:], yg[:], gate[i][:], ALU.mult).then_inc(ygT_ready.sem, 1)
                    out_made.wait(vec, b)
                    here = x_all[:, ds(b * TPB, TPB), :]
                    v.tensor_tensor(here, here, ps[:, OUT_BANK, :].rearrange("p (t c) -> p t c", c=P),
                                    ALU.add).then_inc(x_added.sem, 1)

                def keep_level(b, l):
                    wait_apart(vec, passed["vec"], level_made.at(b, l + 1), level_kept.at(b, l), near_kept.at(b, 0))
                    bank = LEVEL_BANKS[l % 2]
                    v.copy_predicated(diag[:], s["level_masks"][:, l, :].unsqueeze(1).unsqueeze(1).broadcast_to([P, NH, TPB, BLOCK]),
                                      ps[:, bank:bank + NH, 0:TPB * BLOCK].rearrange("p h (c w) -> p h c w", c=TPB)
                                      ).then_inc(level_kept.sem, 1)

                batches(vec, mix, scan)
                x_added.wait(vec, B - 1)

            @block.gpsimd
            def _(pool):
                g = nc.gpsimd

                def mix(b, i):
                    x = zT[:, ds(b, 1), 1:].rearrange("p a t -> p (a t)")
                    users = (td_made, k_made, v_made, r_made, g_made)
                    for f in range(5):
                        wait_apart(pool, passed["pool"], shift_ready.at(b, f + 1), users[f].at(b, 0))
                        g.tensor_tensor(mixed[f][:], shift[f % 2][:], x, ALU.add).then_inc(mixed_ready.sem, 1)

                def scan(b, i):
                    for l in range(LEVELS):
                        src = k0[i] if l == 0 else kx[l % 2]
                        dst = kx[(l + 1) % 2]
                        factors.wait(pool, b, l + 1)
                        if l == 0:
                            k_kept.wait(pool, b)
                            kT_made.free(pool, b)
                        else:
                            k_next.wait(pool, b, l)
                            if l <= DIAG_LEVELS:
                                level_made.wait(pool, b, l + 1)
                            else:
                                far_made.wait(pool, b, 1)
                        m = 1 << l
                        g.tensor_tensor(dst[:].rearrange("p (k m) -> p k m", m=m), src[:].rearrange("p (k m) -> p k m", m=m),
                                        k_factor[l][:].rearrange("p n two -> p (n two)").unsqueeze(2).broadcast_to([P, T // m, m]),
                                        ALU.mult).then_inc(k_next.sem, 1)
                    gn.scale(pool, b, yn[:].rearrange("p c (h w) -> p (c h) w", w=HS))

                batches(pool, mix, scan)

            @block.scalar
            def _(act):
                a = nc.scalar

                def mix(b, i):
                    lora_made.wait(act, b)
                    miu_made.free(act, b)
                    a.activation(lora[:], ps[:, 0, :], ACT.Tanh).then_inc(lora_kept.sem, 1)
                    a.activation(lora4[:], ps[0:LORA, 1, :], ACT.Tanh).then_inc(lora_kept.sem, 1)
                    td_made.wait(act, b)
                    w_made.free(act, b)
                    a.activation(td_hidden[:], ps[0:HS, TD_BANK, :], ACT.Tanh).then_inc(td_kept.sem, 1)
                    w_made.wait(act, b)
                    decay_ready.free(act, b)
                    a.activation(rate[:], ps[:, W_BANK, :], ACT.Exp, bias=s["td_miu"][:, 0:1]).then_inc(rate_ready.sem, 1)
                    rate_ready.wait(act, b)
                    if not isinstance(b, int) or b >= 2:
                        factors.free(act, b - 1)
                        chain.free(act, b - 1)
                    a.activation(decay[i][:], rate[:], ACT.Exp, scale=-1.0).then_inc(decay_ready.sem, 1)
                    k_made.wait(act, b)
                    if not isinstance(b, int) or b >= 2:
                        level_made.free(act, b - 1)
                        k_next.free(act, b - 1)
                        q_next.free(act, b - 1)
                        y_made.free(act, b - 1)
                    a.activation(k0[i][:], ps[:, K_BANK, :], ACT.Copy).then_inc(k_kept.sem, 1)
                    v_made.wait(act, b)
                    a.activation(v_rows[i][:].rearrange("p c w -> p (c w)"), ps[:, V_BANK, :], ACT.Copy).then_inc(v_kept.sem, 1)
                    r_made.wait(act, b)
                    a.activation(q0[i][:], ps[:, R_BANK, :], ACT.Copy).then_inc(r_kept.sem, 1)
                    g_made.wait(act, b)
                    g_kept.free(act, b)
                    a.activation(gate_tanh[:], ps[:, G_BANK, :], ACT.Tanh, scale=0.5).then_inc(gt_kept.sem, 1)

                def scan(b, i):
                    for l in range(LEVELS):
                        src = decay[i] if l == 0 else block_decay[l - 1]
                        pairs = src[:].rearrange("p (n two) -> p n two", two=2)
                        if l:
                            chain.wait(act, b, l)
                        else:
                            decay_ready.wait(act, b)
                            q_next.free(act, b)
                            k_next.free(act, b)
                        a.activation(q_factor[l][:, :, 1], pairs[:, :, 0], ACT.Copy)
                        a.activation(k_factor[l][:, :, 0], pairs[:, :, 1], ACT.Copy).then_inc(factors.sem, 1)
                    kT_made.wait(act, b)
                    kv_made.free(act, b)
                    a.activation(kT[:].rearrange("p c w -> p (c w)"), ps[:, KT_BANK, :], ACT.Copy).then_inc(kT_kept.sem, 1)
                    far_made.wait(act, b)
                    y_made.free(act, b)
                    bank = LEVEL_BANKS[0]
                    far = ps[:, bank:bank + NH, :].rearrange("p h (c t) -> p h c t", c=TPB)
                    for at, to in ((slice(0, 32), slice(32, 64)), (slice(64, 96), slice(96, 128)), (slice(0, 64), slice(64, 128))):
                        a.activation(aT[at, :, :, to], far[at, :, :, to], ACT.Copy).then_inc(far_kept.sem, 1)
                    level_kept.wait(act, b)
                    for q in range(P // BLOCK):
                        at = slice(q * BLOCK, (q + 1) * BLOCK)
                        a.activation(aT[at, :, :, at], diag[at, :, :, :], ACT.Copy).then_inc(near_kept.sem, 1)
                    gn.squares(act, b)

                batches(act, mix, scan)

            @block.tensor
            def _(pe):
                t = nc.tensor

                def mix(b, i):
                    def project(bank, weights, f, made, rows=P):
                        mixed_ready.wait(pe, b, f + 1)
                        t.matmul(ps[0:rows, bank, :], weights, mixed[f][:], start=True, stop=True).then_inc(made.sem, 1)

                    xm_ready.wait(pe, b)
                    g_kept.free(pe, b)
                    shift_ready.free(pe, b)
                    t.matmul(ps[:, 0, :], s["A_lora"][:, 0:P], xm[:], start=True, stop=True)
                    k_kept.free(pe, b)
                    t.matmul(ps[0:LORA, 1, :], s["A_lora"][:, P:], xm[:], start=True, stop=True).then_inc(lora_made.sem, 1)
                    lora_kept.wait(pe, b)
                    r_kept.free(pe, b)
                    ru_kept.free(pe, b)
                    v_kept.free(pe, b)
                    for f in range(5):
                        if f == 4:
                            shift_ready.wait(pe, b, 1)
                            rows, lhsT, rhs = LORA, s["B_lora4"][:], lora4[:]
                        else:
                            rows, lhsT, rhs = P, s["B_lora"][:, f, :], lora[:]
                        t.matmul(ps[:, MIU_BANK[f], :], lhsT, rhs, start=True, stop=True).then_inc(miu_made.sem, 1)
                    shift_ready.wait(pe, b, F_K + 1)
                    project(TD_BANK, s["td_A"][:], F_W, td_made, HS)
                    td_kept.wait(pe, b)
                    shift_ready.wait(pe, b, F_V + 1)
                    t.matmul(ps[:, W_BANK, :], s["td_B"][:], td_hidden[:], start=True, stop=True).then_inc(w_made.sem, 1)
                    shift_ready.wait(pe, b, F_R + 1)
                    project(K_BANK, s["WkT"][:], F_K, k_made)
                    mixed_ready.wait(pe, b, F_V + 1)
                    for c in range(TPB):
                        last = t.matmul(ps[:, V_BANK, c * P:(c + 1) * P], mixed[F_V][:, c * P:(c + 1) * P], s["WvT"][:],
                                        start=True, stop=True)
                    last.then_inc(v_made.sem, 1)
                    shift_ready.wait(pe, b, F_G + 1)
                    project(R_BANK, s["WrT"][:], F_R, r_made)
                    rate_ready.wait(pe, b)
                    project(G_BANK, s["WgT"][:], F_G, g_made)

                def scan(b, i):
                    for l in range(DIAG_LEVELS + 1):
                        bank = LEVEL_BANKS[l % 2]
                        if l == 0:
                            needs = [ru_kept.at(b), k_kept.at(b), x_added.at(b, 0)]
                            q, k = ru[i], k0[i]
                        elif l == 1:
                            needs = [r_kept.at(b), (gn.done, b + 1), yg_ready.at(b, 0)]
                            q, k = q0[i], k0[i]
                        else:
                            needs = [q_next.at(b, l - 1), k_next.at(b, l - 1), level_kept.at(b, l - 1)]
                            q, k = qx[(l - 1) % 2], kx[(l - 1) % 2]
                        wait_apart(pe, passed["pe"], *needs)
                        for c in range(TPB):
                            for block_ in range(P // BLOCK):
                                for h in range(NH):
                                    at = slice(h * HS, (h + 1) * HS)
                                    tok = slice(c * P + block_ * BLOCK, c * P + (block_ + 1) * BLOCK)
                                    last = t.matmul(ps[block_ * BLOCK:(block_ + 1) * BLOCK, bank + h, c * BLOCK:(c + 1) * BLOCK],
                                                    k[at, tok], q[at, tok], start=True, stop=True)
                        last.then_inc(level_made.sem, 1)
                    bank = LEVEL_BANKS[0]
                    for half in (BLOCK, 2 * BLOCK):
                        l = 5 if half == BLOCK else 6
                        wait_apart(pe, passed["pe"], q_next.at(b, l), k_next.at(b, l), level_kept.at(b, DIAG_LEVELS))
                        q, k = qx[l % 2], kx[l % 2]
                        for c in range(TPB):
                            for first in range(0, P, 2 * half):
                                for h in range(NH):
                                    at = slice(h * HS, (h + 1) * HS)
                                    last = t.matmul(ps[first:first + half, bank + h, c * P + first + half:c * P + first + 2 * half],
                                                    k[at, c * P + first:c * P + first + half],
                                                    q[at, c * P + first + half:c * P + first + 2 * half],
                                                    start=True, stop=True)
                        last.then_inc(far_made.sem, 1)
                    k_next.wait(pe, b, LEVELS)
                    level_kept.wait(pe, b)
                    for c in range(TPB):
                        last = t.transpose(ps[:, KT_BANK, c * P:(c + 1) * P], kx[LEVELS % 2][:, c * P:(c + 1) * P], s["ident"][:])
                    last.then_inc(kT_made.sem, 1)
                    kT_kept.wait(pe, b)
                    v_kept.wait(pe, b)
                    for c in range(TPB - 1):
                        last = t.matmul(ps[:, KV_BANK, c * P:(c + 1) * P], kT[:, c, :], v_rows[i][:, c, :], start=True, stop=True)
                    last.then_inc(kv_made.sem, 1)
                    far_kept.wait(pe, b)
                    near_kept.wait(pe, b)
                    q_next.wait(pe, b, LEVELS)
                    for c in range(TPB):
                        to = c * P
                        if c:
                            state_step.wait(pe, b, 2 * c)
                            t.matmul(ps[:, Y_BANK, to:to + P], qx[LEVELS % 2][:, to:to + P], state[c - 1][:], start=True, stop=False)
                        for h in range(NH):
                            last = t.matmul(ps[:, Y_BANK, to + h * HS:to + (h + 1) * HS], aT[:, h, c, :],
                                            v_rows[i][:, c, h * HS:(h + 1) * HS], start=(c == 0), stop=(c == 0 or h == NH - 1))
                    last.then_inc(y_made.sem, 1)
                    gn.wait_done(pe, b)
                    for c in range(TPB):
                        last = t.transpose(ps[:, YT_BANK, c * P:(c + 1) * P], yn[:, c, :], s["ident"][:])
                    last.then_inc(yn_turned.sem, 1)
                    ygT_ready.wait(pe, b)
                    for c in range(TPB):
                        last = t.matmul(ps[:, OUT_BANK, c * P:(c + 1) * P], ygT[:, c * P:(c + 1) * P], s["WoT"][:],
                                        start=True, stop=True)
                    last.then_inc(out_made.sem, 1)

                batches(pe, mix, scan)


MIU_BANK = (2, 3, 0, 1, 2)
TD_BANK, W_BANK, K_BANK, V_BANK, R_BANK, G_BANK = 3, 0, 1, 3, 2, 0
LEVEL_BANKS = (4, 6)
KT_BANK, KV_BANK, Y_BANK, YT_BANK, OUT_BANK = 6, 7, 6, 7, 4


def program(nc, d, out):
    with Phase(nc) as ctx:
        def sb(name, shape, dt=F32):
            return ctx.enter_context(nc.sbuf_tensor(own(nc, name), shape, dt))

        ps = ctx.enter_context(nc.psum_tensor("ps", [P, 8, 512], F32))
        x_all, z_all = sb("x_all", [P, NT, P]), sb("z_all", [P, NT, P])
        y_all = sb("y_all", [P, NT, P])
        qd = nc.dram_tensor("q_split", (P, SPLITS, TOK), BF16, kind="Internal").ap()
        kd = nc.dram_tensor("k_split", (P, SPLITS, TOK), BF16, kind="Internal").ap()
        xs = nc.dram_tensor("sorted_in", (SLOTS * P, P), F32, kind="Internal").ap()
        ys = nc.dram_tensor("sorted_out", (SLOTS * P, P), F32, kind="Internal").ap()
        s = load_constants(nc, ctx, d, y_all, xs)
        logits, slot, expert = sb("logits", [P, NT, E]), sb("slot", [P, NT], I32), sb("expert", [P, SLOTS], I32)

        def ffn(x_dram):
            with ExitStack() as inner:
                v_all = inner.enter_context(nc.sbuf_tensor(own(nc, "v_all"), [P, NT, H, DK + 1], F32))
                qkv_phase(nc, ps, s, x_all, z_all, v_all, x_dram, qd, kd)
                attention_phase(nc, ps, s, v_all, y_all, qd, kd)
            project_phase(nc, ps, s, x_all, z_all, y_all, logits)
            route_phase(nc, ps, s, y_all, logits, slot, expert, xs)
            expert_phase(nc, ps, s, expert, xs, ys)
            combine_phase(nc, x_all, y_all, slot, ys)

        ffn(d["L0_attn_x"])
        with ExitStack() as inner:
            zT = inner.enter_context(nc.sbuf_tensor("zT", [P, B, T + 1], F32))
            turn_phase(nc, ps, s, x_all, zT)
            recurrence_phase(nc, ps, s, x_all, zT)
        ffn(None)
        out_stored = ctx.semaphore("out_stored")
        with nc.Block() as block:
            @block.sync
            def _(sp):
                sp.dma_start(out.rearrange("b t c -> (b t) c").rearrange("(n p) c -> p n c", p=P), x_all[:]).then_inc(out_stored, 16)
                sp.wait_ge(out_stored, 16)


_INS = ['L0_attn_x', 'L0_ffn_w_qkv', 'L0_ffn_w_proj', 'L0_ffn_ln1_w', 'L0_ffn_ln1_b', 'L0_ffn_ln2_w', 'L0_ffn_ln2_b',
        'L0_attn_miu_x', 'L0_attn_A_lora', 'L0_attn_B_lora', 'L0_attn_td_miu', 'L0_attn_td_A', 'L0_attn_td_B',
        'L0_attn_u', 'L0_attn_gn_gamma', 'L0_attn_gn_beta', 'L0_ffn_gate_w', 'L0_ffn_gate_b', 'L0_ffn_w1', 'L0_ffn_w2']


def kernel(**inputs):
    import numpy as _np
    import concourse.bacc as _bacc
    from concourse import mybir as _mybir
    from concourse.bass_utils import run_bass_kernel_spmd as _run

    nc = _bacc.Bacc("TRN2", target_bir_lowering=False, num_devices=1)
    arrays, d = {}, {}

    def give(name, a):
        a = _np.ascontiguousarray(a)
        arrays[f"in_{name}"] = a
        d[name] = nc.dram_tensor(f"in_{name}", a.shape, _mybir.dt.from_np(a.dtype), kind="ExternalInput").ap()

    for name in _INS:
        give(name, inputs[name])
    for name in ("Wk", "Wv", "Wr", "Wg", "Wo"):
        give(name + "T", _np.asarray(inputs["L0_attn_" + name]).T)
    give("lambda_columns", _np.asarray(inputs["L0_attn_lambda_"]).reshape(5, P).T)
    give("ident", _np.eye(P, dtype=_np.float32))
    give("below", _np.triu(_np.ones((P, P), _np.float32), 1))
    give("counts", _np.tile(_np.arange(SLOTS, dtype=_np.float32), (P, 1)))
    give("restart", _np.tile((_np.arange(E * NT) % NT != 0).astype(_np.float32), (P, 1)))
    key, query = _np.arange(P)[:, None] % BLOCK, _np.arange(BLOCK)[None, :]
    masks = [key == query]
    for level in range(DIAG_LEVELS):
        m = 1 << level
        masks.append((key // (2 * m) == query // (2 * m)) & (key % (2 * m) < m) & (query % (2 * m) >= m))
    give("level_masks", _np.stack(masks, axis=1).astype(_np.int32))
    out = nc.dram_tensor("out_0", (8, 512, 128), _mybir.dt.float32, kind="ExternalOutput").ap()
    program(nc, d, out)
    r = _run(nc, [arrays], core_ids=[0])
    return r.results[0]["out_0"]
```

```python
from contextlib import ExitStack

import concourse.bass as bass
from concourse import mybir

F32 = mybir.dt.float32
BF16 = mybir.dt.bfloat16
I32 = mybir.dt.int32
ALU = mybir.AluOpType
ACT = mybir.ActivationFunctionType
AX_X = mybir.AxisListType.X
ds = bass.ds

P = 128
B, T = 8, 512
TOK = B * T
NT = TOK // P
TPB = T // P
H, DK = 16, 8
GROUP = 4
NG = H // GROUP
SPLITS = 3
ROWS = SPLITS * SPLITS * DK
MAXROW = 96
STACK = MAXROW + SPLITS
VW = 32
E, HID = 8, 512
HC = HID // P
SLOTS = TOK // P + E
EPS = 1e-5
SL = 8
ST = NT // SL
SW = ST * P


def own(nc, name):
    return f"{name}_{nc.next_id()}"


class Phase(ExitStack):

    def __init__(self, nc):
        super().__init__()
        self.nc, self.semaphores = nc, []

    def semaphore(self, name):
        self.semaphores.append(self.nc.alloc_semaphore(own(self.nc, name)))
        return self.semaphores[-1]

    def __exit__(self, *failure):
        if failure[0] is None:
            self.nc.clear_and_free_semaphores(self.semaphores)
            self.nc.all_engine_barrier()
        return super().__exit__(*failure)


def wait_apart(eng, passed, *waits):
    for sem, value in waits:
        eng.wait_ge(sem, value)
    eng.sem_inc(passed, 1)


def pipeline(eng, count, stages, step):
    peeled = stages + stages % 2 + 2
    for j in range(peeled):
        step(j, j % 2, lambda k, j=j: j >= k)
    with eng.Fori(peeled // 2, count // 2) as pair:
        for i in range(2):
            step(2 * pair + i, i, lambda k: True)
    for j in range(count, count + stages):
        step(j, j % 2, lambda k, j=j: j - k < count)


def after(eng, sem, j, back=0, per=1):
    if not isinstance(j, int) or j - back >= 0:
        eng.wait_ge(sem, (j - back + 1) * per)


def after_same_parity(eng, sem, j, i, back=0, per=16):
    if not isinstance(j, int) or j - back >= 0:
        eng.wait_ge(sem, (j - back - i) * (per // 2) + per)


class LayerNorm:

    def __init__(self, nc, ctx, name, tiles, eps, width=P, bufs=1):
        self.nc, self.tiles, self.eps, self.width, self.bufs = nc, tiles, eps, width, bufs

        def sb(what, shape, dt=F32):
            return ctx.enter_context(nc.sbuf_tensor(own(nc, f"{name}_{what}"), shape, dt))

        self.total, self.mean = sb("total", [P, tiles]), sb("mean", [P, tiles])
        self.square_sum, self.power = sb("square_sum", [P, tiles]), sb("power", [P, tiles])
        self.square = sb("square", [P, tiles, width])
        self.var, self.rstd = sb("var", [P, bufs, tiles]), sb("rstd", [P, bufs, tiles])
        self.centered = [sb(f"centered{i}", [P, tiles, width]) for i in range(bufs)]

        def sem(what):
            return ctx.semaphore(f"{name}_{what}")

        self.passed = sem("passed")
        self.mean_step, self.sum_step, self.pool_step = sem("mean_step"), sem("sum_step"), sem("pool_step")
        self.is_centered, self.is_squared = sem("is_centered"), sem("is_squared")
        self.var_ready, self.done = sem("var_ready"), sem("done")

    def wide(self, a):
        return a.unsqueeze(2).broadcast_to([P, self.tiles, self.width])

    def start(self, pool):
        self.nc.gpsimd.memset(self.power[:], -0.5).then_inc(self.done, 1)

    def center(self, vec, n, src, i=0):
        v = self.nc.vector
        v.tensor_reduce(self.total[:], src, AX_X, ALU.add).then_inc(self.mean_step, 1)
        vec.wait_ge(self.mean_step, 2 * n + 1)
        v.tensor_scalar(self.mean[:], self.total[:], 1.0 / self.width, None, ALU.mult).then_inc(self.mean_step, 1)
        vec.wait_ge(self.mean_step, 2 * n + 2)
        if not isinstance(n, int) or n >= self.bufs:
            vec.wait_ge(self.done, n - self.bufs + 2)
        v.tensor_tensor(self.centered[i][:], src, self.wide(self.mean[:]), ALU.subtract).then_inc(self.is_centered, 1)

    def squares(self, act, n, i=0):
        act.wait_ge(self.is_centered, n + 1)
        self.nc.scalar.activation(self.square[:], self.centered[i][:], ACT.Square).then_inc(self.is_squared, 1)

    def variance(self, vec, n, i=0):
        v = self.nc.vector
        vec.wait_ge(self.is_squared, n + 1)
        if self.bufs > 1 and (not isinstance(n, int) or n >= 1):
            vec.wait_ge(self.var_ready, n)
        v.tensor_reduce(self.square_sum[:], self.square[:], AX_X, ALU.add).then_inc(self.sum_step, 1)
        vec.wait_ge(self.sum_step, n + 1)
        v.tensor_scalar(self.var[:, i, :], self.square_sum[:], 1.0 / self.width, self.eps, ALU.mult,
                        ALU.add).then_inc(self.var_ready, 1)

    def scale(self, pool, n, dst, i=0, *waits):
        g = self.nc.gpsimd
        pool.wait_ge(self.var_ready, n + 1)
        pool.wait_ge(self.done, n + 1)
        g.tensor_tensor(self.rstd[:, i, :], self.var[:, i, :], self.power[:], ALU.pow).then_inc(self.pool_step, 1)
        wait_apart(pool, self.passed, (self.pool_step, n + 1), *waits)
        g.tensor_tensor(dst, self.centered[i][:], self.wide(self.rstd[:, i, :]), ALU.mult).then_inc(self.done, 1)

    def wait_done(self, eng, n):
        eng.wait_ge(self.done, n + 2)

    def done_free(self, eng, n):
        eng.wait_ge(self.done, n + 1)


def load_constants(nc, ctx, d, zeros, xs):
    s = {}

    def sb(name, shape, dt=F32):
        s[name] = ctx.enter_context(nc.sbuf_tensor(own(nc, name), shape, dt))
        return s[name]

    loads = [(sb("ident", [P, P]), d["ident"]), (sb("w_qkv", [P, 3 * P]), d["w_qkv"]),
             (sb("w_proj", [P, P]), d["L0_ffn_w_proj"])]
    for name in ("ln1_w", "ln1_b", "ln2_w", "ln2_b"):
        loads.append((sb(name, [P, 1]), d["L0_ffn_" + name].rearrange("(c a) -> c a", a=1)))
    loads += [(sb("gate_w", [P, E]), d["L0_ffn_gate_w"]),
              (sb("gate_b", [P, E]), d["L0_ffn_gate_b"].rearrange("(a e) -> a e", a=1).broadcast_to([P, E])),
              (sb("below", [P, P]), d["below"]),
              (sb("counts", [P, SLOTS]), d["counts"]), (sb("restart", [P, E * NT]), d["restart"]),
              (sb("w1", [P, E, HID]), d["L0_ffn_w1"].rearrange("e c h -> c e h")),
              (sb("w2", [P, E, HC, P]), d["L0_ffn_w2"].rearrange("e (k c) d -> c e k d", c=P))]
    a = "L0_attn_"
    for name in ("WkT", "WvT", "WrT", "WgT", "WoT"):
        loads.append((sb(name, [P, P]), d[name]))
    loads += [(sb("A_lora", [P, 5 * LORA]), d[a + "A_lora"]), (sb("td_A", [P, HS]), d[a + "td_A"]),
              (sb("td_B", [HS, P]), d[a + "td_B"]), (sb("B_lora4", [LORA, P]), d[a + "B_lora"][4]),
              (sb("lambda", [P, 5]), d["lambda_columns"]), (sb("miu_x", [P, 1]), d[a + "miu_x"].rearrange("a b c -> c (a b)")),
              (sb("td_miu", [P, 1]), d[a + "td_miu"].rearrange("a b c -> c (a b)")),
              (sb("u", [P, 1]), d[a + "u"].rearrange("h (n a) -> (h n) a", a=1)),
              (sb("gn_w", [P, 1]), d[a + "gn_gamma"].rearrange("(c a) -> c a", a=1)),
              (sb("gn_b", [P, 1]), d[a + "gn_beta"].rearrange("(c a) -> c a", a=1)),
              (sb("level_masks", [P, DIAG_LEVELS + 1, BLOCK], I32), d["level_masks"])]
    sb("B_lora", [P, 4, P])
    sb("gn_w_half", [P, 1])
    sb("gn_b_half", [P, 1])
    sb("ident16", [P, P], BF16)
    sb("ones", [P, P])
    loaded = ctx.semaphore("constants_loaded")
    cast = ctx.semaphore("ident_cast")
    zeros_set, zeroed = ctx.semaphore("zeros_set"), ctx.semaphore("zeroed")
    with nc.Block() as block:
        @block.sync
        def _(sp):
            for dst, src in loads:
                sp.dma_start(dst[:], src).then_inc(loaded, 16)
            sp.wait_ge(zeros_set, 2)
            for f in range(4):
                at = slice(f * LORA, (f + 1) * LORA)
                sp.dma_start(s["B_lora"][at, f, :], d[a + "B_lora"][f]).then_inc(loaded, 16)
            sp.wait_ge(loaded, 16 * (len(loads) + 4))

        @block.vector
        def _(vec):
            vec.wait_ge(loaded, 16 * (len(loads) + 4))
            nc.vector.tensor_copy(s["ident16"][:], s["ident"][:]).then_inc(cast, 1)
            nc.vector.memset(s["ones"][:], 1.0).then_inc(cast, 1)
            vec.wait_ge(cast, 2)

        @block.gpsimd
        def _(pool):
            nc.gpsimd.memset(s["B_lora"][:], 0.0).then_inc(zeros_set, 1)
            nc.gpsimd.memset(zeros[:], 0.0).then_inc(zeros_set, 1)
            pool.wait_ge(zeros_set, 2)
            rows = xs.rearrange("(n p) c -> p n c", p=P)
            for i in range(0, SLOTS, NT // 4):
                pool.dma_start(rows[:, i:i + NT // 4, :], zeros[:, 0:NT // 4, :]).then_inc(zeroed, 16)
            pool.wait_ge(zeroed, 16 * (SLOTS // (NT // 4)))
    return s


def qkv_phase(nc, ps, s, x_all, z_all, v_all, x_dram, qd, kd):
    with Phase(nc) as ctx:
        def sb(name, shape, dt=F32):
            return ctx.enter_context(nc.sbuf_tensor(own(nc, name), shape, dt))

        sems = []

        def sem(name):
            x = ctx.semaphore(name)
            sems.append(x)
            return x

        def sbs(name, shape, dt=F32):
            return [sb(f"{name}{i}", shape, dt) for i in range(2)]

        def sem(name):
            return ctx.semaphore(name)

        lna = LayerNorm(nc, ctx, "lna", ST, EPS, bufs=2)
        lnb = LayerNorm(nc, ctx, "lnb", ST, EPS, bufs=2)
        zn, hT = sbs("zn", [P, ST, P]), sbs("hT", [P, SW])
        parts = {k: sbs(k + "_parts", [P, SPLITS, SW], BF16) for k in "qk"}
        rest = {k: sbs(k + "_rest", [P, SW]) for k in "qk"}
        x_loaded = [sem("x_loaded0"), sem("x_loaded1")]
        ones_set, turned, h_ready = sem("ones_set"), sem("turned"), sem("h_ready")
        made = {k: sem(k + "_made") for k in "qkv"}
        high, mid, low, diff = ({k: sem(k + w) for k in "qk"} for w in ("_high", "_mid", "_low", "_diff"))
        v_kept, stored = sem("v_kept"), {k: [sem(k + "_stored0"), sem(k + "_stored1")] for k in "qk"}
        psT, psV = [ps[:, i, :] for i in range(2)], [ps[:, 6 + i, :] for i in range(2)]
        psX = {"q": [ps[:, 2 + i, :] for i in range(2)], "k": [ps[:, 4 + i, :] for i in range(2)]}

        with nc.Block() as block:
            @block.sync
            def _(sp):
                def load(n, i):
                    sp.dma_start(x_all[:, ds(n * ST, ST), :], src[:, ds(n * ST, ST), :]).then_inc(x_loaded[i], 16)

                def step(j, i, present):
                    o = 1 - i
                    if x_dram is not None and present(0):
                        after_same_parity(sp, x_loaded[i], j, i, 2)
                        load(j, i)
                    if present(3):
                        for k, dram in (("q", qd), ("k", kd)):
                            after(sp, low[k], j, 3)
                            sp.dma_start(dram.rearrange("(c i) h t -> (i h) c t", i=DK)[:, :, ds((j - 3) * SW, SW)],
                                         parts[k][o][:]).then_inc(stored[k][o], 16)

                if x_dram is not None:
                    src = x_dram.rearrange("b t c -> (b t) c").rearrange("(n p) c -> p n c", p=P)
                pipeline(sp, SL, 3, step)
                for k in "qk":
                    for i in range(2):
                        sp.wait_ge(stored[k][i], 16 * SL // 2)

            @block.vector
            def _(vec):
                v = nc.vector

                def step(j, i, present):
                    o = 1 - i
                    if present(0):
                        if x_dram is not None:
                            after_same_parity(vec, x_loaded[i], j, i)
                        lna.center(vec, j, x_all[:, ds(j * ST, ST), :], i)
                    if present(1):
                        lna.wait_done(vec, j - 1)
                        lnb.center(vec, j - 1, z_all[:, ds((j - 1) * ST, ST), :], o)
                    if present(3):
                        after(vec, made["v"], j, 3)
                        v.tensor_copy(v_all[:, ds((j - 3) * ST, ST), :, 0:DK],
                                      psV[o].rearrange("p (t h d) -> p t h d", h=H, d=DK)).then_inc(v_kept, 1)
                        for k in "qk":
                            after(vec, high[k], j, 3)
                            after(vec, low[k], j, 5)
                            v.tensor_tensor(rest[k][o][:], psX[k][o], parts[k][o][:, 0, :],
                                            ALU.subtract).then_inc(diff[k], 1)
                    if present(0):
                        lna.variance(vec, j, i)
                    if present(1):
                        lnb.variance(vec, j - 1, o)

                vec.wait_ge(ones_set, 1)
                pipeline(vec, SL, 3, step)

            @block.scalar
            def _(act):
                a = nc.scalar

                def step(j, i, present):
                    o = 1 - i
                    if present(3):
                        for k in "qk":
                            after(act, made[k], j, 3)
                            after_same_parity(act, stored[k][o], j - 3, o, 2)
                            a.activation(parts[k][o][:, 0, :], psX[k][o], ACT.Copy).then_inc(high[k], 1)
                    if present(0):
                        lna.squares(act, j, i)
                    if present(1):
                        lnb.squares(act, j - 1, o)
                    if present(2):
                        after(act, turned, j, 2)
                        after(act, made["v"], j, 4)
                        a.activation(hT[i][:], psT[i], ACT.Identity, bias=s["ln1_b"][:, 0:1],
                                     scale=s["ln1_w"][:, 0:1]).then_inc(h_ready, 1)
                    if present(3):
                        for k in "qk":
                            after(act, diff[k], j, 3)
                            a.activation(parts[k][o][:, 1, :], rest[k][o][:], ACT.Copy).then_inc(mid[k], 1)

                pipeline(act, SL, 3, step)

            @block.gpsimd
            def _(pool):
                g = nc.gpsimd

                def step(j, i, present):
                    o = 1 - i
                    if present(0):
                        lna.scale(pool, j, z_all[:, ds(j * ST, ST), :], i)
                    if present(1):
                        free = [] if isinstance(j, int) and j < 3 else [(turned, j - 2)]
                        lnb.scale(pool, j - 1, zn[o][:], o, *free)
                    if present(3):
                        for k in "qk":
                            after(pool, mid[k], j, 3)
                            g.tensor_tensor(parts[k][o][:, 2, :], rest[k][o][:], parts[k][o][:, 1, :],
                                            ALU.subtract).then_inc(low[k], 1)

                lna.start(pool)
                lnb.start(pool)
                g.memset(v_all[:], 1.0).then_inc(ones_set, 1)
                pipeline(pool, SL, 3, step)

            @block.tensor
            def _(pe):
                t = nc.tensor

                def step(j, i, present):
                    o = 1 - i
                    if present(3):
                        after(pe, h_ready, j, 3)
                        for m, k in enumerate("qk"):
                            after(pe, diff[k], j, 5)
                            t.matmul(psX[k][o], s["w_qkv"][:, m * P:(m + 1) * P], hT[o][:],
                                     start=True, stop=True).then_inc(made[k], 1)
                        after(pe, v_kept, j, 5)
                        for q in range(ST):
                            last = t.matmul(psV[o][:, q * P:(q + 1) * P], hT[o][:, q * P:(q + 1) * P],
                                            s["w_qkv"][:, 2 * P:], start=True, stop=True)
                        last.then_inc(made["v"], 1)
                    if present(2):
                        lnb.wait_done(pe, j - 2)
                        for q in range(ST):
                            last = t.transpose(psT[i][:, q * P:(q + 1) * P], zn[i][:, q, :], s["ident"][:])
                        last.then_inc(turned, 1)

                pipeline(pe, SL, 3, step)


def attention_phase(nc, ps, s, v_all, y_all, qd, kd):
    with Phase(nc) as ctx:
        def sb(name, shape, dt=F32):
            return ctx.enter_context(nc.sbuf_tensor(own(nc, name), shape, dt))

        def sem(name):
            return ctx.semaphore(name)

        qs = [sb(f"q_stack{i}", [P, GROUP, T], BF16) for i in range(NG)]
        ks = [sb(f"k_stack{i}", [P, GROUP, T], BF16) for i in range(NG)]
        vs = [sb(f"v_stack{i}", [P, TPB, GROUP, VW]) for i in range(NG)]
        probs = [sb(f"probs{i}", [P, GROUP, T]) for i in range(2)]
        maxima = [sb(f"maxima{i}", [P, GROUP, TPB]) for i in range(2)]
        neg_rest = sb("neg_rest", [P, GROUP * TPB])
        neg_parts = sb("neg_parts", [P, SPLITS, GROUP * TPB], BF16)
        max_rows = [sb(f"max_rows{i}", [SPLITS * GROUP * TPB, P], BF16) for i in range(2)]
        oT = sb("oT", [P, T])
        inv = sb("inv", [P, TPB, GROUP])

        stacks_set = sem("stacks_set")
        loaded = [sem(f"stack_loaded{i}") for i in range(NG)]
        pool_passed, pe_passed = sem("pool_passed"), sem("pe_passed")
        v_staged = sem("v_staged")
        s_ready, s_read = sem("s_ready"), sem("s_read")
        e_ready, e_read = sem("e_ready"), sem("e_read")
        pv_unit = sem("pv_unit")
        split_step, split_done, rows_turned, rows_kept, rows_placed = (
            sem("split_step"), sem("split_done"), sem("rows_turned"), sem("rows_kept"), sem("rows_placed"))
        o_kept, o_turned, inv_ready, o_done = sem("o_kept"), sem("o_turned"), sem("inv_ready"), sem("o_done")

        psS = ps[:, 0:4, :]
        psE = ps[:, 4:6, :]
        psO = [ps[:, 6, :], ps[:, 7, :]]
        NMAX = GROUP * TPB
        PER_LOAD = 16 * (2 * SPLITS + SPLITS - 1)
        PLACED = 16

        def bodies(eng, step):
            for g in range(NG):
                step(0, g, True, False)
            with eng.Fori(1, B - 1) as b:
                for g in range(NG):
                    step(b, g, False, False)
            for g in range(NG):
                step(B - 1, g, False, True)

        with nc.Block() as block:
            @block.sync
            def _(sp):
                def load_group(b, g):
                    heads = slice(g * GROUP, (g + 1) * GROUP)
                    for a in range(SPLITS):
                        row = a * SPLITS * DK
                        for st, dram, turn in ((qs, qd, 0), (ks, kd, a)):
                            first = (SPLITS - turn) * DK
                            sp.dma_start(st[g][row:row + first, :, :],
                                         dram[turn * DK:, heads, ds(b * T, T)]).then_inc(loaded[g], 16)
                            if turn:
                                sp.dma_start(st[g][row + first:row + SPLITS * DK, :, :],
                                             dram[0:turn * DK, heads, ds(b * T, T)]).then_inc(loaded[g], 16)

                sp.wait_ge(stacks_set, 3)
                for g in range(NG):
                    load_group(0, g)
                with sp.Fori(1, B) as b:
                    for g in range(NG):
                        sp.wait_ge(e_ready, GROUP * TPB * (NG * b + g - NG + 1))
                        load_group(b, g)

            @block.gpsimd
            def _(pool):
                g_ = nc.gpsimd
                for i in range(NG):
                    last = g_.memset(qs[i][:], 0.0)
                last.then_inc(stacks_set, 1)

                def stage(b, g):
                    g_.tensor_copy(vs[g][:, :, :, 0:DK + 1],
                                   v_all[:, ds(b * TPB, TPB), g * GROUP:(g + 1) * GROUP, :]).then_inc(v_staged, 1)

                def place(g, i, count):
                    wait_apart(pool, pool_passed, (rows_kept, count))
                    pool.dma_start(qs[g][MAXROW:STACK, :, :],
                                   max_rows[i][:]).then_inc(rows_placed, 16)

                def split_max(i, group):
                    m = maxima[i][:].rearrange("p h q -> p (h q)")
                    turned = [] if isinstance(group, int) and group == 0 else [(rows_turned, group)]
                    wait_apart(pool, pool_passed, (s_read, 8 * group + 8), *turned)
                    g_.tensor_scalar(neg_rest[:], m, -1.0, None, ALU.mult).then_inc(split_step, 1)
                    wait_apart(pool, pool_passed, (split_step, 4 * group + 1))
                    g_.tensor_copy(neg_parts[:, 0, :], neg_rest[:]).then_inc(split_step, 1)
                    wait_apart(pool, pool_passed, (split_step, 4 * group + 2))
                    g_.tensor_tensor(neg_rest[:], neg_rest[:], neg_parts[:, 0, :], ALU.subtract).then_inc(split_step, 1)
                    wait_apart(pool, pool_passed, (split_step, 4 * group + 3))
                    g_.tensor_copy(neg_parts[:, 1, :], neg_rest[:]).then_inc(split_step, 1)
                    wait_apart(pool, pool_passed, (split_step, 4 * group + 4))
                    g_.tensor_tensor(neg_parts[:, 2, :], neg_rest[:], neg_parts[:, 1, :],
                                     ALU.subtract).then_inc(split_done, 1)

                pool.wait_ge(stacks_set, 3)
                for g in range(NG):
                    stage(0, g)
                split_max(0, 0)
                place(0, 0, 1)
                split_max(1, 1)

                def step(b, g, first, last):
                    if not (last and g == NG - 1):
                        place((g + 1) % NG, (g + 1) % 2, NG * b + g + 2)
                    if not first or g > 0:
                        bb, gg = (b, g - 1) if g else (b - 1, NG - 1)
                        if not last or g == 0:
                            pool.wait_ge(pv_unit, TPB * (NG * b + g))
                            stage(bb + 1, gg)
                    if not (last and g >= NG - 2):
                        split_max(g % 2, NG * b + g + 2)

                bodies(pool, step)

            @block.tensor
            def _(pe):
                t = nc.tensor

                def s_pair(g, u, pair, count):
                    if not (isinstance(count, int) and count < 2):
                        pe.wait_ge(s_read, count - 1)
                    for h in (2 * pair, 2 * pair + 1):
                        last = t.matmul(psS[:, h, :], qs[g][0:MAXROW, h, u * P:(u + 1) * P], ks[g][0:MAXROW, h, :],
                                        start=True, stop=True)
                    last.then_inc(s_ready, 1)

                def e_head(g, u, h, count):
                    if not (isinstance(count, int) and count < 2):
                        pe.wait_ge(e_read, count - 1)
                    t.matmul(psE[:, h % 2, :], ks[g][0:STACK, h, u * P:(u + 1) * P], qs[g][0:STACK, h, :],
                             start=True, stop=True).then_inc(e_ready, 1)

                def pv(g, u, unit):
                    pe.wait_ge(e_read, 4 * unit + 4)
                    for h in range(GROUP):
                        last = t.matmul(psO[g % 2][VW * h:VW * (h + 1), :], vs[g][:, u, h, :], probs[u % 2][:, h, :],
                                        start=(u == 0), stop=(u == TPB - 1))
                    last.then_inc(pv_unit, 1)

                def turn_max(g, count, *bank_free):
                    wait_apart(pe, pe_passed, (split_done, count), *bank_free)
                    t.transpose(psO[g % 2][0:SPLITS * NMAX, 0:P // 2].bitcast(BF16),
                                neg_parts[:].rearrange("p c m -> p (c m)"), s["ident16"][:]).then_inc(rows_turned, 1)

                pe.wait_ge(stacks_set, 3)
                for i in range(2):
                    pe.wait_ge(loaded[i], PER_LOAD)
                    for u in range(TPB):
                        for pair in range(2):
                            s_pair(i, u, pair, 8 * i + 2 * u + pair)
                    if i == 0:
                        turn_max(0, 1)

                def step(b, g, first, last):
                    G = NG * b + g
                    ahead = not (last and g >= NG - 2)
                    g2, b2 = (g + 2) % NG, (b if g < 2 else b + 1)
                    for u in range(TPB):
                        if u == 0:
                            pe.wait_ge(rows_placed, PLACED * (G + 1))
                            if ahead:
                                pe.wait_ge(loaded[g2], PER_LOAD * (b2 + 1))
                        unit = TPB * G + u
                        e_head(g, u, 0, 4 * unit)
                        e_head(g, u, 1, 4 * unit + 1)
                        if u > 0:
                            if u == 1:
                                pe.wait_ge(v_staged, G + 1)
                                if not (first and g < 2):
                                    pe.wait_ge(rows_kept, G + 1)
                                    pe.wait_ge(o_done, G - 1)
                                else:
                                    pe.wait_ge(rows_kept, G + 1)
                            pv(g, u - 1, unit - 1)
                            if u == 2 and not (last and g == NG - 1):
                                turn_max((g + 1) % NG, G + 2, *([] if first and g == 0 else [(o_done, G)]))
                        elif not (first and g == 0):
                            pv((g - 1) % NG, TPB - 1, unit - 1)
                        e_head(g, u, 2, 4 * unit + 2)
                        e_head(g, u, 3, 4 * unit + 3)
                        if u == 1 and not (first and g == 0):
                            turn_o((g - 1) % NG, G)
                        if ahead:
                            for pair in range(2):
                                s_pair(g2, u, pair, 8 * (G + 2) + 2 * u + pair)

                def turn_o(g, count):
                    pe.wait_ge(o_kept, count)
                    for q in range(TPB):
                        last = t.transpose(psO[g % 2][:, q * P:(q + 1) * P], oT[:, q * P:(q + 1) * P], s["ident"][:])
                    last.then_inc(o_turned, 1)

                bodies(pe, step)
                pv(NG - 1, TPB - 1, TPB * NG * B - 1)
                turn_o(NG - 1, NG * B)

            @block.scalar
            def _(act):
                a = nc.scalar

                def keep_rows(g, i, count):
                    act.wait_ge(rows_turned, count)
                    if not (isinstance(count, int) and count < 3):
                        act.wait_ge(rows_placed, PLACED * (count - 2))
                    a.activation(max_rows[i][:], psO[g % 2][0:SPLITS * NMAX, 0:P // 2].bitcast(BF16),
                                 ACT.Copy).then_inc(rows_kept, 1)

                def keep_o(g, count):
                    act.wait_ge(pv_unit, TPB * count)
                    if not (isinstance(count, int) and count < 2):
                        act.wait_ge(o_turned, count - 1)
                    a.activation(oT[:], psO[g % 2], ACT.Copy).then_inc(o_kept, 1)

                keep_rows(0, 0, 1)

                def step(b, g, first, last):
                    G = NG * b + g
                    for u in range(TPB):
                        unit = TPB * G + u
                        for h in range(GROUP):
                            act.wait_ge(e_ready, 4 * unit + h + 1)
                            if h == 0 and not (first and g == 0 and u < 2):
                                act.wait_ge(pv_unit, unit - 1)
                            a.activation(probs[u % 2][:, h, :], psE[:, h % 2, :], ACT.Exp,
                                         scale=float(DK) ** -0.5).then_inc(e_read, 1)
                            if u == 2 and h == 1 and not (last and g == NG - 1):
                                keep_rows((g + 1) % NG, (g + 1) % 2, G + 2)
                            if u == 0 and h == 3 and not (first and g == 0):
                                keep_o((g - 1) % NG, G)

                bodies(act, step)
                keep_o(NG - 1, NG * B)

            @block.vector
            def _(vec):
                v = nc.vector
                for i in range(NG):
                    v.memset(ks[i][:], 0.0).then_inc(inv_ready, 1)
                vec.wait_ge(inv_ready, NG)
                for i in range(NG):
                    last = v.memset(ks[i][MAXROW:STACK, :, :], 1.0)
                last.then_inc(stacks_set, 1)
                for i in range(NG):
                    last = v.memset(vs[i][:], 0.0)
                last.then_inc(stacks_set, 1)
                def reduce_pair(i, u, pair, group):
                    vec.wait_ge(s_ready, 8 * group + 2 * u + pair + 1)
                    if u == 0 and pair == 0 and not (isinstance(group, int) and group < 2):
                        vec.wait_ge(split_done, group - 1)
                    v.tensor_reduce(maxima[i][:, 2 * pair:2 * pair + 2, u:u + 1], psS[:, 2 * pair:2 * pair + 2, :], AX_X,
                                    ALU.max).then_inc(s_read, 1)

                def normalize(b, g, count):
                    vec.wait_ge(o_turned, count)
                    if not (isinstance(count, int) and count == 1):
                        vec.wait_ge(o_done, count - 1)
                    o = psO[g % 2].rearrange("p (q h w) -> p q h w", q=TPB, h=GROUP)
                    v.reciprocal(inv[:], o[:, :, :, DK]).then_inc(inv_ready, 1)
                    vec.wait_ge(inv_ready, NG + count)
                    v.tensor_tensor(y_all[:, ds(b * TPB, TPB), g * GROUP * DK:(g + 1) * GROUP * DK].rearrange(
                        "p q (h d) -> p q h d", h=GROUP), o[:, :, :, 0:DK],
                        inv[:].unsqueeze(3).broadcast_to([P, TPB, GROUP, DK]), ALU.mult).then_inc(o_done, 1)

                for i in range(2):
                    for u in range(TPB):
                        for pair in range(2):
                            reduce_pair(i, u, pair, i)

                def step(b, g, first, last):
                    G = NG * b + g
                    for u in range(TPB):
                        if u == 1 and not (first and g == 0):
                            bb, gg = (b, g - 1) if g else (b - 1, NG - 1)
                            normalize(bb, gg, G)
                        if not (last and g >= NG - 2):
                            for pair in range(2):
                                reduce_pair(g % 2, u, pair, G + 2)
                bodies(vec, step)
                normalize(B - 1, NG - 1, NG * B)


def project_phase(nc, ps, s, x_all, z_all, y_all, logits):
    with Phase(nc) as ctx:
        def sb(name, shape, dt=F32):
            return ctx.enter_context(nc.sbuf_tensor(own(nc, name), shape, dt))

        def sem(name):
            return ctx.semaphore(name)

        def sbs(name, shape, dt=F32):
            return [sb(f"{name}{i}", shape, dt) for i in range(2)]

        ln = LayerNorm(nc, ctx, "ln2", ST, EPS, bufs=2)
        y_in, normed = sbs("y_in", [P, ST, P]), sbs("normed", [P, ST, P])
        yT, h2T, x1 = sbs("yT", [P, SW]), sbs("h2T", [P, SW]), sb("x1", [P, ST, P])
        y_loaded, norm_stored = [sem("y_loaded0"), sem("y_loaded1")], [sem("norm_stored0"), sem("norm_stored1")]
        y_turned, y_kept, projected, x1_ready, halved = (
            sem("y_turned"), sem("y_kept"), sem("projected"), sem("x1_ready"), sem("halved"))
        h_turned, h_kept, gated, logits_kept = sem("h_turned"), sem("h_kept"), sem("gated"), sem("logits_kept")
        psY, psP, psH = ([ps[:, 2 * m + i, :] for i in range(2)] for m in range(3))
        psL = [ps[:, 6 + i, 0:ST * E] for i in range(2)]

        with nc.Block() as block:
            @block.sync
            def _(sp):
                def step(j, i, present):
                    o = 1 - i
                    if present(0):
                        after(sp, y_turned, j, 2)
                        sp.dma_start(y_in[i][:], y_all[:, ds(j * ST, ST), :]).then_inc(y_loaded[i], 16)
                    if present(2):
                        ln.wait_done(sp, j - 2)
                        sp.dma_start(y_all[:, ds((j - 2) * ST, ST), :], normed[i][:]).then_inc(norm_stored[i], 16)

                pipeline(sp, SL, 2, step)
                for i in range(2):
                    sp.wait_ge(norm_stored[i], 16 * SL // 2)

            @block.tensor
            def _(pe):
                t = nc.tensor

                def step(j, i, present):
                    o = 1 - i
                    if present(3):
                        after(pe, h_kept, j, 3)
                        after(pe, logits_kept, j, 5)
                        for q in range(ST):
                            last = t.matmul(psL[o][:, q * E:(q + 1) * E], h2T[o][:, q * P:(q + 1) * P], s["gate_w"][:],
                                            start=True, stop=True)
                        last.then_inc(gated, 1)
                    if present(1):
                        after(pe, y_kept, j, 1)
                        after(pe, x1_ready, j, 3)
                        for q in range(ST):
                            last = t.matmul(psP[o][:, q * P:(q + 1) * P], yT[o][:, q * P:(q + 1) * P], s["w_proj"][:],
                                            start=True, stop=True)
                        last.then_inc(projected, 1)
                    if present(0):
                        after_same_parity(pe, y_loaded[i], j, i)
                        after(pe, y_kept, j, 2)
                        for q in range(ST):
                            last = t.transpose(psY[i][:, q * P:(q + 1) * P], y_in[i][:, q, :], s["ident"][:])
                        last.then_inc(y_turned, 1)
                    if present(2):
                        ln.wait_done(pe, j - 2)
                        after(pe, h_kept, j, 4)
                        for q in range(ST):
                            last = t.transpose(psH[i][:, q * P:(q + 1) * P], normed[i][:, q, :], s["ident"][:])
                        last.then_inc(h_turned, 1)

                pipeline(pe, SL, 3, step)

            @block.scalar
            def _(act):
                a = nc.scalar

                def step(j, i, present):
                    o = 1 - i
                    if present(0):
                        after(act, y_turned, j)
                        after(act, projected, j, 2)
                        a.activation(yT[i][:], psY[i], ACT.Copy).then_inc(y_kept, 1)
                    if present(1):
                        ln.squares(act, j - 1, o)
                    if present(2):
                        after(act, h_turned, j, 2)
                        after(act, gated, j, 4)
                        a.activation(h2T[i][:], psH[i], ACT.Identity, bias=s["ln2_b"][:, 0:1],
                                     scale=s["ln2_w"][:, 0:1]).then_inc(h_kept, 1)

                pipeline(act, SL, 2, step)

            @block.vector
            def _(vec):
                v = nc.vector

                def step(j, i, present):
                    o = 1 - i
                    if present(1):
                        here = ds((j - 1) * ST, ST)
                        after(vec, projected, j, 1)
                        after(vec, halved, j, 2)
                        v.tensor_tensor(x1[:], z_all[:, here, :], psP[o].rearrange("p (t c) -> p t c", c=P),
                                        ALU.add).then_inc(x1_ready, 1)
                        after(vec, x1_ready, j, 1)
                        ln.center(vec, j - 1, x1[:], o)
                        v.scalar_tensor_tensor(x_all[:, here, :], x1[:], 0.5, x_all[:, here, :], ALU.mult,
                                               ALU.add).then_inc(halved, 1)
                    if present(3):
                        after(vec, gated, j, 3)
                        v.tensor_tensor(logits[:, ds((j - 3) * ST, ST), :], psL[o].rearrange("p (t e) -> p t e", e=E),
                                        s["gate_b"][:].unsqueeze(1).broadcast_to([P, ST, E]),
                                        ALU.add).then_inc(logits_kept, 1)
                    if present(1):
                        ln.variance(vec, j - 1, o)

                pipeline(vec, SL, 3, step)
                vec.wait_ge(logits_kept, SL)
                vec.wait_ge(halved, SL)

            @block.gpsimd
            def _(pool):
                def step(j, i, present):
                    o = 1 - i
                    if present(1):
                        free = [] if isinstance(j, int) and j < 3 else [(norm_stored[o], 8 * (j - 1 - o)), (h_turned, j - 2)]
                        ln.scale(pool, j - 1, normed[o][:], o, *free)

                ln.start(pool)
                pipeline(pool, SL, 1, step)


def route_phase(nc, ps, s, y_all, logits, slot, expert, xs):
    with Phase(nc) as ctx:
        def sb(name, shape, dt=F32):
            return ctx.enter_context(nc.sbuf_tensor(own(nc, name), shape, dt))

        def sem(name):
            return ctx.semaphore(name)

        best, first = sb("best", [P, NT]), sb("first", [P, NT])
        equal, one_hot = sb("equal", [P, NT, E]), sb("one_hot", [P, NT, E])
        tile_count, running = sb("tile_count", [P, E, NT]), sb("running", [P, E, NT])
        tiles, tiles_end, base = sb("tiles", [P, E]), sb("tiles_end", [P, E]), sb("base", [P, E])
        place, slot_f, over = sb("place", [P, NT, E]), sb("slot_f", [P, NT]), sb("over", [P, SLOTS, E])
        expert_f = sb("expert_f", [P, SLOTS])
        step, one_hot_ready, ranked, slots_ready, scattered = (
            sem("step"), sem("one_hot_ready"), sem("ranked"), sem("slots_ready"), sem("scattered"))
        rank = ps[:, 0, 0:NT * E]
        count = ps[:, 0, NT * E:2 * NT * E]
        c = s["counts"]

        with nc.Block() as block:
            @block.vector
            def _(vec):
                v = nc.vector
                done = [0]

                def link(ins):
                    done[0] += 1
                    ins.then_inc(step, 1)
                    vec.wait_ge(step, done[0])

                experts = c[:, 0:E].unsqueeze(1)
                link(v.tensor_reduce(best[:], logits[:], AX_X, ALU.max))
                link(v.tensor_tensor(equal[:], logits[:], best[:].unsqueeze(2).broadcast_to([P, NT, E]), ALU.is_equal))
                link(v.tensor_scalar(over[:, 0, :], c[:, 0:E], float(E), None, ALU.subtract))
                link(v.tensor_tensor(equal[:], equal[:], over[:, 0:1, :].broadcast_to([P, NT, E]), ALU.mult))
                link(v.tensor_reduce(first[:], equal[:], AX_X, ALU.min))
                link(v.tensor_tensor(one_hot[:], over[:, 0:1, :].broadcast_to([P, NT, E]),
                                     first[:].unsqueeze(2).broadcast_to([P, NT, E]), ALU.is_equal))
                link(v.tensor_copy(base[:], c[:, 0:E]))
                v.tensor_copy(slot_f[:], first[:]).then_inc(one_hot_ready, 1)
                vec.wait_ge(ranked, 1)
                link(v.tensor_copy(tile_count[:], count.rearrange("p (t e) -> p e t", e=E)))
                link(v.tensor_tensor_scan(running[:].rearrange("p e t -> p (e t)"), s["restart"][:],
                                          tile_count[:].rearrange("p e t -> p (e t)"), 0.0, ALU.mult, ALU.add))
                link(v.tensor_scalar(place[:, :, 0], c[:, 0:NT], float(P), None, ALU.mult))
                total = running[:, :, NT - 1]
                above = equal[:].rearrange("p t e -> p (t e)").rearrange("p (e t) -> p e t", e=E)
                link(v.tensor_tensor(above, total.unsqueeze(2).broadcast_to([P, E, NT]),
                                     place[:, :, 0].unsqueeze(1).broadcast_to([P, E, NT]), ALU.is_gt))
                link(v.tensor_reduce(tiles[:], above, AX_X, ALU.add))
                link(v.tensor_tensor_scan(tiles_end[:], s["ones"][:, 0:E], tiles[:], 0.0, ALU.mult, ALU.add))
                link(v.tensor_tensor(base[:], tiles_end[:], tiles[:], ALU.subtract))
                link(v.tensor_tensor(running[:], running[:], tile_count[:], ALU.subtract))
                link(v.tensor_tensor(place[:], running[:].rearrange("p e t -> p t e"),
                                     rank.rearrange("p (t e) -> p t e", e=E), ALU.add))
                link(v.tensor_scalar(base[:], base[:], float(P), None, ALU.mult))
                link(v.tensor_tensor(place[:], place[:], base[:].unsqueeze(1).broadcast_to([P, NT, E]), ALU.add))
                link(v.tensor_tensor(place[:], place[:], one_hot[:], ALU.mult))
                link(v.tensor_reduce(slot_f[:], place[:], AX_X, ALU.add))
                link(v.tensor_copy(slot[:], slot_f[:]))
                link(v.tensor_tensor(over[:], c[:, 0:SLOTS].unsqueeze(2).broadcast_to([P, SLOTS, E]),
                                     tiles_end[:].unsqueeze(1).broadcast_to([P, SLOTS, E]), ALU.is_ge))
                link(v.tensor_reduce(expert_f[:], over[:], AX_X, ALU.add))
                link(v.tensor_scalar(expert_f[:], expert_f[:], float(E - 1), None, ALU.min))
                v.tensor_copy(expert[:], expert_f[:]).then_inc(slots_ready, 1)

            @block.tensor
            def _(pe):
                t = nc.tensor
                hot = one_hot[:].rearrange("p t e -> p (t e)")
                pe.wait_ge(one_hot_ready, 1)
                t.matmul(rank, s["below"][:], hot, start=True, stop=True)
                t.matmul(count, s["ones"][:], hot, start=True, stop=True).then_inc(ranked, 1)

            @block.gpsimd
            def _(pool):
                pool.wait_ge(slots_ready, 1)
                for i in range(NT):
                    pool.indirect_dma_start(xs, bass.IndirectOffsetOnAxis(ap=slot[:, i:i + 1], axis=0),
                                            y_all[:, i, :], None).then_inc(scattered, 16)
                pool.wait_ge(scattered, 16 * NT)


def expert_phase(nc, ps, s, expert, xs, ys):
    with Phase(nc) as ctx:
        def sb(name, shape, dt=F32):
            return [ctx.enter_context(nc.sbuf_tensor(own(nc, f"{name}{i}"), shape, dt)) for i in range(2)]

        def sem(name):
            return ctx.semaphore(name)

        xt, xT, hid, hidT, yt = sb("xt", [P, P]), sb("xT", [P, P]), sb("hid", [P, HID]), sb("hidT", [P, HID]), sb("yt", [P, P])
        x_loaded, x_turned, xT_kept = [sem("x_loaded0"), sem("x_loaded1")], sem("x_turned"), sem("xT_kept")
        first_done, hid_kept, hid_turned, hidT_kept = (
            sem("first_done"), sem("hid_kept"), sem("hid_turned"), sem("hidT_kept"))
        passed = sem("passed")
        second_done, y_kept, y_stored = sem("second_done"), sem("y_kept"), [sem("y_stored0"), sem("y_stored1")]
        psX, psH, psT, psY = ([ps[:, 2 * k + i, :] for i in range(2)] for k in range(4))

        with nc.Block() as block:
            @block.sync
            def _(sp):
                def load(j, i):
                    sp.dma_start(xt[i][:], xs[ds(j * P, P), :]).then_inc(x_loaded[i], 16)

                load(0, 0)
                load(1, 1)
                with sp.Fori(1, SLOTS // 2) as pair:
                    for i in range(2):
                        sp.wait_ge(x_turned, 2 * pair + i - 1)
                        load(2 * pair + i, i)

            @block.tensor
            def _(pe):
                t = nc.tensor

                def weights_of(j):
                    return pe.value_load(expert[0:1, ds(j, 1)], min_val=0, max_val=E - 1)

                def step(j, i, present):
                    o = 1 - i
                    if present(0):
                        after_same_parity(pe, x_loaded[i], j, i)
                        after(pe, xT_kept, j, 2)
                        t.transpose(psX[i][:, 0:P], xt[i][:], s["ident"][:]).then_inc(x_turned, 1)
                    if present(1):
                        after(pe, xT_kept, j, 1)
                        after(pe, hid_kept, j, 3)
                        e = weights_of(j - 1)
                        t.matmul(psH[o], xT[o][:], s["w1"][:, ds(e, 1), :], start=True, stop=True).then_inc(first_done, 1)
                    if present(2):
                        after(pe, hid_kept, j, 2)
                        after(pe, hidT_kept, j, 4)
                        for c in range(HC):
                            last = t.transpose(psT[i][:, c * P:(c + 1) * P], hid[i][:, c * P:(c + 1) * P], s["ident"][:])
                        last.then_inc(hid_turned, 1)
                    if present(3):
                        after(pe, hidT_kept, j, 3)
                        after(pe, y_kept, j, 5)
                        e = weights_of(j - 3)
                        for c in range(HC):
                            last = t.matmul(psY[o][:, 0:P], hidT[o][:, c * P:(c + 1) * P], s["w2"][:, ds(e, 1), c, :],
                                            start=(c == 0), stop=(c == HC - 1))
                        last.then_inc(second_done, 1)

                pipeline(pe, SLOTS, 3, step)

            @block.scalar
            def _(act):
                a = nc.scalar

                def step(j, i, present):
                    o = 1 - i
                    if present(0):
                        after(act, x_turned, j, 0)
                        after(act, first_done, j, 2)
                        a.activation(xT[i][:], psX[i][:, 0:P], ACT.Identity, bias=s["ln2_b"][:, 0:1],
                                     scale=s["ln2_w"][:, 0:1]).then_inc(xT_kept, 1)
                    if present(1):
                        after(act, first_done, j, 1)
                        after(act, hid_turned, j, 3)
                        a.activation(hid[o][:], psH[o], ACT.Gelu_apprx_tanh).then_inc(hid_kept, 1)

                pipeline(act, SLOTS, 3, step)

            @block.vector
            def _(vec):
                v = nc.vector

                def step(j, i, present):
                    o = 1 - i
                    if present(2):
                        after(vec, hid_turned, j, 2)
                        after(vec, second_done, j, 4)
                        v.tensor_copy(hidT[i][:], psT[i]).then_inc(hidT_kept, 1)
                    if present(3):
                        after(vec, second_done, j, 3)
                        if not isinstance(j, int) or j >= 5:
                            vec.wait_ge(y_stored[o], 8 * (j - 3 - o))
                        v.tensor_copy(yt[o][:], psY[o][:, 0:P]).then_inc(y_kept, 1)

                pipeline(vec, SLOTS, 3, step)

            @block.gpsimd
            def _(pool):
                with pool.Fori(0, SLOTS // 2) as pair:
                    for i in range(2):
                        wait_apart(pool, passed, (y_kept, 2 * pair + i + 1))
                        pool.dma_start(ys[ds((2 * pair + i) * P, P), :], yt[i][:]).then_inc(y_stored[i], 16)
                for i in range(2):
                    pool.wait_ge(y_stored[i], 16 * (SLOTS // 2))


def combine_phase(nc, x_all, y_all, slot, ys):
    with Phase(nc) as ctx:
        gathered = [ctx.semaphore(f"gathered{i}") for i in range(SL)]
        added = ctx.semaphore("added")
        with nc.Block() as block:
            @block.gpsimd
            def _(pool):
                for i in range(NT):
                    pool.indirect_dma_start(y_all[:, i, :], None, ys,
                                            bass.IndirectOffsetOnAxis(ap=slot[:, i:i + 1], axis=0)
                                            ).then_inc(gathered[i // ST], 16)

            @block.vector
            def _(vec):
                for n in range(SL):
                    vec.wait_ge(gathered[n], 16 * ST)
                    here = slice(n * ST, (n + 1) * ST)
                    nc.vector.scalar_tensor_tensor(x_all[:, here, :], y_all[:, here, :], 0.5, x_all[:, here, :],
                                                   ALU.mult, ALU.add).then_inc(added, 1)
                vec.wait_ge(added, SL)


class Signal:

    def __init__(self, nc, ctx, name, per=1):
        self.sem, self.per = ctx.semaphore(name), per

    def wait(self, eng, b, k=None):
        eng.wait_ge(self.sem, self.per * b + (self.per if k is None else k) + 1)

    def at(self, b, k=None):
        return self.sem, self.per * b + (self.per if k is None else k) + 1

    def free(self, eng, b):
        if not isinstance(b, int) or b > 0:
            self.wait(eng, b, 0)


F_W, F_K, F_V, F_R, F_G = range(5)
LORA = 32
NH, HS = 2, 64
BLOCK = 32
DIAG_LEVELS = 5
LEVELS = 7
GN_EPS = 1e-5 * NH


def turn_phase(nc, ps, s, x_all, zT):
    with Phase(nc) as ctx:
        ln = LayerNorm(nc, ctx, "lnr", ST, EPS, bufs=2)
        normed = [ctx.enter_context(nc.sbuf_tensor(own(nc, f"r_normed{i}"), [P, ST, P], F32)) for i in range(2)]
        turned, kept, zero = (ctx.semaphore(n) for n in ("r_turned", "r_kept", "r_zero"))
        with nc.Block() as block:
            @block.vector
            def _(vec):
                def step(j, i, present):
                    o = 1 - i
                    if present(0):
                        ln.center(vec, j, x_all[:, ds(j * ST, ST), :], i)
                    if present(1):
                        ln.variance(vec, j - 1, o)

                pipeline(vec, SL, 1, step)

            @block.scalar
            def _(act):
                def step(j, i, present):
                    o = 1 - i
                    if present(0):
                        after(act, ln.var_ready, j, 1)
                        ln.squares(act, j, i)
                    if present(1):
                        after(act, turned, j, 1)
                        nc.scalar.activation(zT[:, ds(j - 1, 1), 1:], ps[:, o:o + 1, :], ACT.Copy).then_inc(kept, 1)

                pipeline(act, SL, 1, step)

            @block.gpsimd
            def _(pool):
                def step(j, i, present):
                    if present(0):
                        ln.scale(pool, j, normed[i][:], i, *([] if isinstance(j, int) and j < 2 else [(turned, j - 1)]))

                ln.start(pool)
                nc.gpsimd.memset(zT[:, :, 0:1], 0.0).then_inc(zero, 1)
                pipeline(pool, SL, 0, step)

            @block.tensor
            def _(pe):
                def step(j, i, present):
                    if present(0):
                        ln.wait_done(pe, j)
                        after(pe, kept, j, 2)
                        for q in range(ST):
                            last = nc.tensor.transpose(ps[:, i, q * P:(q + 1) * P], normed[i][:, q, :], s["ident"][:])
                        last.then_inc(turned, 1)

                pipeline(pe, SL, 0, step)


def recurrence_phase(nc, ps, s, x_all, zT):
    with Phase(nc) as ctx:
        def sb(name, shape, dt=F32):
            return ctx.enter_context(nc.sbuf_tensor(own(nc, "r_" + name), shape, dt))

        def two(name, shape, dt=F32):
            return [sb(f"{name}{i}", shape, dt) for i in range(2)]

        def signal(name, per=1):
            x = Signal(nc, ctx, "r_" + name, per)
            signals.append(x)
            return x

        signals = []
        passed = {e: ctx.semaphore("r_passed_" + e) for e in ("vec", "pool", "pe")}
        dxa, xm, lora, lora4 = sb("dxa", [P, T]), sb("xm", [P, T]), sb("lora", [P, T]), sb("lora4", [LORA, T])
        shift, mixed = two("shift", [P, T]), [sb(f"mixed{f}", [P, T]) for f in range(5)]
        td_hidden, rate, gate_tanh = sb("td_hidden", [HS, T]), sb("rate", [P, T]), sb("gate_tanh", [P, T])
        q0, k0, ru, v_rows, decay, gate = (two("q0", [P, T]), two("k0", [P, T]), two("ru", [P, T]),
                                           two("v_rows", [P, TPB, P]), two("decay", [P, T]), two("gate", [P, T]))
        qx, kx = two("qx", [P, T]), two("kx", [P, T])
        block_decay = [sb(f"block_decay{l}", [P, T >> l]) for l in range(1, LEVELS + 1)]
        q_factor = [sb(f"q_factor{l}", [P, T >> (l + 1), 2]) for l in range(LEVELS)]
        k_factor = [sb(f"k_factor{l}", [P, T >> (l + 1), 2]) for l in range(LEVELS)]
        diag = sb("diag", [P, NH, TPB, BLOCK])
        aT = sb("aT", [P, NH, TPB, P])
        kT = sb("kT", [P, TPB, P])
        state = [sb(f"state{c}", [P, P]) for c in range(1, TPB)]
        gn = LayerNorm(nc, ctx, "gn", TPB * NH, GN_EPS, HS)
        yn, yg, ygT = sb("yn", [P, TPB, P]), sb("yg", [P, T]), sb("ygT", [P, T])

        dxa_ready, xm_ready, shift_ready = signal("dxa_ready"), signal("xm_ready"), signal("shift_ready", 5)
        lora_made, lora_kept, miu_made, mixed_ready = (
            signal("lora_made"), signal("lora_kept", 2), signal("miu_made", 5), signal("mixed_ready", 5))
        td_made, td_kept, w_made, rate_ready, decay_ready = (
            signal("td_made"), signal("td_kept"), signal("w_made"), signal("rate_ready"), signal("decay_ready"))
        k_made, r_made, v_made, g_made = signal("k_made"), signal("r_made"), signal("v_made"), signal("g_made")
        k_kept, r_kept, ru_kept, v_kept, gt_kept, g_kept = (
            signal("k_kept"), signal("r_kept"), signal("ru_kept"), signal("v_kept"), signal("gt_kept"), signal("g_kept"))
        factors, chain = signal("factors", LEVELS), signal("chain", LEVELS)
        q_next, k_next = signal("q_next", LEVELS), signal("k_next", LEVELS)
        level_made, level_kept = signal("level_made", DIAG_LEVELS + 1), signal("level_kept", DIAG_LEVELS + 1)
        far_made, far_kept, near_kept = signal("far_made", 2), signal("far_kept", 3), signal("near_kept", BLOCK // 8)
        kT_made, kT_kept, kv_made, state_step = (
            signal("kT_made"), signal("kT_kept"), signal("kv_made"), signal("state_step", 2 * (TPB - 1)))
        y_made, yn_turned, yg_ready, ygT_ready, out_made, x_added = (
            signal("y_made"), signal("yn_turned"), signal("yg_ready"), signal("ygT_ready"), signal("out_made"),
            signal("x_added"))

        def batches(eng, **parts):
            def run(b, i, *wanted):
                for kind, part in ORDER:
                    here = parts.get(f"{kind}_{part}")
                    if here is not None and kind in wanted:
                        here(*{"scan": (b, i), "mix": (b + 1, 1 - i), "tail": (b - 1, 1 - i), "next": (b + 2, i)}[kind])

            run(-2, 0, "next")
            run(-1, 1, "mix", "next")
            run(0, 0, "scan", "mix", "next")
            with eng.Fori(0, B // 2 - 2) as pair:
                run(2 * pair + 1, 1, "scan", "mix", "tail", "next")
                run(2 * pair + 2, 0, "scan", "mix", "tail", "next")
            run(B - 3, 1, "scan", "mix", "tail", "next")
            run(B - 2, 0, "scan", "mix", "tail")
            run(B - 1, 1, "scan", "tail")
            run(B, 0, "tail")

        started, halved = ctx.semaphore("r_started"), ctx.semaphore("r_halved")
        with nc.Block() as block:
            @block.gpsimd
            def _(pool):
                g = nc.gpsimd
                gn.start(pool)
                for x in signals:
                    pool.sem_inc(x.sem, 1)
                n = 0
                for x, value in ([(diag, 0.0), (aT, 0.0)] + [(x, 0.0) for x in state]
                                 + [(x, 1.0) for x in q_factor + k_factor]):
                    g.memset(x[:], value).then_inc(started, 1)
                    n += 1
                pool.wait_ge(started, n)

            @block.vector
            def _(vec):
                nc.vector.tensor_scalar(s["gn_w_half"][:], s["gn_w"][:], 0.5, None, ALU.mult).then_inc(halved, 1)
                nc.vector.tensor_scalar(s["gn_b_half"][:], s["gn_b"][:], 0.5, None, ALU.mult).then_inc(halved, 1)
                vec.wait_ge(halved, 2)

        with nc.Block() as block:
            @block.vector
            def _(vec):
                v = nc.vector

                def next_xm(b, i):
                    x = zT[:, ds(b, 1), 1:].rearrange("p a t -> p (a t)")
                    before = zT[:, ds(b, 1), 0:T].rearrange("p a t -> p (a t)")
                    shift_ready.free(vec, b)
                    v.tensor_tensor(dxa[:], before, x, ALU.subtract).then_inc(dxa_ready.sem, 1)
                    dxa_ready.wait(vec, b)
                    lora_made.free(vec, b)
                    v.scalar_tensor_tensor(xm[:], dxa[:], s["miu_x"][:, 0:1], x, ALU.mult, ALU.add).then_inc(xm_ready.sem, 1)

                def mix_shift(f):
                    def part(b, i):
                        miu_made.wait(vec, b, f + 1)
                        if f >= 2:
                            mixed_ready.wait(vec, b, f - 1)
                        else:
                            mixed_ready.free(vec, b)
                        v.scalar_tensor_tensor(shift[f % 2][:], ps[:, MIU_BANK[f], :], s["lambda"][:, f:f + 1], dxa[:],
                                               ALU.add, ALU.mult).then_inc(shift_ready.sem, 1)
                    return part

                def mix_r(b, i):
                    r_kept.wait(vec, b)
                    if not isinstance(b, int) or b >= 2:
                        level_made.free(vec, b - 1)
                    v.tensor_scalar(ru[i][:], q0[i][:], s["u"][:, 0:1], None, ALU.mult).then_inc(ru_kept.sem, 1)

                def mix_g(b, i):
                    gt_kept.wait(vec, b)
                    if not isinstance(b, int) or b >= 2:
                        ygT_ready.free(vec, b - 1)
                    v.scalar_tensor_tensor(gate[i][:], gate_tanh[:], 1.0, ps[:, G_BANK, :], ALU.add,
                                           ALU.mult).then_inc(g_kept.sem, 1)

                def mix_chain(b, i):
                    decay_ready.wait(vec, b)
                    for l in range(LEVELS):
                        src = decay[i] if l == 0 else block_decay[l - 1]
                        pairs = src[:].rearrange("p (n two) -> p n two", two=2)
                        if l:
                            chain.wait(vec, b, l)
                        else:
                            factors.free(vec, b)
                            state_step.free(vec, b)
                        v.tensor_tensor(block_decay[l][:], pairs[:, :, 0], pairs[:, :, 1], ALU.mult).then_inc(chain.sem, 1)

                def scan_start(b, i):
                    keep_level(b, 0)
                    next_q(b, i, 0)

                def next_q(b, i, l):
                    src = q0[i] if l == 0 else qx[l % 2]
                    dst = qx[(l + 1) % 2]
                    factors.wait(vec, b, l + 1)
                    if l == 0:
                        r_kept.wait(vec, b)
                        y_made.free(vec, b)
                        q_next.free(vec, b)
                    else:
                        q_next.wait(vec, b, l)
                        if l <= DIAG_LEVELS:
                            level_made.wait(vec, b, l + 1)
                        else:
                            far_made.wait(vec, b, 1)
                    m = 1 << l
                    v.tensor_tensor(dst[:].rearrange("p (k m) -> p k m", m=m), src[:].rearrange("p (k m) -> p k m", m=m),
                                    q_factor[l][:].rearrange("p n two -> p (n two)").unsqueeze(2).broadcast_to([P, T // m, m]),
                                    ALU.mult).then_inc(q_next.sem, 1)

                def scan_level(l):
                    def part(b, i):
                        keep_level(b, l)
                        next_q(b, i, l)
                    return part

                def scan_far(b, i):
                    next_q(b, i, DIAG_LEVELS + 1)

                def scan_state(b, i):
                    kv_made.wait(vec, b)
                    for c in range(1, TPB):
                        for h in range(NH):
                            at = slice(h * HS, (h + 1) * HS)
                            kv = ps[at, KV_BANK, (c - 1) * P + h * HS:(c - 1) * P + (h + 1) * HS]
                            n = 2 * (c - 1) + h
                            if c == 1:
                                v.tensor_copy(state[0][at, at], kv).then_inc(state_step.sem, 1)
                            else:
                                state_step.wait(vec, b, n - 1)
                                v.scalar_tensor_tensor(state[c - 1][at, at], state[c - 2][at, at],
                                                       block_decay[LEVELS - 1][at, c - 1:c], kv, ALU.mult,
                                                       ALU.add).then_inc(state_step.sem, 1)

                def scan_y(b, i):
                    y_made.wait(vec, b)
                    gn.center(vec, b, ps[:, Y_BANK, :].rearrange("p (n w) -> p n w", w=HS))

                def tail_norm(b, i):
                    gn.variance(vec, b)

                def tail_turn(b, i):
                    yn_turned.wait(vec, b)
                    ygT_ready.free(vec, b)
                    v.tensor_scalar(yg[:], ps[:, YT_BANK, :], s["gn_w_half"][:, 0:1], s["gn_b_half"][:, 0:1], ALU.mult,
                                    ALU.add).then_inc(yg_ready.sem, 1)
                    yg_ready.wait(vec, b)
                    out_made.free(vec, b)
                    v.tensor_tensor(ygT[:], yg[:], gate[i][:], ALU.mult).then_inc(ygT_ready.sem, 1)

                def tail_out(b, i):
                    out_made.wait(vec, b)
                    here = x_all[:, ds(b * TPB, TPB), :]
                    v.tensor_tensor(here, here, ps[:, OUT_BANK, :].rearrange("p (t c) -> p t c", c=P),
                                    ALU.add).then_inc(x_added.sem, 1)

                def keep_level(b, l):
                    wait_apart(vec, passed["vec"], level_made.at(b, l + 1), level_kept.at(b, l), near_kept.at(b, 0))
                    v.copy_predicated(diag[:], s["level_masks"][:, l, :].unsqueeze(1).unsqueeze(1).broadcast_to([P, NH, TPB, BLOCK]),
                                      ps[:, LEVEL_BANK:LEVEL_BANK + NH, 0:TPB * BLOCK].rearrange("p h (c w) -> p h c w", c=TPB)
                                      ).then_inc(level_kept.sem, 1)

                batches(vec, next_xm=next_xm, **{f"mix_shift{f}": mix_shift(f) for f in range(5)}, mix_r=mix_r,
                        mix_g=mix_g, mix_chain=mix_chain, scan_start=scan_start, **{f"scan_level{l}": scan_level(l) for l in range(1, DIAG_LEVELS + 1)},
                        scan_far=scan_far, scan_state=scan_state, scan_y=scan_y,
                        tail_norm=tail_norm, tail_turn=tail_turn, tail_out=tail_out)
                x_added.wait(vec, B - 1)

            @block.gpsimd
            def _(pool):
                g = nc.gpsimd

                users = (td_made, k_made, v_made, r_made, g_made)

                def mix_mixed(f):
                    def part(b, i):
                        x = zT[:, ds(b, 1), 1:].rearrange("p a t -> p (a t)")
                        wait_apart(pool, passed["pool"], shift_ready.at(b, f + 1), users[f].at(b, 0))
                        g.tensor_tensor(mixed[f][:], shift[f % 2][:], x, ALU.add).then_inc(mixed_ready.sem, 1)
                    return part

                def next_k(b, i, l):
                    src = k0[i] if l == 0 else kx[l % 2]
                    dst = kx[(l + 1) % 2]
                    factors.wait(pool, b, l + 1)
                    if l == 0:
                        k_kept.wait(pool, b)
                        kT_made.free(pool, b)
                    else:
                        k_next.wait(pool, b, l)
                        if l <= DIAG_LEVELS:
                            level_made.wait(pool, b, l + 1)
                        else:
                            far_made.wait(pool, b, 1)
                    m = 1 << l
                    g.tensor_tensor(dst[:].rearrange("p (k m) -> p k m", m=m), src[:].rearrange("p (k m) -> p k m", m=m),
                                    k_factor[l][:].rearrange("p n two -> p (n two)").unsqueeze(2).broadcast_to([P, T // m, m]),
                                    ALU.mult).then_inc(k_next.sem, 1)

                def scan_level(l):
                    return lambda b, i: next_k(b, i, l)

                def scan_far(b, i):
                    next_k(b, i, DIAG_LEVELS + 1)

                def tail_norm(b, i):
                    gn.scale(pool, b, yn[:].rearrange("p c (h w) -> p (c h) w", w=HS))

                batches(pool, **{f"mix_mixed{f}": mix_mixed(f) for f in range(5)}, mix_first_k=scan_level(0),
                        **{f"scan_level{l}": scan_level(l) for l in range(1, DIAG_LEVELS + 1)}, scan_far=scan_far,
                        tail_norm=tail_norm)

            @block.scalar
            def _(act):
                a = nc.scalar

                def mix_lora(b, i):
                    lora_made.wait(act, b)
                    miu_made.free(act, b)
                    a.activation(lora[:], ps[:, 0, :], ACT.Tanh).then_inc(lora_kept.sem, 1)
                    a.activation(lora4[:], ps[0:LORA, 1, :], ACT.Tanh).then_inc(lora_kept.sem, 1)

                def mix_td(b, i):
                    td_made.wait(act, b)
                    w_made.free(act, b)
                    a.activation(td_hidden[:], ps[0:HS, TD_BANK, :], ACT.Tanh).then_inc(td_kept.sem, 1)

                def mix_rate(b, i):
                    w_made.wait(act, b)
                    decay_ready.free(act, b)
                    a.activation(rate[:], ps[:, W_BANK, :], ACT.Exp, bias=s["td_miu"][:, 0:1]).then_inc(rate_ready.sem, 1)
                    rate_ready.wait(act, b)
                    if not isinstance(b, int) or b >= 2:
                        factors.free(act, b - 1)
                        chain.free(act, b - 1)
                    a.activation(decay[i][:], rate[:], ACT.Exp, scale=-1.0).then_inc(decay_ready.sem, 1)

                def mix_k(b, i):
                    k_made.wait(act, b)
                    if not isinstance(b, int) or b >= 2:
                        level_made.free(act, b - 1)
                        k_next.free(act, b - 1)
                        q_next.free(act, b - 1)
                        y_made.free(act, b - 1)
                    a.activation(k0[i][:], ps[:, K_BANK, :], ACT.Copy).then_inc(k_kept.sem, 1)

                def mix_v(b, i):
                    v_made.wait(act, b)
                    a.activation(v_rows[i][:].rearrange("p c w -> p (c w)"), ps[:, V_BANK, :], ACT.Copy).then_inc(v_kept.sem, 1)

                def mix_r(b, i):
                    r_made.wait(act, b)
                    a.activation(q0[i][:], ps[:, R_BANK, :], ACT.Copy).then_inc(r_kept.sem, 1)

                def mix_g(b, i):
                    g_made.wait(act, b)
                    g_kept.free(act, b)
                    a.activation(gate_tanh[:], ps[:, G_BANK, :], ACT.Tanh, scale=0.5).then_inc(gt_kept.sem, 1)

                def mix_chain(b, i):
                    for l in range(LEVELS):
                        src = decay[i] if l == 0 else block_decay[l - 1]
                        pairs = src[:].rearrange("p (n two) -> p n two", two=2)
                        if l:
                            chain.wait(act, b, l)
                        else:
                            decay_ready.wait(act, b)
                            q_next.free(act, b)
                            k_next.free(act, b)
                        a.activation(q_factor[l][:, :, 1], pairs[:, :, 0], ACT.Copy)
                        a.activation(k_factor[l][:, :, 0], pairs[:, :, 1], ACT.Copy).then_inc(factors.sem, 1)

                def scan_keys(b, i):
                    kT_made.wait(act, b)
                    kv_made.free(act, b)
                    a.activation(kT[:].rearrange("p c w -> p (c w)"), ps[:, KT_BANK, :], ACT.Copy).then_inc(kT_kept.sem, 1)
                    far_made.wait(act, b)
                    y_made.free(act, b)
                    bank = LEVEL_BANK
                    far = ps[:, bank:bank + NH, :].rearrange("p h (c t) -> p h c t", c=TPB)
                    for at, to in ((slice(0, 32), slice(32, 64)), (slice(64, 96), slice(96, 128)), (slice(0, 64), slice(64, 128))):
                        a.activation(aT[at, :, :, to], far[at, :, :, to], ACT.Copy).then_inc(far_kept.sem, 1)
                    level_kept.wait(act, b)
                    for q in range(P // BLOCK):
                        at = slice(q * BLOCK, (q + 1) * BLOCK)
                        a.activation(aT[at, :, :, at], diag[at, :, :, :], ACT.Copy).then_inc(near_kept.sem, 1)

                def scan_y(b, i):
                    gn.squares(act, b)

                batches(act, mix_lora=mix_lora, mix_td=mix_td, mix_rate=mix_rate, mix_k=mix_k, mix_v=mix_v, mix_r=mix_r,
                        mix_g=mix_g, mix_chain=mix_chain, scan_keys=scan_keys, scan_y=scan_y)

            @block.tensor
            def _(pe):
                t = nc.tensor

                def project(b, bank, weights, f, made, rows=P):
                    mixed_ready.wait(pe, b, f + 1)
                    t.matmul(ps[0:rows, bank, :], weights, mixed[f][:], start=True, stop=True).then_inc(made.sem, 1)

                def mix_lora(b, i):
                    xm_ready.wait(pe, b)
                    g_kept.free(pe, b)
                    shift_ready.free(pe, b)
                    t.matmul(ps[:, 0, :], s["A_lora"][:, 0:P], xm[:], start=True, stop=True)
                    k_kept.free(pe, b)
                    t.matmul(ps[0:LORA, 1, :], s["A_lora"][:, P:], xm[:], start=True, stop=True).then_inc(lora_made.sem, 1)

                def mix_shift(f):
                    def part(b, i):
                        if f == 0:
                            lora_kept.wait(pe, b)
                            r_kept.free(pe, b)
                            ru_kept.free(pe, b)
                        elif f == 1:
                            v_kept.free(pe, b)
                        elif f == 4:
                            shift_ready.wait(pe, b, 1)
                        if f == 4:
                            lhsT, rhs = s["B_lora4"][:], lora4[:]
                        else:
                            lhsT, rhs = s["B_lora"][:, f, :], lora[:]
                        t.matmul(ps[:, MIU_BANK[f], :], lhsT, rhs, start=True, stop=True).then_inc(miu_made.sem, 1)
                    return part

                def mix_td(b, i):
                    shift_ready.wait(pe, b, F_K + 1)
                    project(b, TD_BANK, s["td_A"][:], F_W, td_made, HS)

                def mix_rate(b, i):
                    td_kept.wait(pe, b)
                    shift_ready.wait(pe, b, F_V + 1)
                    t.matmul(ps[:, W_BANK, :], s["td_B"][:], td_hidden[:], start=True, stop=True).then_inc(w_made.sem, 1)

                def mix_k(b, i):
                    shift_ready.wait(pe, b, F_R + 1)
                    project(b, K_BANK, s["WkT"][:], F_K, k_made)

                def mix_v(b, i):
                    mixed_ready.wait(pe, b, F_V + 1)
                    for c in range(TPB):
                        last = t.matmul(ps[:, V_BANK, c * P:(c + 1) * P], mixed[F_V][:, c * P:(c + 1) * P], s["WvT"][:],
                                        start=True, stop=True)
                    last.then_inc(v_made.sem, 1)

                def mix_r(b, i):
                    shift_ready.wait(pe, b, F_G + 1)
                    project(b, R_BANK, s["WrT"][:], F_R, r_made)

                def mix_g(b, i):
                    rate_ready.wait(pe, b)
                    project(b, G_BANK, s["WgT"][:], F_G, g_made)

                def level(b, i, l):
                    if l == 0:
                        needs = [ru_kept.at(b), k_kept.at(b)]
                        q, k = ru[i], k0[i]
                    elif l == 1:
                        needs = [r_kept.at(b), level_kept.at(b, 1)]
                        q, k = q0[i], k0[i]
                    else:
                        needs = [q_next.at(b, l - 1), k_next.at(b, l - 1), level_kept.at(b, l)]
                        q, k = qx[(l - 1) % 2], kx[(l - 1) % 2]
                    wait_apart(pe, passed["pe"], *needs)
                    for c in range(TPB):
                        for block_ in range(P // BLOCK):
                            for h in range(NH):
                                at = slice(h * HS, (h + 1) * HS)
                                tok = slice(c * P + block_ * BLOCK, c * P + (block_ + 1) * BLOCK)
                                last = t.matmul(ps[block_ * BLOCK:(block_ + 1) * BLOCK, LEVEL_BANK + h, c * BLOCK:(c + 1) * BLOCK],
                                                k[at, tok], q[at, tok], start=True, stop=True)
                    last.then_inc(level_made.sem, 1)

                def scan_start(b, i):
                    level(b, i, 0)

                def scan_level(l):
                    return lambda b, i: level(b, i, l)

                def scan_far(b, i):
                    bank = LEVEL_BANK
                    for half in (BLOCK, 2 * BLOCK):
                        l = 5 if half == BLOCK else 6
                        wait_apart(pe, passed["pe"], q_next.at(b, l), k_next.at(b, l), level_kept.at(b))
                        q, k = qx[l % 2], kx[l % 2]
                        for c in range(TPB):
                            for first in range(0, P, 2 * half):
                                for h in range(NH):
                                    at = slice(h * HS, (h + 1) * HS)
                                    last = t.matmul(ps[first:first + half, bank + h, c * P + first + half:c * P + first + 2 * half],
                                                    k[at, c * P + first:c * P + first + half],
                                                    q[at, c * P + first + half:c * P + first + 2 * half],
                                                    start=True, stop=True)
                        last.then_inc(far_made.sem, 1)

                def scan_keys(b, i):
                    k_next.wait(pe, b, LEVELS)
                    x_added.free(pe, b)
                    for c in range(TPB):
                        last = t.transpose(ps[:, KT_BANK, c * P:(c + 1) * P], kx[LEVELS % 2][:, c * P:(c + 1) * P], s["ident"][:])
                    last.then_inc(kT_made.sem, 1)

                def scan_state(b, i):
                    kT_kept.wait(pe, b)
                    v_kept.wait(pe, b)
                    yg_ready.free(pe, b)
                    for c in range(TPB - 1):
                        last = t.matmul(ps[:, KV_BANK, c * P:(c + 1) * P], kT[:, c, :], v_rows[i][:, c, :], start=True, stop=True)
                    last.then_inc(kv_made.sem, 1)

                def scan_y(b, i):
                    far_kept.wait(pe, b)
                    near_kept.wait(pe, b)
                    q_next.wait(pe, b, LEVELS)
                    for c in range(TPB):
                        to = c * P
                        if c:
                            state_step.wait(pe, b, 2 * c)
                            t.matmul(ps[:, Y_BANK, to:to + P], qx[LEVELS % 2][:, to:to + P], state[c - 1][:], start=True, stop=False)
                        for h in range(NH):
                            last = t.matmul(ps[:, Y_BANK, to + h * HS:to + (h + 1) * HS], aT[:, h, c, :],
                                            v_rows[i][:, c, h * HS:(h + 1) * HS], start=(c == 0), stop=(c == 0 or h == NH - 1))
                    last.then_inc(y_made.sem, 1)

                def tail_turn(b, i):
                    gn.wait_done(pe, b)
                    for c in range(TPB):
                        last = t.transpose(ps[:, YT_BANK, c * P:(c + 1) * P], yn[:, c, :], s["ident"][:])
                    last.then_inc(yn_turned.sem, 1)

                def tail_out(b, i):
                    ygT_ready.wait(pe, b)
                    for c in range(TPB):
                        last = t.matmul(ps[:, OUT_BANK, c * P:(c + 1) * P], ygT[:, c * P:(c + 1) * P], s["WoT"][:],
                                        start=True, stop=True)
                    last.then_inc(out_made.sem, 1)

                batches(pe, mix_lora=mix_lora, **{f"mix_shift{f}": mix_shift(f) for f in range(5)}, mix_td=mix_td,
                        mix_rate=mix_rate, mix_k=mix_k, mix_v=mix_v, mix_r=mix_r, mix_g=mix_g,
                        scan_start=scan_start, **{f"scan_level{l}": scan_level(l) for l in range(1, DIAG_LEVELS + 1)},
                        scan_far=scan_far, scan_keys=scan_keys, scan_state=scan_state, scan_y=scan_y,
                        tail_turn=tail_turn, tail_out=tail_out)


MIU_BANK = (2, 3, 0, 1, 2)
TD_BANK, W_BANK, K_BANK, V_BANK, R_BANK, G_BANK = 3, 0, 1, 3, 2, 0
LEVEL_BANK = 4
KT_BANK, KV_BANK, Y_BANK, YT_BANK, OUT_BANK = 6, 7, 6, 7, 6
ORDER = (("scan", "start"), ("mix", "lora"), ("tail", "norm"), ("scan", "level1"), ("mix", "shift0"),
         ("mix", "mixed0"), ("scan", "level2"), ("mix", "shift1"), ("tail", "turn"), ("mix", "mixed1"),
         ("scan", "level3"), ("mix", "shift2"), ("tail", "out"), ("mix", "td"), ("mix", "mixed2"), ("scan", "level4"),
         ("mix", "shift3"), ("mix", "rate"), ("scan", "level5"), ("mix", "shift4"), ("next", "xm"), ("scan", "far"),
         ("mix", "mixed3"), ("mix", "k"), ("scan", "keys"), ("mix", "mixed4"), ("mix", "v"), ("scan", "state"),
         ("mix", "r"), ("mix", "g"), ("mix", "chain"), ("mix", "first_k"), ("scan", "y"))


def program(nc, d, out):
    with Phase(nc) as ctx:
        def sb(name, shape, dt=F32):
            return ctx.enter_context(nc.sbuf_tensor(own(nc, name), shape, dt))

        ps = ctx.enter_context(nc.psum_tensor("ps", [P, 8, 512], F32))
        x_all, z_all = sb("x_all", [P, NT, P]), sb("z_all", [P, NT, P])
        y_all = sb("y_all", [P, NT, P])
        qd = nc.dram_tensor("q_split", (SPLITS * DK, H, TOK), BF16, kind="Internal").ap()
        kd = nc.dram_tensor("k_split", (SPLITS * DK, H, TOK), BF16, kind="Internal").ap()
        xs = nc.dram_tensor("sorted_in", (SLOTS * P, P), F32, kind="Internal").ap()
        ys = nc.dram_tensor("sorted_out", (SLOTS * P, P), F32, kind="Internal").ap()
        s = load_constants(nc, ctx, d, y_all, xs)
        logits, slot, expert = sb("logits", [P, NT, E]), sb("slot", [P, NT], I32), sb("expert", [P, SLOTS], I32)

        def ffn(x_dram):
            with ExitStack() as inner:
                v_all = inner.enter_context(nc.sbuf_tensor(own(nc, "v_all"), [P, NT, H, DK + 1], F32))
                qkv_phase(nc, ps, s, x_all, z_all, v_all, x_dram, qd, kd)
                attention_phase(nc, ps, s, v_all, y_all, qd, kd)
            project_phase(nc, ps, s, x_all, z_all, y_all, logits)
            route_phase(nc, ps, s, y_all, logits, slot, expert, xs)
            expert_phase(nc, ps, s, expert, xs, ys)
            combine_phase(nc, x_all, y_all, slot, ys)

        ffn(d["L0_attn_x"])
        with ExitStack() as inner:
            zT = inner.enter_context(nc.sbuf_tensor("zT", [P, B, T + 1], F32))
            turn_phase(nc, ps, s, x_all, zT)
            recurrence_phase(nc, ps, s, x_all, zT)
        ffn(None)
        out_stored = ctx.semaphore("out_stored")
        with nc.Block() as block:
            @block.sync
            def _(sp):
                sp.dma_start(out.rearrange("b t c -> (b t) c").rearrange("(n p) c -> p n c", p=P), x_all[:]).then_inc(out_stored, 16)
                sp.wait_ge(out_stored, 16)


_INS = ['L0_attn_x', 'L0_ffn_w_proj', 'L0_ffn_ln1_w', 'L0_ffn_ln1_b', 'L0_ffn_ln2_w', 'L0_ffn_ln2_b',
        'L0_attn_miu_x', 'L0_attn_A_lora', 'L0_attn_B_lora', 'L0_attn_td_miu', 'L0_attn_td_A', 'L0_attn_td_B',
        'L0_attn_u', 'L0_attn_gn_gamma', 'L0_attn_gn_beta', 'L0_ffn_gate_w', 'L0_ffn_gate_b', 'L0_ffn_w1', 'L0_ffn_w2']


def kernel(**inputs):
    import numpy as _np
    import concourse.bacc as _bacc
    from concourse import mybir as _mybir
    from concourse.bass_utils import run_bass_kernel_spmd as _run

    nc = _bacc.Bacc("TRN2", target_bir_lowering=False, num_devices=1)
    arrays, d = {}, {}

    def give(name, a):
        a = _np.ascontiguousarray(a)
        arrays[f"in_{name}"] = a
        d[name] = nc.dram_tensor(f"in_{name}", a.shape, _mybir.dt.from_np(a.dtype), kind="ExternalInput").ap()

    for name in _INS:
        give(name, inputs[name])
    w = _np.array(inputs["L0_ffn_w_qkv"])
    for i in range(0, 2 * P, P):
        w[:, i:i + P] = w[:, i:i + P].reshape(P, H, DK).transpose(0, 2, 1).reshape(P, P)
    give("w_qkv", w)
    for name in ("Wk", "Wv", "Wr", "Wg", "Wo"):
        give(name + "T", _np.asarray(inputs["L0_attn_" + name]).T)
    give("lambda_columns", _np.asarray(inputs["L0_attn_lambda_"]).reshape(5, P).T)
    give("ident", _np.eye(P, dtype=_np.float32))
    give("below", _np.triu(_np.ones((P, P), _np.float32), 1))
    give("counts", _np.tile(_np.arange(SLOTS, dtype=_np.float32), (P, 1)))
    give("restart", _np.tile((_np.arange(E * NT) % NT != 0).astype(_np.float32), (P, 1)))
    key, query = _np.arange(P)[:, None] % BLOCK, _np.arange(BLOCK)[None, :]
    masks = [key == query]
    for level in range(DIAG_LEVELS):
        m = 1 << level
        masks.append((key // (2 * m) == query // (2 * m)) & (key % (2 * m) < m) & (query % (2 * m) >= m))
    give("level_masks", _np.stack(masks, axis=1).astype(_np.int32))
    out = nc.dram_tensor("out_0", (8, 512, 128), _mybir.dt.float32, kind="ExternalOutput").ap()
    program(nc, d, out)
    r = _run(nc, [arrays], core_ids=[0])
    return r.results[0]["out_0"]
```

```python
from contextlib import ExitStack

import concourse.bass as bass
from concourse import mybir

F32 = mybir.dt.float32
BF16 = mybir.dt.bfloat16
I32 = mybir.dt.int32
ALU = mybir.AluOpType
ACT = mybir.ActivationFunctionType
AX_X = mybir.AxisListType.X
ds = bass.ds

P = 128
B, T = 8, 512
TOK = B * T
NT = TOK // P
TPB = T // P
H, DK = 16, 8
GROUP = 4
NG = H // GROUP
SPLITS = 3
ROWS = SPLITS * SPLITS * DK
MAXROW = 96
STACK = MAXROW + SPLITS
TWO_ONES = 1.0 + 0x3F80 * 2.0 ** -23
VW = 32
E, HID = 8, 512
HC = HID // P
SLOTS = TOK // P + E
EPS = 1e-5
RING = 4
SL = 8
ST = NT // SL
SW = ST * P


def own(nc, name):
    return f"{name}_{nc.next_id()}"


class Phase(ExitStack):

    def __init__(self, nc):
        super().__init__()
        self.nc, self.semaphores = nc, []

    def semaphore(self, name):
        self.semaphores.append(self.nc.alloc_semaphore(own(self.nc, name)))
        return self.semaphores[-1]

    def __exit__(self, *failure):
        if failure[0] is None:
            self.nc.clear_and_free_semaphores(self.semaphores)
            self.nc.all_engine_barrier()
        return super().__exit__(*failure)


def wait_apart(eng, passed, *waits):
    for sem, value in waits:
        eng.wait_ge(sem, value)
    eng.sem_inc(passed, 1)


def pipeline(eng, count, stages, step, unroll=2):
    peeled = -(-(stages + stages % 2 + 2) // unroll) * unroll
    for j in range(peeled):
        step(j, j % unroll, lambda k, j=j: j >= k)
    with eng.Fori(peeled // unroll, count // unroll) as turn:
        for i in range(unroll):
            step(unroll * turn + i, i, lambda k: True)
    for j in range(count, count + stages):
        step(j, j % unroll, lambda k, j=j: j - k < count)


def after(eng, sem, j, back=0, per=1):
    if not isinstance(j, int) or j - back >= 0:
        eng.wait_ge(sem, (j - back + 1) * per)


def after_same_parity(eng, sem, j, i, back=0, per=16):
    if not isinstance(j, int) or j - back >= 0:
        eng.wait_ge(sem, (j - back - i) * (per // 2) + per)


class LayerNorm:

    def __init__(self, nc, ctx, name, tiles, eps, width=P, bufs=1):
        self.nc, self.tiles, self.eps, self.width, self.bufs = nc, tiles, eps, width, bufs

        def sb(what, shape, dt=F32):
            return ctx.enter_context(nc.sbuf_tensor(own(nc, f"{name}_{what}"), shape, dt))

        self.total, self.mean = sb("total", [P, tiles]), sb("mean", [P, tiles])
        self.square_sum, self.power = sb("square_sum", [P, tiles]), sb("power", [P, tiles])
        self.square = sb("square", [P, tiles, width])
        self.var, self.rstd = sb("var", [P, bufs, tiles]), sb("rstd", [P, bufs, tiles])
        self.centered = [sb(f"centered{i}", [P, tiles, width]) for i in range(bufs)]

        def sem(what):
            return ctx.semaphore(f"{name}_{what}")

        self.passed = sem("passed")
        self.mean_step, self.sum_step, self.pool_step = sem("mean_step"), sem("sum_step"), sem("pool_step")
        self.is_centered, self.is_squared = sem("is_centered"), sem("is_squared")
        self.var_ready, self.done = sem("var_ready"), sem("done")

    def wide(self, a):
        return a.unsqueeze(2).broadcast_to([P, self.tiles, self.width])

    def start(self, pool):
        self.nc.gpsimd.memset(self.power[:], -0.5).then_inc(self.done, 1)

    def center(self, vec, n, src, i=0):
        v = self.nc.vector
        v.tensor_reduce(self.total[:], src, AX_X, ALU.add).then_inc(self.mean_step, 1)
        vec.wait_ge(self.mean_step, 2 * n + 1)
        v.tensor_scalar(self.mean[:], self.total[:], 1.0 / self.width, None, ALU.mult).then_inc(self.mean_step, 1)
        vec.wait_ge(self.mean_step, 2 * n + 2)
        if not isinstance(n, int) or n >= self.bufs:
            vec.wait_ge(self.done, n - self.bufs + 2)
        v.tensor_tensor(self.centered[i][:], src, self.wide(self.mean[:]), ALU.subtract).then_inc(self.is_centered, 1)

    def squares(self, act, n, i=0):
        act.wait_ge(self.is_centered, n + 1)
        self.nc.scalar.activation(self.square[:], self.centered[i][:], ACT.Square).then_inc(self.is_squared, 1)

    def variance(self, vec, n, i=0):
        v = self.nc.vector
        vec.wait_ge(self.is_squared, n + 1)
        if self.bufs > 1 and (not isinstance(n, int) or n >= 1):
            vec.wait_ge(self.var_ready, n)
        v.tensor_reduce(self.square_sum[:], self.square[:], AX_X, ALU.add).then_inc(self.sum_step, 1)
        vec.wait_ge(self.sum_step, n + 1)
        v.tensor_scalar(self.var[:, i, :], self.square_sum[:], 1.0 / self.width, self.eps, ALU.mult,
                        ALU.add).then_inc(self.var_ready, 1)

    def power_(self, pool, n, i=0):
        pool.wait_ge(self.var_ready, n + 1)
        pool.wait_ge(self.done, n + 1)
        self.nc.gpsimd.tensor_tensor(self.rstd[:, i, :], self.var[:, i, :], self.power[:],
                                     ALU.pow).then_inc(self.pool_step, 1)

    def scale(self, pool, n, dst, i=0, *waits):
        self.power_(pool, n, i)
        wait_apart(pool, self.passed, (self.pool_step, n + 1), *waits)
        self.nc.gpsimd.tensor_tensor(dst, self.centered[i][:], self.wide(self.rstd[:, i, :]), ALU.mult).then_inc(self.done, 1)

    def scale_on_vector(self, vec, n, dst, i=0):
        vec.wait_ge(self.pool_step, n + 1)
        self.nc.vector.tensor_tensor(dst, self.centered[i][:], self.wide(self.rstd[:, i, :]), ALU.mult).then_inc(self.done, 1)

    def wait_done(self, eng, n):
        eng.wait_ge(self.done, n + 2)

    def done_free(self, eng, n):
        eng.wait_ge(self.done, n + 1)


def slices_of(x_dram):
    return x_dram.rearrange("b t c -> (b t) c").rearrange("(n p) c -> p n c", p=P)


def tiles_of(dram):
    return dram.rearrange("(n p) c -> p n c", p=P)


def load_constants(nc, ctx, d, x_all, padding, xs):
    s = {}

    def sb(name, shape, dt=F32):
        s[name] = ctx.enter_context(nc.sbuf_tensor(own(nc, name), shape, dt))
        return s[name]

    def column(name):
        return d["L0_ffn_" + name].rearrange("(c a) -> c a", a=1)

    first = [(sb("ident", [P, P]), d["ident"]), (sb("w_qkv", [P, 3 * P]), d["w_qkv"]),
             (sb("ln1_w", [P, 1]), column("ln1_w")), (sb("ln1_b", [P, 1]), column("ln1_b"))]
    rest = [(sb("w_proj", [P, P]), d["L0_ffn_w_proj"]),
            (sb("ln2_w", [P, 1]), column("ln2_w")), (sb("ln2_b", [P, 1]), column("ln2_b")),
            (sb("gate_w", [P, E]), d["L0_ffn_gate_w"]),
            (sb("gate_b", [P, E]), d["L0_ffn_gate_b"].rearrange("(a e) -> a e", a=1).broadcast_to([P, E])),
            (sb("below", [P, P]), d["below"]),
            (sb("counts", [P, SLOTS]), d["counts"]), (sb("restart", [P, E * NT]), d["restart"]),
            (sb("token", [P, NT]), d["token"]),
            (sb("w1", [P, E, HID]), d["L0_ffn_w1"].rearrange("e c h -> c e h")),
            (sb("w2", [P, E, HC, P]), d["L0_ffn_w2"].rearrange("e (k c) d -> c e k d", c=P))]
    a = "L0_attn_"
    for name in ("WkT", "WvT", "WrT", "WgT", "WoT"):
        rest.append((sb(name, [P, P]), d[name]))
    rest += [(sb("A_lora", [P, 5 * LORA]), d[a + "A_lora"]), (sb("td_A", [P, HS]), d[a + "td_A"]),
             (sb("td_B", [HS, P]), d[a + "td_B"]), (sb("B_lora4", [LORA, P]), d[a + "B_lora"][4]),
             (sb("lambda", [P, 5]), d["lambda_columns"]), (sb("miu_x", [P, 1]), d[a + "miu_x"].rearrange("a b c -> c (a b)")),
             (sb("td_miu", [P, 1]), d[a + "td_miu"].rearrange("a b c -> c (a b)")),
             (sb("u", [P, 1]), d[a + "u"].rearrange("h (n a) -> (h n) a", a=1)),
             (sb("gn_w", [P, 1]), d[a + "gn_gamma"].rearrange("(c a) -> c a", a=1)),
             (sb("gn_b", [P, 1]), d[a + "gn_beta"].rearrange("(c a) -> c a", a=1)),
             (sb("level_masks", [P, DIAG_LEVELS + 1, BLOCK], I32), d["level_masks"])]
    sb("B_lora", [P, 4, P])
    sb("gn_w_half", [P, 1])
    sb("gn_b_half", [P, 1])
    sb("ident16", [P, P], BF16)
    sb("ones", [P, P])
    loaded, rest_loaded = ctx.semaphore("constants_loaded"), ctx.semaphore("rest_loaded")
    s["x_loaded"] = [ctx.semaphore("x_loaded0"), ctx.semaphore("x_loaded1")]
    cast = ctx.semaphore("ident_cast")
    zeros_set, zeroed = ctx.semaphore("zeros_set"), ctx.semaphore("zeroed")
    x_slices = slices_of(d["L0_attn_x"])

    def load_rest(sp):
        with sp.Fori(1, SL // 2) as pair:
            for i in range(2):
                sp.wait_ge(s["x_loaded"][i], 16 * pair)
                here = ds((2 * pair + i) * ST, ST)
                sp.dma_start(x_all[:, here, :], x_slices[:, here, :]).then_inc(s["x_loaded"][i], 16)
        for dst, src in rest:
            sp.dma_start(dst[:], src).then_inc(rest_loaded, 16)
        for f in range(4):
            at = slice(f * LORA, (f + 1) * LORA)
            sp.dma_start(s["B_lora"][at, f, :], d[a + "B_lora"][f]).then_inc(rest_loaded, 16)
        for copy in xs:
            for i in range(0, SLOTS, NT // 4):
                sp.dma_start(tiles_of(copy)[:, i:i + NT // 4, :], padding[:, 0:NT // 4, :]).then_inc(zeroed, 16)

    def wait_rest(sp):
        sp.wait_ge(rest_loaded, 16 * (len(rest) + 4))
        sp.wait_ge(zeroed, 16 * 2 * (SLOTS // (NT // 4)))

    with nc.Block() as block:
        @block.sync
        def _(sp):
            for dst, src in first:
                sp.dma_start(dst[:], src).then_inc(loaded, 16)
            for i in range(2):
                here = slice(i * ST, (i + 1) * ST)
                sp.dma_start(x_all[:, here, :], x_slices[:, here, :]).then_inc(s["x_loaded"][i], 16)
            sp.wait_ge(loaded, 16 * len(first))
            sp.wait_ge(zeros_set, 3)

        @block.vector
        def _(vec):
            vec.wait_ge(loaded, 16 * len(first))
            nc.vector.tensor_copy(s["ident16"][:], s["ident"][:]).then_inc(cast, 1)
            nc.vector.memset(s["ones"][:], 1.0).then_inc(cast, 1)
            vec.wait_ge(cast, 2)

        @block.gpsimd
        def _(pool):
            nc.gpsimd.memset(s["B_lora"][:], 0.0).then_inc(zeros_set, 1)
            nc.gpsimd.memset(padding[:, 0:NT // 4, 0:P], 0.0).then_inc(zeros_set, 1)
            nc.gpsimd.memset(padding[:, 0:NT // 4, P:], float(TOK)).then_inc(zeros_set, 1)
    return s, load_rest, wait_rest


def qkv_phase(nc, ps, s, x_all, z_all, v_all, qd, kd, load=None):
    with Phase(nc) as ctx:
        def sb(name, shape, dt=F32):
            return ctx.enter_context(nc.sbuf_tensor(own(nc, name), shape, dt))

        sems = []

        def sem(name):
            x = ctx.semaphore(name)
            sems.append(x)
            return x

        def sbs(name, shape, dt=F32):
            return [sb(f"{name}{i}", shape, dt) for i in range(2)]

        def sem(name):
            return ctx.semaphore(name)

        lna = LayerNorm(nc, ctx, "lna", ST, EPS, bufs=2)
        lnb = LayerNorm(nc, ctx, "lnb", ST, EPS, bufs=2)
        zn, hT = sbs("zn", [P, ST, P]), sbs("hT", [P, SW])
        parts = {k: sbs(k + "_parts", [P, SPLITS, SW], BF16) for k in "qk"}
        rest = {k: sbs(k + "_rest", [P, SW]) for k in "qk"}
        ones_set, turned, h_ready = sem("ones_set"), sem("turned"), sem("h_ready")
        made = {k: sem(k + "_made") for k in "qkv"}
        high, mid, low, diff = ({k: sem(k + w) for k in "qk"} for w in ("_high", "_mid", "_low", "_diff"))
        v_kept, stored = sem("v_kept"), {k: [sem(k + "_stored0"), sem(k + "_stored1")] for k in "qk"}
        psT, psV = [ps[:, i, :] for i in range(2)], [ps[:, 6 + i, :] for i in range(2)]
        psX = {"q": [ps[:, 2 + i, :] for i in range(2)], "k": [ps[:, 4 + i, :] for i in range(2)]}

        with nc.Block() as block:
            @block.sync
            def _(sp):
                def step(j, i, present):
                    o = 1 - i
                    if present(3):
                        for k, dram in (("q", qd), ("k", kd)):
                            after(sp, low[k], j, 3)
                            sp.dma_start(dram.rearrange("(c i) h t -> (i h) c t", i=DK)[:, :, ds((j - 3) * SW, SW)],
                                         parts[k][o][:]).then_inc(stored[k][o], 16)

                if load is not None:
                    load[0](sp)
                pipeline(sp, SL, 3, step)
                for k in "qk":
                    for i in range(2):
                        sp.wait_ge(stored[k][i], 16 * SL // 2)
                if load is not None:
                    load[1](sp)

            @block.vector
            def _(vec):
                v = nc.vector

                def step(j, i, present):
                    o = 1 - i
                    if present(0):
                        if load is not None:
                            after_same_parity(vec, s["x_loaded"][i], j, i)
                        lna.center(vec, j, x_all[:, ds(j * ST, ST), :], i)
                    if present(1):
                        lna.wait_done(vec, j - 1)
                        lnb.center(vec, j - 1, z_all[:, ds((j - 1) * ST, ST), :], o)
                    if present(3):
                        for k in "qk":
                            after(vec, high[k], j, 3)
                            after(vec, low[k], j, 5)
                            v.tensor_tensor(rest[k][o][:], psX[k][o], parts[k][o][:, 0, :],
                                            ALU.subtract).then_inc(diff[k], 1)
                    if present(0):
                        lna.variance(vec, j, i)
                    if present(1):
                        lnb.variance(vec, j - 1, o)

                pipeline(vec, SL, 3, step)

            @block.scalar
            def _(act):
                a = nc.scalar

                def step(j, i, present):
                    o = 1 - i
                    if present(3):
                        for k in "qk":
                            after(act, made[k], j, 3)
                            after_same_parity(act, stored[k][o], j - 3, o, 2)
                            a.activation(parts[k][o][:, 0, :], psX[k][o], ACT.Copy).then_inc(high[k], 1)
                    if present(0):
                        lna.squares(act, j, i)
                    if present(1):
                        lnb.squares(act, j - 1, o)
                    if present(2):
                        after(act, turned, j, 2)
                        after(act, made["v"], j, 4)
                        a.activation(hT[i][:], psT[i], ACT.Identity, bias=s["ln1_b"][:, 0:1],
                                     scale=s["ln1_w"][:, 0:1]).then_inc(h_ready, 1)
                    if present(3):
                        after(act, made["v"], j, 3)
                        if isinstance(j, int) and j == 3:
                            act.wait_ge(ones_set, 1)
                        a.activation(v_all[:, ds((j - 3) * ST, ST), :, 0:DK],
                                     psV[o].rearrange("p (t h d) -> p t h d", h=H, d=DK), ACT.Copy).then_inc(v_kept, 1)
                    if present(3):
                        for k in "qk":
                            after(act, diff[k], j, 3)
                            a.activation(parts[k][o][:, 1, :], rest[k][o][:], ACT.Copy).then_inc(mid[k], 1)

                pipeline(act, SL, 3, step)

            @block.gpsimd
            def _(pool):
                g = nc.gpsimd

                def step(j, i, present):
                    o = 1 - i
                    if present(0):
                        lna.scale(pool, j, z_all[:, ds(j * ST, ST), :], i)
                    if present(1):
                        free = [] if isinstance(j, int) and j < 3 else [(turned, j - 2)]
                        lnb.scale(pool, j - 1, zn[o][:], o, *free)
                    if present(3):
                        for k in "qk":
                            after(pool, mid[k], j, 3)
                            g.tensor_tensor(parts[k][o][:, 2, :], rest[k][o][:], parts[k][o][:, 1, :],
                                            ALU.subtract).then_inc(low[k], 1)

                lna.start(pool)
                lnb.start(pool)
                g.memset(v_all[:, :, :, DK:], 1.0).then_inc(ones_set, 1)
                pipeline(pool, SL, 3, step)

            @block.tensor
            def _(pe):
                t = nc.tensor

                def step(j, i, present):
                    o = 1 - i
                    if present(3):
                        after(pe, h_ready, j, 3)
                        for m, k in enumerate("qk"):
                            after(pe, diff[k], j, 5)
                            t.matmul(psX[k][o], s["w_qkv"][:, m * P:(m + 1) * P], hT[o][:],
                                     start=True, stop=True).then_inc(made[k], 1)
                        after(pe, v_kept, j, 5)
                        for q in range(ST):
                            last = t.matmul(psV[o][:, q * P:(q + 1) * P], hT[o][:, q * P:(q + 1) * P],
                                            s["w_qkv"][:, 2 * P:], start=True, stop=True)
                        last.then_inc(made["v"], 1)
                    if present(2):
                        lnb.wait_done(pe, j - 2)
                        for q in range(ST):
                            last = t.transpose(psT[i][:, q * P:(q + 1) * P], zn[i][:, q, :], s["ident"][:])
                        last.then_inc(turned, 1)

                pipeline(pe, SL, 3, step)


def attention_phase(nc, ps, s, v_all, y_all, qd, kd):
    with Phase(nc) as ctx:
        def sb(name, shape, dt=F32):
            return ctx.enter_context(nc.sbuf_tensor(own(nc, name), shape, dt))

        def sem(name):
            return ctx.semaphore(name)

        qs = [sb(f"q_stack{i}", [P, GROUP, T], BF16) for i in range(NG)]
        ks = [sb(f"k_stack{i}", [P, GROUP, T], BF16) for i in range(NG)]
        vs = [sb(f"v_stack{i}", [P, TPB, GROUP, VW]) for i in range(NG)]
        probs = [sb(f"probs{i}", [P, GROUP, T]) for i in range(2)]
        maxima = [sb(f"maxima{i}", [P, GROUP, TPB]) for i in range(2)]
        neg_rest = sb("neg_rest", [P, GROUP * TPB])
        neg_parts = sb("neg_parts", [P, SPLITS, GROUP * TPB], BF16)
        max_rows = [sb(f"max_rows{i}", [SPLITS * GROUP * TPB, P], BF16) for i in range(2)]
        oT = sb("oT", [P, T])
        inv = sb("inv", [P, TPB, GROUP])

        k_zeroed, k_set = [sem("k_zeroed0"), sem("k_zeroed1")], [sem("k_set0"), sem("k_set1")]
        q_set, v_set = sem("q_set"), sem("v_set")
        loaded = [sem(f"stack_loaded{i}") for i in range(NG)]
        pool_passed, pe_passed = sem("pool_passed"), sem("pe_passed")
        v_staged = sem("v_staged")
        s_ready, s_read = sem("s_ready"), sem("s_read")
        e_ready, e_read = sem("e_ready"), sem("e_read")
        pv_unit = sem("pv_unit")
        split_step, split_done, rows_turned, rows_kept, rows_placed = (
            sem("split_step"), sem("split_done"), sem("rows_turned"), sem("rows_kept"), sem("rows_placed"))
        o_kept, o_turned, inv_ready, o_done = sem("o_kept"), sem("o_turned"), sem("inv_ready"), sem("o_done")

        psS = ps[:, 0:4, :]
        psE = ps[:, 4:6, :]
        psO = [ps[:, 6, :], ps[:, 7, :]]
        NMAX = GROUP * TPB
        PER_LOAD = 16 * (2 * SPLITS + SPLITS - 1)
        PLACED = 16

        def in_pairs(stack):
            return stack.rearrange("p h t -> p (h t)").bitcast(F32)

        def set_keys(eng, engine, half):
            stacks = ks[2 * half:2 * half + 2]
            for stack in stacks:
                engine.memset(in_pairs(stack[:]), 0.0).then_inc(k_zeroed[half], 1)
            eng.wait_ge(k_zeroed[half], 2)
            for stack in stacks:
                engine.memset(in_pairs(stack[MAXROW:STACK, :, :]), TWO_ONES).then_inc(k_set[half], 1)

        def bodies(eng, step):
            for g in range(NG):
                step(0, g, True, False)
            with eng.Fori(1, B - 1) as b:
                for g in range(NG):
                    step(b, g, False, False)
            for g in range(NG):
                step(B - 1, g, False, True)

        with nc.Block() as block:
            @block.sync
            def _(sp):
                def load_group(b, g):
                    heads = slice(g * GROUP, (g + 1) * GROUP)
                    for a in range(SPLITS):
                        row = a * SPLITS * DK
                        for st, dram, turn in ((qs, qd, 0), (ks, kd, a)):
                            first = (SPLITS - turn) * DK
                            sp.dma_start(st[g][row:row + first, :, :],
                                         dram[turn * DK:, heads, ds(b * T, T)]).then_inc(loaded[g], 16)
                            if turn:
                                sp.dma_start(st[g][row + first:row + SPLITS * DK, :, :],
                                             dram[0:turn * DK, heads, ds(b * T, T)]).then_inc(loaded[g], 16)

                for g in range(NG):
                    sp.wait_ge(q_set, g + 1)
                    sp.wait_ge(k_set[g // 2], g % 2 + 1)
                    load_group(0, g)
                with sp.Fori(1, B) as b:
                    for g in range(NG):
                        sp.wait_ge(e_ready, GROUP * TPB * (NG * b + g - NG + 1))
                        load_group(b, g)

            @block.gpsimd
            def _(pool):
                g_ = nc.gpsimd
                for i in range(NG):
                    g_.memset(in_pairs(qs[i][:]), 0.0).then_inc(q_set, 1)
                for i in range(NG):
                    last = g_.memset(vs[i][:], 0.0)
                last.then_inc(v_set, 1)
                set_keys(pool, g_, 1)
                pool.wait_ge(k_set[1], 2)

                def stage(b, g):
                    g_.tensor_copy(vs[g][:, :, :, 0:DK + 1],
                                   v_all[:, ds(b * TPB, TPB), g * GROUP:(g + 1) * GROUP, :]).then_inc(v_staged, 1)

                def place(g, i, count):
                    wait_apart(pool, pool_passed, (rows_kept, count))
                    pool.dma_start(qs[g][MAXROW:STACK, :, :],
                                   max_rows[i][:]).then_inc(rows_placed, 16)

                def split_max(i, group):
                    m = maxima[i][:].rearrange("p h q -> p (h q)")
                    turned = [] if isinstance(group, int) and group == 0 else [(rows_turned, group)]
                    wait_apart(pool, pool_passed, (s_read, 8 * group + 8), *turned)
                    g_.tensor_scalar(neg_rest[:], m, -1.0, None, ALU.mult).then_inc(split_step, 1)
                    wait_apart(pool, pool_passed, (split_step, 4 * group + 1))
                    g_.tensor_copy(neg_parts[:, 0, :], neg_rest[:]).then_inc(split_step, 1)
                    wait_apart(pool, pool_passed, (split_step, 4 * group + 2))
                    g_.tensor_tensor(neg_rest[:], neg_rest[:], neg_parts[:, 0, :], ALU.subtract).then_inc(split_step, 1)
                    wait_apart(pool, pool_passed, (split_step, 4 * group + 3))
                    g_.tensor_copy(neg_parts[:, 1, :], neg_rest[:]).then_inc(split_step, 1)
                    wait_apart(pool, pool_passed, (split_step, 4 * group + 4))
                    g_.tensor_tensor(neg_parts[:, 2, :], neg_rest[:], neg_parts[:, 1, :],
                                     ALU.subtract).then_inc(split_done, 1)

                pool.wait_ge(v_set, 1)
                for g in range(NG):
                    stage(0, g)
                split_max(0, 0)
                place(0, 0, 1)
                split_max(1, 1)

                def step(b, g, first, last):
                    if not (last and g == NG - 1):
                        place((g + 1) % NG, (g + 1) % 2, NG * b + g + 2)
                    if not first or g > 0:
                        bb, gg = (b, g - 1) if g else (b - 1, NG - 1)
                        if not last or g == 0:
                            pool.wait_ge(pv_unit, TPB * (NG * b + g))
                            stage(bb + 1, gg)
                    if not (last and g >= NG - 2):
                        split_max(g % 2, NG * b + g + 2)

                bodies(pool, step)

            @block.tensor
            def _(pe):
                t = nc.tensor

                def s_pair(g, u, pair, count):
                    if not (isinstance(count, int) and count < 2):
                        pe.wait_ge(s_read, count - 1)
                    for h in (2 * pair, 2 * pair + 1):
                        last = t.matmul(psS[:, h, :], qs[g][0:MAXROW, h, u * P:(u + 1) * P], ks[g][0:MAXROW, h, :],
                                        start=True, stop=True)
                    last.then_inc(s_ready, 1)

                def e_head(g, u, h, count):
                    if not (isinstance(count, int) and count < 2):
                        pe.wait_ge(e_read, count - 1)
                    t.matmul(psE[:, h % 2, :], ks[g][0:STACK, h, u * P:(u + 1) * P], qs[g][0:STACK, h, :],
                             start=True, stop=True).then_inc(e_ready, 1)

                def pv(g, u, unit):
                    pe.wait_ge(e_read, 4 * unit + 4)
                    for h in range(GROUP):
                        last = t.matmul(psO[g % 2][VW * h:VW * (h + 1), :], vs[g][:, u, h, :], probs[u % 2][:, h, :],
                                        start=(u == 0), stop=(u == TPB - 1))
                    last.then_inc(pv_unit, 1)

                def turn_max(g, count, *bank_free):
                    wait_apart(pe, pe_passed, (split_done, count), *bank_free)
                    t.transpose(psO[g % 2][0:SPLITS * NMAX, 0:P // 2].bitcast(BF16),
                                neg_parts[:].rearrange("p c m -> p (c m)"), s["ident16"][:]).then_inc(rows_turned, 1)

                for i in range(2):
                    pe.wait_ge(loaded[i], PER_LOAD)
                    for u in range(TPB):
                        for pair in range(2):
                            s_pair(i, u, pair, 8 * i + 2 * u + pair)
                    if i == 0:
                        turn_max(0, 1)

                def step(b, g, first, last):
                    G = NG * b + g
                    ahead = not (last and g >= NG - 2)
                    g2, b2 = (g + 2) % NG, (b if g < 2 else b + 1)
                    for u in range(TPB):
                        if u == 0:
                            pe.wait_ge(rows_placed, PLACED * (G + 1))
                            if ahead:
                                pe.wait_ge(loaded[g2], PER_LOAD * (b2 + 1))
                        unit = TPB * G + u
                        e_head(g, u, 0, 4 * unit)
                        e_head(g, u, 1, 4 * unit + 1)
                        if u > 0:
                            if u == 1:
                                pe.wait_ge(v_staged, G + 1)
                                if not (first and g < 2):
                                    pe.wait_ge(rows_kept, G + 1)
                                    pe.wait_ge(o_done, G - 1)
                                else:
                                    pe.wait_ge(rows_kept, G + 1)
                            pv(g, u - 1, unit - 1)
                            if u == 2 and not (last and g == NG - 1):
                                turn_max((g + 1) % NG, G + 2, *([] if first and g == 0 else [(o_done, G)]))
                        elif not (first and g == 0):
                            pv((g - 1) % NG, TPB - 1, unit - 1)
                        e_head(g, u, 2, 4 * unit + 2)
                        e_head(g, u, 3, 4 * unit + 3)
                        if u == 1 and not (first and g == 0):
                            turn_o((g - 1) % NG, G)
                        if ahead:
                            for pair in range(2):
                                s_pair(g2, u, pair, 8 * (G + 2) + 2 * u + pair)

                def turn_o(g, count):
                    pe.wait_ge(o_kept, count)
                    for q in range(TPB):
                        last = t.transpose(psO[g % 2][:, q * P:(q + 1) * P], oT[:, q * P:(q + 1) * P], s["ident"][:])
                    last.then_inc(o_turned, 1)

                bodies(pe, step)
                pv(NG - 1, TPB - 1, TPB * NG * B - 1)
                turn_o(NG - 1, NG * B)

            @block.scalar
            def _(act):
                a = nc.scalar

                def keep_rows(g, i, count):
                    act.wait_ge(rows_turned, count)
                    if not (isinstance(count, int) and count < 3):
                        act.wait_ge(rows_placed, PLACED * (count - 2))
                    a.activation(max_rows[i][:], psO[g % 2][0:SPLITS * NMAX, 0:P // 2].bitcast(BF16),
                                 ACT.Copy).then_inc(rows_kept, 1)

                def keep_o(g, count):
                    act.wait_ge(pv_unit, TPB * count)
                    if not (isinstance(count, int) and count < 2):
                        act.wait_ge(o_turned, count - 1)
                    a.activation(oT[:], psO[g % 2], ACT.Copy).then_inc(o_kept, 1)

                keep_rows(0, 0, 1)

                def step(b, g, first, last):
                    G = NG * b + g
                    for u in range(TPB):
                        unit = TPB * G + u
                        for h in range(GROUP):
                            act.wait_ge(e_ready, 4 * unit + h + 1)
                            if h == 0 and not (first and g == 0 and u < 2):
                                act.wait_ge(pv_unit, unit - 1)
                            a.activation(probs[u % 2][:, h, :], psE[:, h % 2, :], ACT.Exp,
                                         scale=float(DK) ** -0.5).then_inc(e_read, 1)
                            if u == 2 and h == 1 and not (last and g == NG - 1):
                                keep_rows((g + 1) % NG, (g + 1) % 2, G + 2)
                            if u == 0 and h == 3 and not (first and g == 0):
                                keep_o((g - 1) % NG, G)

                bodies(act, step)
                keep_o(NG - 1, NG * B)

            @block.vector
            def _(vec):
                v = nc.vector
                set_keys(vec, v, 0)

                def reduce_pair(i, u, pair, group):
                    vec.wait_ge(s_ready, 8 * group + 2 * u + pair + 1)
                    if u == 0 and pair == 0 and not (isinstance(group, int) and group < 2):
                        vec.wait_ge(split_done, group - 1)
                    v.tensor_reduce(maxima[i][:, 2 * pair:2 * pair + 2, u:u + 1], psS[:, 2 * pair:2 * pair + 2, :], AX_X,
                                    ALU.max).then_inc(s_read, 1)

                def normalize(b, g, count):
                    vec.wait_ge(o_turned, count)
                    if not (isinstance(count, int) and count == 1):
                        vec.wait_ge(o_done, count - 1)
                    o = psO[g % 2].rearrange("p (q h w) -> p q h w", q=TPB, h=GROUP)
                    v.reciprocal(inv[:], o[:, :, :, DK]).then_inc(inv_ready, 1)
                    vec.wait_ge(inv_ready, count)
                    v.tensor_tensor(y_all[:, ds(b * TPB, TPB), g * GROUP * DK:(g + 1) * GROUP * DK].rearrange(
                        "p q (h d) -> p q h d", h=GROUP), o[:, :, :, 0:DK],
                        inv[:].unsqueeze(3).broadcast_to([P, TPB, GROUP, DK]), ALU.mult).then_inc(o_done, 1)

                for i in range(2):
                    for u in range(TPB):
                        for pair in range(2):
                            reduce_pair(i, u, pair, i)

                def step(b, g, first, last):
                    G = NG * b + g
                    for u in range(TPB):
                        if u == 1 and not (first and g == 0):
                            bb, gg = (b, g - 1) if g else (b - 1, NG - 1)
                            normalize(bb, gg, G)
                        if not (last and g >= NG - 2):
                            for pair in range(2):
                                reduce_pair(g % 2, u, pair, G + 2)
                bodies(vec, step)
                normalize(B - 1, NG - 1, NG * B)


def project_phase(nc, ps, s, x_all, z_all, y_all, logits):
    with Phase(nc) as ctx:
        def sb(name, shape, dt=F32):
            return ctx.enter_context(nc.sbuf_tensor(own(nc, name), shape, dt))

        def sem(name):
            return ctx.semaphore(name)

        def sbs(name, shape, dt=F32):
            return [sb(f"{name}{i}", shape, dt) for i in range(2)]

        ln = LayerNorm(nc, ctx, "ln2", ST, EPS, bufs=2)
        y_in, normed = sbs("y_in", [P, ST, P]), sbs("normed", [P, ST, P])
        yT, h2T, x1 = sbs("yT", [P, SW]), sbs("h2T", [P, SW]), sb("x1", [P, ST, P])
        y_loaded, norm_stored = [sem("y_loaded0"), sem("y_loaded1")], [sem("norm_stored0"), sem("norm_stored1")]
        y_turned, y_kept, projected, x1_ready, halved = (
            sem("y_turned"), sem("y_kept"), sem("projected"), sem("x1_ready"), sem("halved"))
        h_turned, h_kept, gated, logits_kept = sem("h_turned"), sem("h_kept"), sem("gated"), sem("logits_kept")
        psY, psP, psH = ([ps[:, 2 * m + i, :] for i in range(2)] for m in range(3))
        psL = [ps[:, 6 + i, 0:ST * E] for i in range(2)]

        with nc.Block() as block:
            @block.sync
            def _(sp):
                def step(j, i, present):
                    o = 1 - i
                    if present(0):
                        after(sp, y_turned, j, 2)
                        sp.dma_start(y_in[i][:], y_all[:, ds(j * ST, ST), :]).then_inc(y_loaded[i], 16)
                    if present(2):
                        ln.wait_done(sp, j - 2)
                        sp.dma_start(y_all[:, ds((j - 2) * ST, ST), :], normed[i][:]).then_inc(norm_stored[i], 16)

                pipeline(sp, SL, 2, step)
                for i in range(2):
                    sp.wait_ge(norm_stored[i], 16 * SL // 2)

            @block.tensor
            def _(pe):
                t = nc.tensor

                def step(j, i, present):
                    o = 1 - i
                    if present(1):
                        after(pe, y_kept, j, 1)
                        after(pe, x1_ready, j, 3)
                        for q in range(ST):
                            last = t.matmul(psP[o][:, q * P:(q + 1) * P], yT[o][:, q * P:(q + 1) * P], s["w_proj"][:],
                                            start=True, stop=True)
                        last.then_inc(projected, 1)
                    if present(0):
                        after_same_parity(pe, y_loaded[i], j, i)
                        after(pe, y_kept, j, 2)
                        for q in range(ST):
                            last = t.transpose(psY[i][:, q * P:(q + 1) * P], y_in[i][:, q, :], s["ident"][:])
                        last.then_inc(y_turned, 1)
                    if present(3):
                        after(pe, h_kept, j, 3)
                        after(pe, logits_kept, j, 5)
                        for q in range(ST):
                            last = t.matmul(psL[o][:, q * E:(q + 1) * E], h2T[o][:, q * P:(q + 1) * P], s["gate_w"][:],
                                            start=True, stop=True)
                        last.then_inc(gated, 1)
                    if present(2):
                        ln.wait_done(pe, j - 2)
                        after(pe, h_kept, j, 4)
                        for q in range(ST):
                            last = t.transpose(psH[i][:, q * P:(q + 1) * P], normed[i][:, q, :], s["ident"][:])
                        last.then_inc(h_turned, 1)

                pipeline(pe, SL, 3, step)

            @block.scalar
            def _(act):
                a = nc.scalar

                def step(j, i, present):
                    o = 1 - i
                    if present(0):
                        after(act, y_turned, j)
                        after(act, projected, j, 2)
                        a.activation(yT[i][:], psY[i], ACT.Copy).then_inc(y_kept, 1)
                    if present(1):
                        ln.squares(act, j - 1, o)
                    if present(2):
                        after(act, h_turned, j, 2)
                        after(act, gated, j, 4)
                        a.activation(h2T[i][:], psH[i], ACT.Identity, bias=s["ln2_b"][:, 0:1],
                                     scale=s["ln2_w"][:, 0:1]).then_inc(h_kept, 1)

                pipeline(act, SL, 2, step)

            @block.vector
            def _(vec):
                v = nc.vector

                def step(j, i, present):
                    o = 1 - i
                    if present(1):
                        here = ds((j - 1) * ST, ST)
                        after(vec, projected, j, 1)
                        after(vec, halved, j, 2)
                        v.tensor_tensor(x1[:], z_all[:, here, :], psP[o].rearrange("p (t c) -> p t c", c=P),
                                        ALU.add).then_inc(x1_ready, 1)
                        after(vec, x1_ready, j, 1)
                        ln.center(vec, j - 1, x1[:], o)
                        v.scalar_tensor_tensor(x_all[:, here, :], x1[:], 0.5, x_all[:, here, :], ALU.mult,
                                               ALU.add).then_inc(halved, 1)
                    if present(3):
                        after(vec, gated, j, 3)
                        v.tensor_tensor(logits[:, ds((j - 3) * ST, ST), :], psL[o].rearrange("p (t e) -> p t e", e=E),
                                        s["gate_b"][:].unsqueeze(1).broadcast_to([P, ST, E]),
                                        ALU.add).then_inc(logits_kept, 1)
                    if present(1):
                        ln.variance(vec, j - 1, o)

                pipeline(vec, SL, 3, step)
                vec.wait_ge(logits_kept, SL)
                vec.wait_ge(halved, SL)

            @block.gpsimd
            def _(pool):
                def step(j, i, present):
                    o = 1 - i
                    if present(1):
                        free = [] if isinstance(j, int) and j < 3 else [(norm_stored[o], 8 * (j - 1 - o)), (h_turned, j - 2)]
                        ln.scale(pool, j - 1, normed[o][:], o, *free)

                ln.start(pool)
                pipeline(pool, SL, 1, step)


def route_phase(nc, ps, s, rows, logits, slot, expert, xs):
    with Phase(nc) as ctx:
        def sb(name, shape, dt=F32):
            return ctx.enter_context(nc.sbuf_tensor(own(nc, name), shape, dt))

        def sem(name):
            return ctx.semaphore(name)

        best, first = sb("best", [P, NT]), sb("first", [P, NT])
        equal, one_hot = sb("equal", [P, NT, E]), sb("one_hot", [P, NT, E])
        tile_count, running = sb("tile_count", [P, E, NT]), sb("running", [P, E, NT])
        tiles, tiles_end, base = sb("tiles", [P, E]), sb("tiles_end", [P, E]), sb("base", [P, E])
        place, slot_f, over = sb("place", [P, NT, E]), sb("slot_f", [P, NT]), sb("over", [P, SLOTS, E])
        expert_f = sb("expert_f", [P, SLOTS])
        step, one_hot_ready, ranked, slots_ready, scattered, numbered = (
            sem("step"), sem("one_hot_ready"), sem("ranked"), sem("slots_ready"), sem("scattered"), sem("numbered"))
        rank = ps[:, 0, 0:NT * E]
        count = ps[:, 0, NT * E:2 * NT * E]
        c = s["counts"]

        with nc.Block() as block:
            @block.vector
            def _(vec):
                v = nc.vector
                v.tensor_copy(rows[:, :, P:], s["token"][:].unsqueeze(2)).then_inc(numbered, 1)
                done = [0]

                def link(ins):
                    done[0] += 1
                    ins.then_inc(step, 1)
                    vec.wait_ge(step, done[0])

                experts = c[:, 0:E].unsqueeze(1)
                link(v.tensor_reduce(best[:], logits[:], AX_X, ALU.max))
                link(v.tensor_tensor(equal[:], logits[:], best[:].unsqueeze(2).broadcast_to([P, NT, E]), ALU.is_equal))
                link(v.tensor_scalar(over[:, 0, :], c[:, 0:E], float(E), None, ALU.subtract))
                link(v.tensor_tensor(equal[:], equal[:], over[:, 0:1, :].broadcast_to([P, NT, E]), ALU.mult))
                link(v.tensor_reduce(first[:], equal[:], AX_X, ALU.min))
                link(v.tensor_tensor(one_hot[:], over[:, 0:1, :].broadcast_to([P, NT, E]),
                                     first[:].unsqueeze(2).broadcast_to([P, NT, E]), ALU.is_equal))
                link(v.tensor_copy(base[:], c[:, 0:E]))
                v.tensor_copy(slot_f[:], first[:]).then_inc(one_hot_ready, 1)
                vec.wait_ge(ranked, 1)
                link(v.tensor_copy(tile_count[:], count.rearrange("p (t e) -> p e t", e=E)))
                link(v.tensor_tensor_scan(running[:].rearrange("p e t -> p (e t)"), s["restart"][:],
                                          tile_count[:].rearrange("p e t -> p (e t)"), 0.0, ALU.mult, ALU.add))
                link(v.tensor_scalar(place[:, :, 0], c[:, 0:NT], float(P), None, ALU.mult))
                total = running[:, :, NT - 1]
                above = equal[:].rearrange("p t e -> p (t e)").rearrange("p (e t) -> p e t", e=E)
                link(v.tensor_tensor(above, total.unsqueeze(2).broadcast_to([P, E, NT]),
                                     place[:, :, 0].unsqueeze(1).broadcast_to([P, E, NT]), ALU.is_gt))
                link(v.tensor_reduce(tiles[:], above, AX_X, ALU.add))
                link(v.tensor_tensor_scan(tiles_end[:], s["ones"][:, 0:E], tiles[:], 0.0, ALU.mult, ALU.add))
                link(v.tensor_tensor(base[:], tiles_end[:], tiles[:], ALU.subtract))
                link(v.tensor_tensor(running[:], running[:], tile_count[:], ALU.subtract))
                link(v.tensor_tensor(place[:], running[:].rearrange("p e t -> p t e"),
                                     rank.rearrange("p (t e) -> p t e", e=E), ALU.add))
                link(v.tensor_scalar(base[:], base[:], float(P), None, ALU.mult))
                link(v.tensor_tensor(place[:], place[:], base[:].unsqueeze(1).broadcast_to([P, NT, E]), ALU.add))
                link(v.tensor_tensor(place[:], place[:], one_hot[:], ALU.mult))
                link(v.tensor_reduce(slot_f[:], place[:], AX_X, ALU.add))
                link(v.tensor_copy(slot[:], slot_f[:]))
                link(v.tensor_tensor(over[:], c[:, 0:SLOTS].unsqueeze(2).broadcast_to([P, SLOTS, E]),
                                     tiles_end[:].unsqueeze(1).broadcast_to([P, SLOTS, E]), ALU.is_ge))
                link(v.tensor_reduce(expert_f[:], over[:], AX_X, ALU.add))
                link(v.tensor_scalar(expert_f[:], expert_f[:], float(E - 1), None, ALU.min))
                v.tensor_copy(expert[:], expert_f[:]).then_inc(slots_ready, 1)

            @block.tensor
            def _(pe):
                t = nc.tensor
                hot = one_hot[:].rearrange("p t e -> p (t e)")
                pe.wait_ge(one_hot_ready, 1)
                t.matmul(rank, s["below"][:], hot, start=True, stop=True)
                t.matmul(count, s["ones"][:], hot, start=True, stop=True).then_inc(ranked, 1)

            @block.gpsimd
            def _(pool):
                pool.wait_ge(slots_ready, 1)
                pool.wait_ge(numbered, 1)
                for i in range(NT):
                    pool.indirect_dma_start(xs, bass.IndirectOffsetOnAxis(ap=slot[:, i:i + 1], axis=0),
                                            rows[:, i, :], None).then_inc(scattered, 16)
                pool.wait_ge(scattered, 16 * NT)


def expert_phase(nc, ps, s, expert, xs, ys):
    with Phase(nc) as ctx:
        def sb(name, shape, dt=F32):
            return [ctx.enter_context(nc.sbuf_tensor(own(nc, f"{name}{i}"), shape, dt)) for i in range(2)]

        def sem(name):
            return ctx.semaphore(name)

        xT, hid, hidT = sb("xT", [P, P]), sb("hid", [P, HID]), sb("hidT", [P, HID])
        x_turned, xT_kept = sem("x_turned"), sem("xT_kept")
        first_done, hid_kept, hid_turned, hidT_kept = (
            sem("first_done"), sem("hid_kept"), sem("hid_turned"), sem("hidT_kept"))
        xt = [ctx.enter_context(nc.sbuf_tensor(own(nc, f"xt{i}"), [P, P + 1], F32)) for i in range(RING)]
        x_loaded = [sem(f"x_loaded{i}") for i in range(RING)]
        yt = [ctx.enter_context(nc.sbuf_tensor(own(nc, f"yt{i}"), [P, P], F32)) for i in range(RING)]
        number = [ctx.enter_context(nc.sbuf_tensor(own(nc, f"number{i}"), [P, 1], I32)) for i in range(RING)]
        passed, numbered = sem("passed"), sem("numbered")
        second_done, y_kept, y_stored = sem("second_done"), sem("y_kept"), [sem(f"y_stored{i}") for i in range(RING)]
        psX, psH, psT, psY = ([ps[:, 2 * k + i, :] for i in range(2)] for k in range(4))

        with nc.Block() as block:
            @block.sync
            def _(sp):
                def load(j, i):
                    sp.dma_start(xt[i][:], xs[ds(j * P, P), :]).then_inc(x_loaded[i], 16)

                for j in range(RING):
                    load(j, j)
                with sp.Fori(1, SLOTS // RING) as turn:
                    for i in range(RING):
                        sp.wait_ge(x_turned, RING * (turn - 1) + i + 1)
                        sp.wait_ge(numbered, RING * (turn - 1) + i + 1)
                        load(RING * turn + i, i)

            @block.tensor
            def _(pe):
                t = nc.tensor

                def weights_of(j):
                    return pe.value_load(expert[0:1, ds(j, 1)], min_val=0, max_val=E - 1)

                def step(j, i, present):
                    slot, i = i, i % 2
                    o = 1 - i
                    first_expert = weights_of(j - 1) if present(1) else None
                    second_expert = weights_of(j - 3) if present(3) else None
                    if present(0):
                        pe.wait_ge(x_loaded[slot], (16 // RING) * (j - slot) + 16)
                        after(pe, xT_kept, j, 2)
                        t.transpose(psX[i][:, 0:P], xt[slot][:, 0:P], s["ident"][:]).then_inc(x_turned, 1)
                    if present(1):
                        after(pe, xT_kept, j, 1)
                        after(pe, hid_kept, j, 3)
                        t.matmul(psH[o], xT[o][:], s["w1"][:, ds(first_expert, 1), :], start=True, stop=True).then_inc(first_done, 1)
                    if present(2):
                        after(pe, hid_kept, j, 2)
                        after(pe, hidT_kept, j, 4)
                        for c in range(HC):
                            last = t.transpose(psT[i][:, c * P:(c + 1) * P], hid[i][:, c * P:(c + 1) * P], s["ident"][:])
                        last.then_inc(hid_turned, 1)
                    if present(3):
                        after(pe, hidT_kept, j, 3)
                        after(pe, y_kept, j, 5)
                        for c in range(HC):
                            last = t.matmul(psY[o][:, 0:P], hidT[o][:, c * P:(c + 1) * P], s["w2"][:, ds(second_expert, 1), c, :],
                                            start=(c == 0), stop=(c == HC - 1))
                        last.then_inc(second_done, 1)

                pipeline(pe, SLOTS, 3, step, unroll=RING)

            @block.scalar
            def _(act):
                a = nc.scalar

                def step(j, i, present):
                    i %= 2
                    o = 1 - i
                    if present(0):
                        after(act, x_turned, j, 0)
                        after(act, first_done, j, 2)
                        a.activation(xT[i][:], psX[i][:, 0:P], ACT.Identity, bias=s["ln2_b"][:, 0:1],
                                     scale=s["ln2_w"][:, 0:1]).then_inc(xT_kept, 1)
                    if present(1):
                        after(act, first_done, j, 1)
                        after(act, hid_turned, j, 3)
                        a.activation(hid[o][:], psH[o], ACT.Gelu_apprx_tanh).then_inc(hid_kept, 1)

                pipeline(act, SLOTS, 3, step, unroll=RING)

            @block.vector
            def _(vec):
                v = nc.vector

                def step(j, i, present):
                    out_slot = (i - 3) % RING
                    i %= 2
                    o = 1 - i
                    if present(2):
                        after(vec, hid_turned, j, 2)
                        after(vec, second_done, j, 4)
                        v.tensor_copy(hidT[i][:], psT[i]).then_inc(hidT_kept, 1)
                    if present(3):
                        after(vec, second_done, j, 3)
                        if not isinstance(j, int) or j >= 3 + RING:
                            vec.wait_ge(y_stored[out_slot], (16 // RING) * (j - 3 - out_slot))
                        v.tensor_copy(yt[out_slot][:], psY[o][:, 0:P]).then_inc(y_kept, 1)

                pipeline(vec, SLOTS, 3, step, unroll=RING)

            @block.gpsimd
            def _(pool):
                def step(j, slot, present):
                    out_slot = (slot - 3) % RING
                    if present(2):
                        tile, at = j - 2, (slot - 2) % RING
                        waits = [(x_loaded[at], (16 // RING) * (tile - at) + 16)]
                        if not isinstance(j, int) or tile >= RING:
                            waits.append((y_stored[at], (16 // RING) * (tile - at)))
                        wait_apart(pool, passed, *waits)
                        nc.gpsimd.tensor_copy(number[at][:], xt[at][:, P:]).then_inc(numbered, 1)
                    if present(3):
                        wait_apart(pool, passed, (y_kept, j - 2), (numbered, j - 2))
                        pool.indirect_dma_start(ys, bass.IndirectOffsetOnAxis(ap=number[out_slot][:], axis=0), yt[out_slot][:], None,
                                                bounds_check=TOK - 1, oob_is_err=False).then_inc(y_stored[out_slot], 16)

                pipeline(pool, SLOTS, 3, step, unroll=RING)
                for i in range(RING):
                    pool.wait_ge(y_stored[i], 16 * (SLOTS // RING))


def combine_phase(nc, x_all, y_all, ys, out):
    with Phase(nc) as ctx:
        y_loaded = [ctx.semaphore(f"y_loaded{j}") for j in range(SL)]
        added, stored = ctx.semaphore("added"), ctx.semaphore("stored")
        slices = [slice(j * ST, (j + 1) * ST) for j in range(SL)]
        with nc.Block() as block:
            @block.sync
            def _(sp):
                for j, here in enumerate(slices):
                    sp.dma_start(y_all[:, here, :], tiles_of(ys)[:, here, :]).then_inc(y_loaded[j], 16)

            @block.vector
            def _(vec):
                for j, here in enumerate(slices):
                    vec.wait_ge(y_loaded[j], 16)
                    nc.vector.scalar_tensor_tensor(x_all[:, here, :], y_all[:, here, :], 0.5, x_all[:, here, :],
                                                   ALU.mult, ALU.add).then_inc(added, 1)

            @block.scalar
            def _(act):
                for j, here in enumerate(slices):
                    act.wait_ge(added, j + 1)
                    act.dma_start(slices_of(out)[:, here, :], x_all[:, here, :]).then_inc(stored, 16)
                act.wait_ge(stored, 16 * SL)


def load_outputs(sp, y_all, ys, y_loaded):
    def step(j, i, present):
        here = ds(j * ST, ST)
        after_same_parity(sp, y_loaded[i], j, i, 2)
        sp.dma_start(y_all[:, here, :], tiles_of(ys)[:, here, :]).then_inc(y_loaded[i], 16)

    pipeline(sp, SL, 0, step)


class Signal:

    def __init__(self, nc, ctx, name, per=1):
        self.sem, self.per = ctx.semaphore(name), per

    def wait(self, eng, b, k=None):
        eng.wait_ge(self.sem, self.per * b + (self.per if k is None else k) + 1)

    def at(self, b, k=None):
        return self.sem, self.per * b + (self.per if k is None else k) + 1

    def free(self, eng, b):
        if not isinstance(b, int) or b > 0:
            self.wait(eng, b, 0)


F_W, F_K, F_V, F_R, F_G = range(5)
LORA = 32
NH, HS = 2, 64
BLOCK = 32
DIAG_LEVELS = 5
LEVELS = 7
GN_EPS = 1e-5 * NH


def turn_phase(nc, ps, s, x_all, y_all, ys, zT):
    with Phase(nc) as ctx:
        ln = LayerNorm(nc, ctx, "lnr", ST, EPS, bufs=2)
        normed = [ctx.enter_context(nc.sbuf_tensor(own(nc, f"r_normed{i}"), [P, ST, P], F32)) for i in range(2)]
        y_loaded = [ctx.semaphore(f"y_loaded{i}") for i in range(2)]
        added, turned, kept, zero = (ctx.semaphore(n) for n in ("added", "r_turned", "r_kept", "r_zero"))
        with nc.Block() as block:
            @block.sync
            def _(sp):
                load_outputs(sp, y_all, ys, y_loaded)

            @block.vector
            def _(vec):
                def step(j, i, present):
                    o = 1 - i
                    if present(0):
                        x = x_all[:, ds(j * ST, ST), :]
                        after_same_parity(vec, y_loaded[i], j, i)
                        nc.vector.scalar_tensor_tensor(x, y_all[:, ds(j * ST, ST), :], 0.5, x, ALU.mult,
                                                       ALU.add).then_inc(added, 1)
                        wait_apart(vec, ln.passed, (added, j + 1))
                        ln.center(vec, j, x, i)
                    if present(1):
                        after(vec, turned, j, 3)
                        ln.scale_on_vector(vec, j - 1, normed[o][:], o)
                    if present(0):
                        ln.variance(vec, j, i)

                pipeline(vec, SL, 1, step)

            @block.scalar
            def _(act):
                def step(j, i, present):
                    o = 1 - i
                    if present(0):
                        ln.squares(act, j, i)
                    if present(1):
                        after(act, turned, j, 1)
                        nc.scalar.activation(zT[:, ds(j - 1, 1), 1:], ps[:, o:o + 1, :], ACT.Copy).then_inc(kept, 1)

                pipeline(act, SL, 1, step)

            @block.gpsimd
            def _(pool):
                ln.start(pool)
                nc.gpsimd.memset(zT[:, :, 0:1], 0.0).then_inc(zero, 1)

                def step(j, i, present):
                    ln.power_(pool, j, i)

                pipeline(pool, SL, 0, step)

            @block.tensor
            def _(pe):
                def step(j, i, present):
                    if present(0):
                        ln.wait_done(pe, j)
                        after(pe, kept, j, 2)
                        for q in range(ST):
                            last = nc.tensor.transpose(ps[:, i, q * P:(q + 1) * P], normed[i][:, q, :], s["ident"][:])
                        last.then_inc(turned, 1)

                pipeline(pe, SL, 0, step)


def recurrence_phase(nc, ps, s, x_all, zT):
    with Phase(nc) as ctx:
        def sb(name, shape, dt=F32):
            return ctx.enter_context(nc.sbuf_tensor(own(nc, "r_" + name), shape, dt))

        def two(name, shape, dt=F32):
            return [sb(f"{name}{i}", shape, dt) for i in range(2)]

        def signal(name, per=1):
            x = Signal(nc, ctx, "r_" + name, per)
            signals.append(x)
            return x

        signals = []
        passed = {e: ctx.semaphore("r_passed_" + e) for e in ("vec", "pool", "pe")}
        dxa, xm, lora, lora4 = sb("dxa", [P, T]), sb("xm", [P, T]), sb("lora", [P, T]), sb("lora4", [LORA, T])
        shift, mixed = two("shift", [P, T]), [sb(f"mixed{f}", [P, T]) for f in range(5)]
        td_hidden, rate, gate_tanh = sb("td_hidden", [HS, T]), sb("rate", [P, T]), sb("gate_tanh", [P, T])
        q0, k0, ru, v_rows, decay, gate = (two("q0", [P, T]), two("k0", [P, T]), two("ru", [P, T]),
                                           two("v_rows", [P, TPB, P]), two("decay", [P, T]), two("gate", [P, T]))
        qx, kx = two("qx", [P, T]), two("kx", [P, T])
        block_decay = [sb(f"block_decay{l}", [P, T >> l]) for l in range(1, LEVELS + 1)]
        q_factor = [sb(f"q_factor{l}", [P, T >> (l + 1), 2]) for l in range(LEVELS)]
        k_factor = [sb(f"k_factor{l}", [P, T >> (l + 1), 2]) for l in range(LEVELS)]
        diag = sb("diag", [P, NH, TPB, BLOCK])
        aT = sb("aT", [P, NH, TPB, P])
        kT = sb("kT", [P, TPB, P])
        state = [sb(f"state{c}", [P, P]) for c in range(1, TPB)]
        gn = LayerNorm(nc, ctx, "gn", TPB * NH, GN_EPS, HS)
        yn, yg, ygT = sb("yn", [P, TPB, P]), sb("yg", [P, T]), sb("ygT", [P, T])

        dxa_ready, xm_ready, shift_ready = signal("dxa_ready"), signal("xm_ready"), signal("shift_ready", 5)
        lora_made, lora_kept, miu_made, mixed_ready = (
            signal("lora_made"), signal("lora_kept", 2), signal("miu_made", 5), signal("mixed_ready", 5))
        td_made, td_kept, w_made, rate_ready, decay_ready = (
            signal("td_made"), signal("td_kept"), signal("w_made"), signal("rate_ready"), signal("decay_ready"))
        k_made, r_made, v_made, g_made = signal("k_made"), signal("r_made"), signal("v_made"), signal("g_made")
        k_kept, r_kept, ru_kept, v_kept, gt_kept, g_kept = (
            signal("k_kept"), signal("r_kept"), signal("ru_kept"), signal("v_kept"), signal("gt_kept"), signal("g_kept"))
        factors, chain = signal("factors", LEVELS), signal("chain", LEVELS)
        q_next, k_next = signal("q_next", LEVELS), signal("k_next", LEVELS)
        level_made, level_kept = signal("level_made", DIAG_LEVELS + 1), signal("level_kept", DIAG_LEVELS + 1)
        far_made, far_kept, near_kept = signal("far_made", 2), signal("far_kept", 3), signal("near_kept", BLOCK // 8)
        kT_made, kT_kept, kv_made, state_step = (
            signal("kT_made"), signal("kT_kept"), signal("kv_made"), signal("state_step", 2 * (TPB - 1)))
        y_made, yn_turned, yg_ready, ygT_ready, out_made, x_added = (
            signal("y_made"), signal("yn_turned"), signal("yg_ready"), signal("ygT_ready"), signal("out_made"),
            signal("x_added"))

        def batches(eng, **parts):
            def run(b, i, *wanted):
                for kind, part in ORDER:
                    here = parts.get(f"{kind}_{part}")
                    if here is not None and kind in wanted:
                        here(*{"scan": (b, i), "mix": (b + 1, 1 - i), "tail": (b - 1, 1 - i), "next": (b + 2, i)}[kind])

            run(-2, 0, "next")
            run(-1, 1, "mix", "next")
            run(0, 0, "scan", "mix", "next")
            with eng.Fori(0, B // 2 - 2) as pair:
                run(2 * pair + 1, 1, "scan", "mix", "tail", "next")
                run(2 * pair + 2, 0, "scan", "mix", "tail", "next")
            run(B - 3, 1, "scan", "mix", "tail", "next")
            run(B - 2, 0, "scan", "mix", "tail")
            run(B - 1, 1, "scan", "tail")
            run(B, 0, "tail")

        started, halved = ctx.semaphore("r_started"), ctx.semaphore("r_halved")
        with nc.Block() as block:
            @block.gpsimd
            def _(pool):
                g = nc.gpsimd
                gn.start(pool)
                for x in signals:
                    pool.sem_inc(x.sem, 1)
                n = 0
                for x, value in ([(diag, 0.0), (aT, 0.0)] + [(x, 0.0) for x in state]
                                 + [(x, 1.0) for x in q_factor + k_factor]):
                    g.memset(x[:], value).then_inc(started, 1)
                    n += 1
                pool.wait_ge(started, n)

            @block.vector
            def _(vec):
                nc.vector.tensor_scalar(s["gn_w_half"][:], s["gn_w"][:], 0.5, None, ALU.mult).then_inc(halved, 1)
                nc.vector.tensor_scalar(s["gn_b_half"][:], s["gn_b"][:], 0.5, None, ALU.mult).then_inc(halved, 1)
                vec.wait_ge(halved, 2)

        with nc.Block() as block:
            @block.vector
            def _(vec):
                v = nc.vector

                def next_xm(b, i):
                    x = zT[:, ds(b, 1), 1:].rearrange("p a t -> p (a t)")
                    before = zT[:, ds(b, 1), 0:T].rearrange("p a t -> p (a t)")
                    shift_ready.free(vec, b)
                    v.tensor_tensor(dxa[:], before, x, ALU.subtract).then_inc(dxa_ready.sem, 1)
                    dxa_ready.wait(vec, b)
                    lora_made.free(vec, b)
                    v.scalar_tensor_tensor(xm[:], dxa[:], s["miu_x"][:, 0:1], x, ALU.mult, ALU.add).then_inc(xm_ready.sem, 1)

                def mix_shift(f):
                    def part(b, i):
                        miu_made.wait(vec, b, f + 1)
                        if f >= 2:
                            mixed_ready.wait(vec, b, f - 1)
                        else:
                            mixed_ready.free(vec, b)
                        v.scalar_tensor_tensor(shift[f % 2][:], ps[:, MIU_BANK[f], :], s["lambda"][:, f:f + 1], dxa[:],
                                               ALU.add, ALU.mult).then_inc(shift_ready.sem, 1)
                    return part

                def mix_r(b, i):
                    r_kept.wait(vec, b)
                    if not isinstance(b, int) or b >= 2:
                        level_made.free(vec, b - 1)
                    v.tensor_scalar(ru[i][:], q0[i][:], s["u"][:, 0:1], None, ALU.mult).then_inc(ru_kept.sem, 1)

                def mix_g(b, i):
                    gt_kept.wait(vec, b)
                    if not isinstance(b, int) or b >= 2:
                        ygT_ready.free(vec, b - 1)
                    v.scalar_tensor_tensor(gate[i][:], gate_tanh[:], 1.0, ps[:, G_BANK, :], ALU.add,
                                           ALU.mult).then_inc(g_kept.sem, 1)

                def mix_chain(b, i):
                    decay_ready.wait(vec, b)
                    for l in range(LEVELS):
                        src = decay[i] if l == 0 else block_decay[l - 1]
                        pairs = src[:].rearrange("p (n two) -> p n two", two=2)
                        if l:
                            chain.wait(vec, b, l)
                        else:
                            factors.free(vec, b)
                            state_step.free(vec, b)
                        v.tensor_tensor(block_decay[l][:], pairs[:, :, 0], pairs[:, :, 1], ALU.mult).then_inc(chain.sem, 1)

                def scan_start(b, i):
                    keep_level(b, 0)
                    next_q(b, i, 0)

                def next_q(b, i, l):
                    src = q0[i] if l == 0 else qx[l % 2]
                    dst = qx[(l + 1) % 2]
                    factors.wait(vec, b, l + 1)
                    if l == 0:
                        r_kept.wait(vec, b)
                        y_made.free(vec, b)
                        q_next.free(vec, b)
                    else:
                        q_next.wait(vec, b, l)
                        if l <= DIAG_LEVELS:
                            level_made.wait(vec, b, l + 1)
                        else:
                            far_made.wait(vec, b, 1)
                    m = 1 << l
                    v.tensor_tensor(dst[:].rearrange("p (k m) -> p k m", m=m), src[:].rearrange("p (k m) -> p k m", m=m),
                                    q_factor[l][:].rearrange("p n two -> p (n two)").unsqueeze(2).broadcast_to([P, T // m, m]),
                                    ALU.mult).then_inc(q_next.sem, 1)

                def scan_level(l):
                    def part(b, i):
                        keep_level(b, l)
                        next_q(b, i, l)
                    return part

                def scan_far(b, i):
                    next_q(b, i, DIAG_LEVELS + 1)

                def scan_state(b, i):
                    kv_made.wait(vec, b)
                    for c in range(1, TPB):
                        for h in range(NH):
                            at = slice(h * HS, (h + 1) * HS)
                            kv = ps[at, KV_BANK, (c - 1) * P + h * HS:(c - 1) * P + (h + 1) * HS]
                            n = 2 * (c - 1) + h
                            if c == 1:
                                v.tensor_copy(state[0][at, at], kv).then_inc(state_step.sem, 1)
                            else:
                                state_step.wait(vec, b, n - 1)
                                v.scalar_tensor_tensor(state[c - 1][at, at], state[c - 2][at, at],
                                                       block_decay[LEVELS - 1][at, c - 1:c], kv, ALU.mult,
                                                       ALU.add).then_inc(state_step.sem, 1)

                def scan_y(b, i):
                    y_made.wait(vec, b)
                    gn.center(vec, b, ps[:, Y_BANK, :].rearrange("p (n w) -> p n w", w=HS))

                def tail_norm(b, i):
                    gn.variance(vec, b)

                def tail_turn(b, i):
                    yn_turned.wait(vec, b)
                    ygT_ready.free(vec, b)
                    v.tensor_scalar(yg[:], ps[:, YT_BANK, :], s["gn_w_half"][:, 0:1], s["gn_b_half"][:, 0:1], ALU.mult,
                                    ALU.add).then_inc(yg_ready.sem, 1)
                    yg_ready.wait(vec, b)
                    out_made.free(vec, b)
                    v.tensor_tensor(ygT[:], yg[:], gate[i][:], ALU.mult).then_inc(ygT_ready.sem, 1)

                def tail_out(b, i):
                    out_made.wait(vec, b)
                    here = x_all[:, ds(b * TPB, TPB), :]
                    v.tensor_tensor(here, here, ps[:, OUT_BANK, :].rearrange("p (t c) -> p t c", c=P),
                                    ALU.add).then_inc(x_added.sem, 1)

                def keep_level(b, l):
                    wait_apart(vec, passed["vec"], level_made.at(b, l + 1), level_kept.at(b, l), near_kept.at(b, 0))
                    v.copy_predicated(diag[:], s["level_masks"][:, l, :].unsqueeze(1).unsqueeze(1).broadcast_to([P, NH, TPB, BLOCK]),
                                      ps[:, LEVEL_BANK:LEVEL_BANK + NH, 0:TPB * BLOCK].rearrange("p h (c w) -> p h c w", c=TPB)
                                      ).then_inc(level_kept.sem, 1)

                batches(vec, next_xm=next_xm, **{f"mix_shift{f}": mix_shift(f) for f in range(5)}, mix_r=mix_r,
                        mix_g=mix_g, mix_chain=mix_chain, scan_start=scan_start, **{f"scan_level{l}": scan_level(l) for l in range(1, DIAG_LEVELS + 1)},
                        scan_far=scan_far, scan_state=scan_state, scan_y=scan_y,
                        tail_norm=tail_norm, tail_turn=tail_turn, tail_out=tail_out)
                x_added.wait(vec, B - 1)

            @block.gpsimd
            def _(pool):
                g = nc.gpsimd

                users = (td_made, k_made, v_made, r_made, g_made)

                def mix_mixed(f):
                    def part(b, i):
                        x = zT[:, ds(b, 1), 1:].rearrange("p a t -> p (a t)")
                        wait_apart(pool, passed["pool"], shift_ready.at(b, f + 1), users[f].at(b, 0))
                        g.tensor_tensor(mixed[f][:], shift[f % 2][:], x, ALU.add).then_inc(mixed_ready.sem, 1)
                    return part

                def next_k(b, i, l):
                    src = k0[i] if l == 0 else kx[l % 2]
                    dst = kx[(l + 1) % 2]
                    factors.wait(pool, b, l + 1)
                    if l == 0:
                        k_kept.wait(pool, b)
                        kT_made.free(pool, b)
                    else:
                        k_next.wait(pool, b, l)
                        if l <= DIAG_LEVELS:
                            level_made.wait(pool, b, l + 1)
                        else:
                            far_made.wait(pool, b, 1)
                    m = 1 << l
                    g.tensor_tensor(dst[:].rearrange("p (k m) -> p k m", m=m), src[:].rearrange("p (k m) -> p k m", m=m),
                                    k_factor[l][:].rearrange("p n two -> p (n two)").unsqueeze(2).broadcast_to([P, T // m, m]),
                                    ALU.mult).then_inc(k_next.sem, 1)

                def scan_level(l):
                    return lambda b, i: next_k(b, i, l)

                def scan_far(b, i):
                    next_k(b, i, DIAG_LEVELS + 1)

                def tail_norm(b, i):
                    gn.scale(pool, b, yn[:].rearrange("p c (h w) -> p (c h) w", w=HS))

                batches(pool, **{f"mix_mixed{f}": mix_mixed(f) for f in range(5)}, mix_first_k=scan_level(0),
                        **{f"scan_level{l}": scan_level(l) for l in range(1, DIAG_LEVELS + 1)}, scan_far=scan_far,
                        tail_norm=tail_norm)

            @block.scalar
            def _(act):
                a = nc.scalar

                def mix_lora(b, i):
                    lora_made.wait(act, b)
                    miu_made.free(act, b)
                    a.activation(lora[:], ps[:, 0, :], ACT.Tanh).then_inc(lora_kept.sem, 1)
                    a.activation(lora4[:], ps[0:LORA, 1, :], ACT.Tanh).then_inc(lora_kept.sem, 1)

                def mix_td(b, i):
                    td_made.wait(act, b)
                    w_made.free(act, b)
                    a.activation(td_hidden[:], ps[0:HS, TD_BANK, :], ACT.Tanh).then_inc(td_kept.sem, 1)

                def mix_rate(b, i):
                    w_made.wait(act, b)
                    decay_ready.free(act, b)
                    a.activation(rate[:], ps[:, W_BANK, :], ACT.Exp, bias=s["td_miu"][:, 0:1]).then_inc(rate_ready.sem, 1)
                    rate_ready.wait(act, b)
                    if not isinstance(b, int) or b >= 2:
                        factors.free(act, b - 1)
                        chain.free(act, b - 1)
                    a.activation(decay[i][:], rate[:], ACT.Exp, scale=-1.0).then_inc(decay_ready.sem, 1)

                def mix_k(b, i):
                    k_made.wait(act, b)
                    if not isinstance(b, int) or b >= 2:
                        level_made.free(act, b - 1)
                        k_next.free(act, b - 1)
                        q_next.free(act, b - 1)
                        y_made.free(act, b - 1)
                    a.activation(k0[i][:], ps[:, K_BANK, :], ACT.Copy).then_inc(k_kept.sem, 1)

                def mix_v(b, i):
                    v_made.wait(act, b)
                    a.activation(v_rows[i][:].rearrange("p c w -> p (c w)"), ps[:, V_BANK, :], ACT.Copy).then_inc(v_kept.sem, 1)

                def mix_r(b, i):
                    r_made.wait(act, b)
                    a.activation(q0[i][:], ps[:, R_BANK, :], ACT.Copy).then_inc(r_kept.sem, 1)

                def mix_g(b, i):
                    g_made.wait(act, b)
                    g_kept.free(act, b)
                    a.activation(gate_tanh[:], ps[:, G_BANK, :], ACT.Tanh, scale=0.5).then_inc(gt_kept.sem, 1)

                def mix_chain(b, i):
                    for l in range(LEVELS):
                        src = decay[i] if l == 0 else block_decay[l - 1]
                        pairs = src[:].rearrange("p (n two) -> p n two", two=2)
                        if l:
                            chain.wait(act, b, l)
                        else:
                            decay_ready.wait(act, b)
                            q_next.free(act, b)
                            k_next.free(act, b)
                        a.activation(q_factor[l][:, :, 1], pairs[:, :, 0], ACT.Copy)
                        a.activation(k_factor[l][:, :, 0], pairs[:, :, 1], ACT.Copy).then_inc(factors.sem, 1)

                def scan_keys(b, i):
                    kT_made.wait(act, b)
                    kv_made.free(act, b)
                    a.activation(kT[:].rearrange("p c w -> p (c w)"), ps[:, KT_BANK, :], ACT.Copy).then_inc(kT_kept.sem, 1)
                    far_made.wait(act, b)
                    y_made.free(act, b)
                    bank = LEVEL_BANK
                    far = ps[:, bank:bank + NH, :].rearrange("p h (c t) -> p h c t", c=TPB)
                    for at, to in ((slice(0, 32), slice(32, 64)), (slice(64, 96), slice(96, 128)), (slice(0, 64), slice(64, 128))):
                        a.activation(aT[at, :, :, to], far[at, :, :, to], ACT.Copy).then_inc(far_kept.sem, 1)
                    level_kept.wait(act, b)
                    for q in range(P // BLOCK):
                        at = slice(q * BLOCK, (q + 1) * BLOCK)
                        a.activation(aT[at, :, :, at], diag[at, :, :, :], ACT.Copy).then_inc(near_kept.sem, 1)

                def scan_y(b, i):
                    gn.squares(act, b)

                batches(act, mix_lora=mix_lora, mix_td=mix_td, mix_rate=mix_rate, mix_k=mix_k, mix_v=mix_v, mix_r=mix_r,
                        mix_g=mix_g, mix_chain=mix_chain, scan_keys=scan_keys, scan_y=scan_y)

            @block.tensor
            def _(pe):
                t = nc.tensor

                def project(b, bank, weights, f, made, rows=P):
                    mixed_ready.wait(pe, b, f + 1)
                    t.matmul(ps[0:rows, bank, :], weights, mixed[f][:], start=True, stop=True).then_inc(made.sem, 1)

                def mix_lora(b, i):
                    xm_ready.wait(pe, b)
                    g_kept.free(pe, b)
                    shift_ready.free(pe, b)
                    t.matmul(ps[:, 0, :], s["A_lora"][:, 0:P], xm[:], start=True, stop=True)
                    k_kept.free(pe, b)
                    t.matmul(ps[0:LORA, 1, :], s["A_lora"][:, P:], xm[:], start=True, stop=True).then_inc(lora_made.sem, 1)

                def mix_shift(f):
                    def part(b, i):
                        if f == 0:
                            lora_kept.wait(pe, b)
                            r_kept.free(pe, b)
                            ru_kept.free(pe, b)
                        elif f == 1:
                            v_kept.free(pe, b)
                        elif f == 4:
                            shift_ready.wait(pe, b, 1)
                        if f == 4:
                            lhsT, rhs = s["B_lora4"][:], lora4[:]
                        else:
                            lhsT, rhs = s["B_lora"][:, f, :], lora[:]
                        t.matmul(ps[:, MIU_BANK[f], :], lhsT, rhs, start=True, stop=True).then_inc(miu_made.sem, 1)
                    return part

                def mix_td(b, i):
                    shift_ready.wait(pe, b, F_K + 1)
                    project(b, TD_BANK, s["td_A"][:], F_W, td_made, HS)

                def mix_rate(b, i):
                    td_kept.wait(pe, b)
                    shift_ready.wait(pe, b, F_V + 1)
                    t.matmul(ps[:, W_BANK, :], s["td_B"][:], td_hidden[:], start=True, stop=True).then_inc(w_made.sem, 1)

                def mix_k(b, i):
                    shift_ready.wait(pe, b, F_R + 1)
                    project(b, K_BANK, s["WkT"][:], F_K, k_made)

                def mix_v(b, i):
                    mixed_ready.wait(pe, b, F_V + 1)
                    for c in range(TPB):
                        last = t.matmul(ps[:, V_BANK, c * P:(c + 1) * P], mixed[F_V][:, c * P:(c + 1) * P], s["WvT"][:],
                                        start=True, stop=True)
                    last.then_inc(v_made.sem, 1)

                def mix_r(b, i):
                    shift_ready.wait(pe, b, F_G + 1)
                    project(b, R_BANK, s["WrT"][:], F_R, r_made)

                def mix_g(b, i):
                    rate_ready.wait(pe, b)
                    project(b, G_BANK, s["WgT"][:], F_G, g_made)

                def level(b, i, l):
                    if l == 0:
                        needs = [ru_kept.at(b), k_kept.at(b)]
                        q, k = ru[i], k0[i]
                    elif l == 1:
                        needs = [r_kept.at(b), level_kept.at(b, 1)]
                        q, k = q0[i], k0[i]
                    else:
                        needs = [q_next.at(b, l - 1), k_next.at(b, l - 1), level_kept.at(b, l)]
                        q, k = qx[(l - 1) % 2], kx[(l - 1) % 2]
                    wait_apart(pe, passed["pe"], *needs)
                    for c in range(TPB):
                        for block_ in range(P // BLOCK):
                            for h in range(NH):
                                at = slice(h * HS, (h + 1) * HS)
                                tok = slice(c * P + block_ * BLOCK, c * P + (block_ + 1) * BLOCK)
                                last = t.matmul(ps[block_ * BLOCK:(block_ + 1) * BLOCK, LEVEL_BANK + h, c * BLOCK:(c + 1) * BLOCK],
                                                k[at, tok], q[at, tok], start=True, stop=True)
                    last.then_inc(level_made.sem, 1)

                def scan_start(b, i):
                    level(b, i, 0)

                def scan_level(l):
                    return lambda b, i: level(b, i, l)

                def scan_far(b, i):
                    bank = LEVEL_BANK
                    for half in (BLOCK, 2 * BLOCK):
                        l = 5 if half == BLOCK else 6
                        wait_apart(pe, passed["pe"], q_next.at(b, l), k_next.at(b, l), level_kept.at(b))
                        q, k = qx[l % 2], kx[l % 2]
                        for c in range(TPB):
                            for first in range(0, P, 2 * half):
                                for h in range(NH):
                                    at = slice(h * HS, (h + 1) * HS)
                                    last = t.matmul(ps[first:first + half, bank + h, c * P + first + half:c * P + first + 2 * half],
                                                    k[at, c * P + first:c * P + first + half],
                                                    q[at, c * P + first + half:c * P + first + 2 * half],
                                                    start=True, stop=True)
                        last.then_inc(far_made.sem, 1)

                def scan_keys(b, i):
                    k_next.wait(pe, b, LEVELS)
                    x_added.free(pe, b)
                    for c in range(TPB):
                        last = t.transpose(ps[:, KT_BANK, c * P:(c + 1) * P], kx[LEVELS % 2][:, c * P:(c + 1) * P], s["ident"][:])
                    last.then_inc(kT_made.sem, 1)

                def scan_state(b, i):
                    kT_kept.wait(pe, b)
                    v_kept.wait(pe, b)
                    yg_ready.free(pe, b)
                    for c in range(TPB - 1):
                        last = t.matmul(ps[:, KV_BANK, c * P:(c + 1) * P], kT[:, c, :], v_rows[i][:, c, :], start=True, stop=True)
                    last.then_inc(kv_made.sem, 1)

                def scan_y(b, i):
                    far_kept.wait(pe, b)
                    near_kept.wait(pe, b)
                    q_next.wait(pe, b, LEVELS)
                    for c in range(TPB):
                        to = c * P
                        if c:
                            state_step.wait(pe, b, 2 * c)
                            t.matmul(ps[:, Y_BANK, to:to + P], qx[LEVELS % 2][:, to:to + P], state[c - 1][:], start=True, stop=False)
                        for h in range(NH):
                            last = t.matmul(ps[:, Y_BANK, to + h * HS:to + (h + 1) * HS], aT[:, h, c, :],
                                            v_rows[i][:, c, h * HS:(h + 1) * HS], start=(c == 0), stop=(c == 0 or h == NH - 1))
                    last.then_inc(y_made.sem, 1)

                def tail_turn(b, i):
                    gn.wait_done(pe, b)
                    for c in range(TPB):
                        last = t.transpose(ps[:, YT_BANK, c * P:(c + 1) * P], yn[:, c, :], s["ident"][:])
                    last.then_inc(yn_turned.sem, 1)

                def tail_out(b, i):
                    ygT_ready.wait(pe, b)
                    for c in range(TPB):
                        last = t.matmul(ps[:, OUT_BANK, c * P:(c + 1) * P], ygT[:, c * P:(c + 1) * P], s["WoT"][:],
                                        start=True, stop=True)
                    last.then_inc(out_made.sem, 1)

                batches(pe, mix_lora=mix_lora, **{f"mix_shift{f}": mix_shift(f) for f in range(5)}, mix_td=mix_td,
                        mix_rate=mix_rate, mix_k=mix_k, mix_v=mix_v, mix_r=mix_r, mix_g=mix_g,
                        scan_start=scan_start, **{f"scan_level{l}": scan_level(l) for l in range(1, DIAG_LEVELS + 1)},
                        scan_far=scan_far, scan_keys=scan_keys, scan_state=scan_state, scan_y=scan_y,
                        tail_turn=tail_turn, tail_out=tail_out)


MIU_BANK = (2, 3, 0, 1, 2)
TD_BANK, W_BANK, K_BANK, V_BANK, R_BANK, G_BANK = 3, 0, 1, 3, 2, 0
LEVEL_BANK = 4
KT_BANK, KV_BANK, Y_BANK, YT_BANK, OUT_BANK = 6, 7, 6, 7, 6
ORDER = (("scan", "start"), ("mix", "lora"), ("tail", "norm"), ("scan", "level1"), ("mix", "shift0"),
         ("mix", "mixed0"), ("scan", "level2"), ("mix", "shift1"), ("tail", "turn"), ("mix", "mixed1"),
         ("scan", "level3"), ("mix", "shift2"), ("tail", "out"), ("mix", "td"), ("mix", "mixed2"), ("scan", "level4"),
         ("mix", "shift3"), ("mix", "rate"), ("scan", "level5"), ("mix", "shift4"), ("next", "xm"), ("scan", "far"),
         ("mix", "mixed3"), ("mix", "k"), ("scan", "keys"), ("mix", "mixed4"), ("mix", "v"), ("scan", "state"),
         ("mix", "r"), ("mix", "g"), ("mix", "chain"), ("mix", "first_k"), ("scan", "y"))


def program(nc, d, out):
    with Phase(nc) as ctx:
        def sb(name, shape, dt=F32):
            return ctx.enter_context(nc.sbuf_tensor(own(nc, name), shape, dt))

        ps = ctx.enter_context(nc.psum_tensor("ps", [P, 8, 512], F32))
        x_all, z_all = sb("x_all", [P, NT, P]), sb("z_all", [P, NT, P])
        rows = sb("rows", [P, NT, P + 1])
        y_all = rows[:, :, 0:P]
        qd = nc.dram_tensor("q_split", (SPLITS * DK, H, TOK), BF16, kind="Internal").ap()
        kd = nc.dram_tensor("k_split", (SPLITS * DK, H, TOK), BF16, kind="Internal").ap()
        xs = [nc.dram_tensor(f"sorted{i}", (SLOTS * P, P + 1), F32, kind="Internal").ap() for i in range(2)]
        ys = nc.dram_tensor("expert_out", (TOK, P), F32, kind="Internal").ap()
        s, *load = load_constants(nc, ctx, d, x_all, rows, xs)
        logits, slot, expert = sb("logits", [P, NT, E]), sb("slot", [P, NT], I32), sb("expert", [P, SLOTS], I32)

        def ffn(copy, load=None):
            with ExitStack() as inner:
                v_all = inner.enter_context(nc.sbuf_tensor(own(nc, "v_all"), [P, NT, H, DK + 1], F32))
                qkv_phase(nc, ps, s, x_all, z_all, v_all, qd, kd, load)
                attention_phase(nc, ps, s, v_all, y_all, qd, kd)
            project_phase(nc, ps, s, x_all, z_all, y_all, logits)
            route_phase(nc, ps, s, rows, logits, slot, expert, xs[copy])
            expert_phase(nc, ps, s, expert, xs[copy], ys)

        ffn(0, load)
        with ExitStack() as inner:
            zT = inner.enter_context(nc.sbuf_tensor("zT", [P, B, T + 1], F32))
            turn_phase(nc, ps, s, x_all, y_all, ys, zT)
            recurrence_phase(nc, ps, s, x_all, zT)
        ffn(1)
        combine_phase(nc, x_all, y_all, ys, out)


_INS = ['L0_attn_x', 'L0_ffn_w_proj', 'L0_ffn_ln1_w', 'L0_ffn_ln1_b', 'L0_ffn_ln2_w', 'L0_ffn_ln2_b',
        'L0_attn_miu_x', 'L0_attn_A_lora', 'L0_attn_B_lora', 'L0_attn_td_miu', 'L0_attn_td_A', 'L0_attn_td_B',
        'L0_attn_u', 'L0_attn_gn_gamma', 'L0_attn_gn_beta', 'L0_ffn_gate_w', 'L0_ffn_gate_b', 'L0_ffn_w1', 'L0_ffn_w2']


def kernel(**inputs):
    import numpy as _np
    import concourse.bacc as _bacc
    from concourse import mybir as _mybir
    from concourse.bass_utils import run_bass_kernel_spmd as _run

    nc = _bacc.Bacc("TRN2", target_bir_lowering=False, num_devices=1)
    arrays, d = {}, {}

    def give(name, a):
        a = _np.ascontiguousarray(a)
        arrays[f"in_{name}"] = a
        d[name] = nc.dram_tensor(f"in_{name}", a.shape, _mybir.dt.from_np(a.dtype), kind="ExternalInput").ap()

    for name in _INS:
        give(name, inputs[name])
    w = _np.array(inputs["L0_ffn_w_qkv"])
    for i in range(0, 2 * P, P):
        w[:, i:i + P] = w[:, i:i + P].reshape(P, H, DK).transpose(0, 2, 1).reshape(P, P)
    give("w_qkv", w)
    for name in ("Wk", "Wv", "Wr", "Wg", "Wo"):
        give(name + "T", _np.asarray(inputs["L0_attn_" + name]).T)
    give("lambda_columns", _np.asarray(inputs["L0_attn_lambda_"]).reshape(5, P).T)
    give("ident", _np.eye(P, dtype=_np.float32))
    give("below", _np.triu(_np.ones((P, P), _np.float32), 1))
    give("counts", _np.tile(_np.arange(SLOTS, dtype=_np.float32), (P, 1)))
    give("token", _np.arange(TOK, dtype=_np.float32).reshape(NT, P).T)
    give("restart", _np.tile((_np.arange(E * NT) % NT != 0).astype(_np.float32), (P, 1)))
    key, query = _np.arange(P)[:, None] % BLOCK, _np.arange(BLOCK)[None, :]
    masks = [key == query]
    for level in range(DIAG_LEVELS):
        m = 1 << level
        masks.append((key // (2 * m) == query // (2 * m)) & (key % (2 * m) < m) & (query % (2 * m) >= m))
    give("level_masks", _np.stack(masks, axis=1).astype(_np.int32))
    out = nc.dram_tensor("out_0", (8, 512, 128), _mybir.dt.float32, kind="ExternalOutput").ap()
    program(nc, d, out)
    r = _run(nc, [arrays], core_ids=[0])
    return r.results[0]["out_0"]
```
